# Optimizing a Trainium2 kernel written in Bass

```python
import numpy as np
import jax
import jax.numpy as jnp

def _softmax(x, axis=-1):
    return jax.nn.softmax(x, axis=axis)

def _gelu(x):
    return jax.nn.gelu(x, approximate=True)

def _silu(x):
    return jax.nn.silu(x)

def _sigmoid(x):
    return jax.nn.sigmoid(x)

def _layernorm(x, axis=-1, eps=1e-05):
    m = jnp.mean(x, axis=axis, keepdims=True)
    v = jnp.var(x, axis=axis, keepdims=True)
    return (x - m) / jnp.sqrt(v + eps)

def _scatter_add(tgt, idx, src, axis=0):
    return tgt.at[idx].add(src)

def _segment_sum(src, seg, n):
    return jax.ops.segment_sum(src, seg, n)
kernel_name = 'mk_macaron_d4_jaxref_r4_d25866'

def setup_inputs(seed: int=0):
    np.random.seed(seed)
    _w = jnp.asarray

    def _L0_attn_setup():
        import jax, jax.numpy as jnp
        import numpy as np
        D_MODEL = 256
        N_HEADS = 16
        D_K = D_MODEL // N_HEADS
        WINDOW = 128
        NEG_INF = -1e+30
        key = jax.random.key(seed)
        ks = jax.random.split(key, 9)
        d = D_MODEL
        scale = 0.02
        return {'x': jax.random.normal(ks[0], (1, 512, d), dtype=jnp.float32), 'Wq': jax.random.normal(ks[1], (d, d), dtype=jnp.float32) * scale, 'bq': jax.random.normal(ks[2], (d,), dtype=jnp.float32) * scale, 'Wk': jax.random.normal(ks[3], (d, d), dtype=jnp.float32) * scale, 'bk': jax.random.normal(ks[4], (d,), dtype=jnp.float32) * scale, 'Wv': jax.random.normal(ks[5], (d, d), dtype=jnp.float32) * scale, 'bv': jax.random.normal(ks[6], (d,), dtype=jnp.float32) * scale, 'Wo': jax.random.normal(ks[7], (d, d), dtype=jnp.float32) * scale, 'bo': jax.random.normal(ks[8], (d,), dtype=jnp.float32) * scale}
    _L0_attn_in = _L0_attn_setup()

    def _L0_ffn_setup():
        import jax, jax.numpy as jnp
        import numpy as np
        B, S, DIM = (4, 1024, 256)
        BASE_COUPLING = 0.1
        NUM_CYCLES = 3

        def _gelu(x):
            return jax.nn.gelu(x, approximate=False)

        def _coupling_net(h, w1, b1, w2, b2, w3, b3, w4, b4):
            h = _gelu(h @ w1 + b1)
            h = _gelu(h @ w2 + b2)
            h = _gelu(h @ w3 + b3)
            return jax.nn.sigmoid(h @ w4 + b4)

        def _global_net(h, w1, b1, w2, b2, w3, b3):
            h = _gelu(h @ w1 + b1)
            h = _gelu(h @ w2 + b2)
            return jax.nn.sigmoid(h @ w3 + b3)

        def _twist(x):
            o_r, o_i, p_r, p_i = jnp.split(x, 4, axis=-1)
            return jnp.concatenate([p_r, -p_i, -o_r, o_i], axis=-1)
        key = jax.random.key(seed)
        ks = jax.random.split(key, 9)
        d = DIM

        def w(k, fan_in, fan_out):
            return jax.random.normal(k, (fan_in, fan_out), dtype=jnp.float32) / np.sqrt(fan_in).astype(np.float32)
        inp = {'x': jax.random.normal(ks[0], (B, S, d), dtype=jnp.float32)}
        cn_dims = [(d, d), (d, d // 2), (d // 2, d // 4), (d // 4, 1)]
        for i, (a, b) in enumerate(cn_dims):
            inp[f'cn_w{i + 1}'] = w(ks[1 + i], a, b)
            inp[f'cn_b{i + 1}'] = jnp.zeros((b,), dtype=jnp.float32)
        gc_dims = [(d, d // 2), (d // 2, d // 4), (d // 4, 1)]
        for i, (a, b) in enumerate(gc_dims):
            inp[f'gc_w{i + 1}'] = w(ks[5 + i], a, b)
            inp[f'gc_b{i + 1}'] = jnp.zeros((b,), dtype=jnp.float32)
        inp['adaptive_range'] = jnp.full((1,), 0.2, dtype=jnp.float32)
        return inp
    _L0_ffn_in = _L0_ffn_setup()

    def _L1_attn_setup():
        import jax, jax.numpy as jnp
        import numpy as np
        MODEL_DIM = 256
        NUM_HEADS = 16
        D_K = MODEL_DIM // NUM_HEADS
        MAX_SEQ_LEN = 800
        B, T = (2, 512)
        THETA_BASE = 10000.0
        key = jax.random.key(seed)
        ks = jax.random.split(key, 5)
        scale = 1.0 / np.sqrt(MODEL_DIM)
        x = jax.random.normal(ks[0], (B, T, MODEL_DIM), dtype=jnp.float32)
        wq = jax.random.normal(ks[1], (MODEL_DIM, MODEL_DIM), dtype=jnp.float32) * scale
        wk = jax.random.normal(ks[2], (MODEL_DIM, MODEL_DIM), dtype=jnp.float32) * scale
        wv = jax.random.normal(ks[3], (MODEL_DIM, MODEL_DIM), dtype=jnp.float32) * scale
        wo = jax.random.normal(ks[4], (MODEL_DIM, MODEL_DIM), dtype=jnp.float32) * scale
        bq = jnp.zeros((MODEL_DIM,), jnp.float32)
        bk = jnp.zeros((MODEL_DIM,), jnp.float32)
        bv = jnp.zeros((MODEL_DIM,), jnp.float32)
        bo = jnp.zeros((MODEL_DIM,), jnp.float32)
        theta = THETA_BASE ** (jnp.arange(D_K // 2, dtype=jnp.float32) * (-2.0 / D_K))
        ang = jnp.outer(jnp.arange(MAX_SEQ_LEN, dtype=jnp.float32), theta)
        ang = jnp.repeat(ang, 2, axis=-1)
        return {'x': x, 'wq': wq, 'bq': bq, 'wk': wk, 'bk': bk, 'wv': wv, 'bv': bv, 'wo': wo, 'bo': bo, 'cos': jnp.cos(ang), 'sin': jnp.sin(ang)}
    _L1_attn_in = _L1_attn_setup()

    def _L1_ffn_setup():
        import jax, jax.numpy as jnp
        import numpy as np
        D_MODEL = 256
        D_FF = 1024
        N_EXPERTS = 8
        TOP_K = 2
        D_FF_PER = D_FF // N_EXPERTS
        B, T = (4, 512)
        key = jax.random.key(seed)
        ks = jax.random.split(key, 7)
        b1_bound = 1.0 / np.sqrt(D_MODEL)
        b2_bound = 1.0 / np.sqrt(D_FF_PER)
        return {'x': jax.random.normal(ks[0], (B, T, D_MODEL), dtype=jnp.float32), 'router_w': jax.random.uniform(ks[1], (D_MODEL, N_EXPERTS), minval=-b1_bound, maxval=b1_bound, dtype=jnp.float32), 'router_b': jax.random.uniform(ks[2], (N_EXPERTS,), minval=-b1_bound, maxval=b1_bound, dtype=jnp.float32), 'W1': jax.random.uniform(ks[3], (N_EXPERTS, D_MODEL, D_FF_PER), minval=-b1_bound, maxval=b1_bound, dtype=jnp.float32), 'b1': jax.random.uniform(ks[4], (N_EXPERTS, D_FF_PER), minval=-b1_bound, maxval=b1_bound, dtype=jnp.float32), 'W2': jax.random.uniform(ks[5], (N_EXPERTS, D_FF_PER, D_MODEL), minval=-b2_bound, maxval=b2_bound, dtype=jnp.float32), 'b2': jax.random.uniform(ks[6], (N_EXPERTS, D_MODEL), minval=-b2_bound, maxval=b2_bound, dtype=jnp.float32)}
    _L1_ffn_in = _L1_ffn_setup()

    def _L2_attn_setup():
        import jax, jax.numpy as jnp
        import numpy as np
        D_MODEL = 256
        NHEAD = 16
        HEAD_DIM = D_MODEL // NHEAD
        SCALE = float(np.sqrt(HEAD_DIM))
        key = jax.random.key(seed)
        ks = jax.random.split(key, 6)
        B, T = (2, 512)
        x = jax.random.normal(ks[0], (B, T, D_MODEL), dtype=jnp.float32)
        s = 1.0 / np.sqrt(D_MODEL)
        qkv_w = jax.random.uniform(ks[1], (3 * D_MODEL, D_MODEL), jnp.float32, -s, s)
        qkv_b = jax.random.uniform(ks[2], (3 * D_MODEL,), jnp.float32, -s, s)
        out_w = jax.random.uniform(ks[3], (D_MODEL, D_MODEL), jnp.float32, -s, s)
        out_b = jax.random.uniform(ks[4], (D_MODEL,), jnp.float32, -s, s)
        decay_alpha = jnp.full((NHEAD,), 0.1, dtype=jnp.float32)
        return {'x': x, 'qkv_w': qkv_w, 'qkv_b': qkv_b, 'out_w': out_w, 'out_b': out_b, 'decay_alpha': decay_alpha}
    _L2_attn_in = _L2_attn_setup()

    def _L2_ffn_setup():
        import jax, jax.numpy as jnp
        import numpy as np
        B, C, D, O = (4, 1024, 256, 256)
        PROJ = 64
        RANKS = [1, 2, 4, 8]
        E = len(RANKS)
        CLAMP_MAX = float(np.log(1.0 / 0.01))

        def _l2norm(v, axis):
            return v / jnp.maximum(jnp.linalg.norm(v, axis=axis, keepdims=True), 1e-12)
        key = jax.random.key(seed)
        ks = jax.random.split(key, 16)
        inp = {'x': jax.random.normal(ks[0], (B, C, D), dtype=jnp.float32), 'W': jax.random.normal(ks[1], (O, D), dtype=jnp.float32) / np.sqrt(D), 'Wp': jax.random.normal(ks[2], (PROJ, D), dtype=jnp.float32) / np.sqrt(D), 'bp': jnp.zeros((PROJ,), dtype=jnp.float32), 'sim': jax.random.normal(ks[3], (PROJ, E), dtype=jnp.float32) * 0.01, 'temp': jnp.full((1,), np.log(1.0 / 0.5), dtype=jnp.float32)}
        for i, r in enumerate(RANKS):
            inp[f'Wd{i}'] = jax.random.normal(ks[4 + 2 * i], (r, D), dtype=jnp.float32) / r
            inp[f'Wu{i}'] = jax.random.normal(ks[5 + 2 * i], (O, r), dtype=jnp.float32) * 0.01
        return inp
    _L2_ffn_in = _L2_ffn_setup()

    def _L3_attn_setup():
        import math
        import jax, jax.numpy as jnp
        import numpy as np
        NUM_HEADS = 8
        ATTN_STD = np.array([1.0, 2.0, 4.0, 8.0, 1.0, 2.0, 4.0, 8.0], dtype=np.float32)
        ATTN_OFFSET = np.array([-1.0, -2.0, -4.0, -8.0, -1.0, -2.0, -4.0, -8.0], dtype=np.float32)

        def _gaussian_attn_weights(qlen, dtype):
            stds = jnp.asarray(ATTN_STD, dtype=dtype)[:, None, None]
            offs = jnp.asarray(ATTN_OFFSET, dtype=dtype)[:, None, None]
            q = jnp.arange(qlen, dtype=dtype)[None, :, None]
            k = jnp.arange(qlen, dtype=dtype)[None, None, :]
            dist = k - q - offs
            inv_norm = 1.0 / (stds * math.sqrt(2.0 * math.pi))
            return inv_norm * jnp.exp(-0.5 * (dist / stds) ** 2)
        key = jax.random.key(seed)
        k1, k2, k3 = jax.random.split(key, 3)
        B, L, D = (2, 512, 256)
        values = jax.random.normal(k1, (B, L, D), dtype=jnp.float32)
        input_weights = 0.02 * jax.random.normal(k2, (D, D), dtype=jnp.float32)
        output_weight = 0.02 * jax.random.normal(k3, (D, D), dtype=jnp.float32)
        return {'values': values, 'input_weights': input_weights, 'output_weight': output_weight}
    _L3_attn_in = _L3_attn_setup()

    def _L3_ffn_setup():
        import jax, jax.numpy as jnp
        import numpy as np
        D, H, K, S = (256, 8, 16, 128)
        HD = D // H
        N_TOTAL = S * S
        LN_EPS = 1e-05
        key = jax.random.key(seed)
        ks = jax.random.split(key, 9)
        B, T = (4, 512)
        x = jax.random.normal(ks[0], (B, T, D), dtype=jnp.float32)
        W_in = jax.random.normal(ks[1], (D, D), dtype=jnp.float32) * (1.0 / np.sqrt(D))
        keys_a = jax.random.normal(ks[2], (H, S, HD), dtype=jnp.float32) * 0.02
        keys_b = jax.random.normal(ks[3], (H, S, HD), dtype=jnp.float32) * 0.02
        u_shared = jax.random.normal(ks[4], (HD,), dtype=jnp.float32) * 0.01
        expert_v = jax.random.normal(ks[5], (N_TOTAL, HD), dtype=jnp.float32) * 0.01
        W_out = jax.random.normal(ks[6], (D, D), dtype=jnp.float32) * (1.0 / np.sqrt(D))
        ln_w = jnp.ones((D,), dtype=jnp.float32)
        ln_b = jnp.zeros((D,), dtype=jnp.float32)
        return {'x': x, 'W_in': W_in, 'keys_a': keys_a, 'keys_b': keys_b, 'u_shared': u_shared, 'expert_v': expert_v, 'W_out': W_out, 'ln_w': ln_w, 'ln_b': ln_b}
    _L3_ffn_in = _L3_ffn_setup()
    _d = {'L0_attn_x': _L0_attn_in['x'], 'L0_attn_Wq': _L0_attn_in['Wq'], 'L0_attn_bq': _L0_attn_in['bq'], 'L0_attn_Wk': _L0_attn_in['Wk'], 'L0_attn_bk': _L0_attn_in['bk'], 'L0_attn_Wv': _L0_attn_in['Wv'], 'L0_attn_bv': _L0_attn_in['bv'], 'L0_attn_Wo': _L0_attn_in['Wo'], 'L0_attn_bo': _L0_attn_in['bo'], 'L0_ffn_cn_w1': _L0_ffn_in['cn_w1'], 'L0_ffn_cn_b1': _L0_ffn_in['cn_b1'], 'L0_ffn_cn_w2': _L0_ffn_in['cn_w2'], 'L0_ffn_cn_b2': _L0_ffn_in['cn_b2'], 'L0_ffn_cn_w3': _L0_ffn_in['cn_w3'], 'L0_ffn_cn_b3': _L0_ffn_in['cn_b3'], 'L0_ffn_cn_w4': _L0_ffn_in['cn_w4'], 'L0_ffn_cn_b4': _L0_ffn_in['cn_b4'], 'L0_ffn_gc_w1': _L0_ffn_in['gc_w1'], 'L0_ffn_gc_b1': _L0_ffn_in['gc_b1'], 'L0_ffn_gc_w2': _L0_ffn_in['gc_w2'], 'L0_ffn_gc_b2': _L0_ffn_in['gc_b2'], 'L0_ffn_gc_w3': _L0_ffn_in['gc_w3'], 'L0_ffn_gc_b3': _L0_ffn_in['gc_b3'], 'L0_ffn_adaptive_range': _L0_ffn_in['adaptive_range'], 'L1_attn_wq': _L1_attn_in['wq'], 'L1_attn_bq': _L1_attn_in['bq'], 'L1_attn_wk': _L1_attn_in['wk'], 'L1_attn_bk': _L1_attn_in['bk'], 'L1_attn_wv': _L1_attn_in['wv'], 'L1_attn_bv': _L1_attn_in['bv'], 'L1_attn_wo': _L1_attn_in['wo'], 'L1_attn_bo': _L1_attn_in['bo'], 'L1_attn_cos': _L1_attn_in['cos'], 'L1_attn_sin': _L1_attn_in['sin'], 'L1_ffn_router_w': _L1_ffn_in['router_w'], 'L1_ffn_router_b': _L1_ffn_in['router_b'], 'L1_ffn_W1': _L1_ffn_in['W1'], 'L1_ffn_b1': _L1_ffn_in['b1'], 'L1_ffn_W2': _L1_ffn_in['W2'], 'L1_ffn_b2': _L1_ffn_in['b2'], 'L2_attn_qkv_w': _L2_attn_in['qkv_w'], 'L2_attn_qkv_b': _L2_attn_in['qkv_b'], 'L2_attn_out_w': _L2_attn_in['out_w'], 'L2_attn_out_b': _L2_attn_in['out_b'], 'L2_attn_decay_alpha': _L2_attn_in['decay_alpha'], 'L2_ffn_W': _L2_ffn_in['W'], 'L2_ffn_Wp': _L2_ffn_in['Wp'], 'L2_ffn_bp': _L2_ffn_in['bp'], 'L2_ffn_sim': _L2_ffn_in['sim'], 'L2_ffn_temp': _L2_ffn_in['temp'], 'L2_ffn_Wd0': _L2_ffn_in['Wd0'], 'L2_ffn_Wu0': _L2_ffn_in['Wu0'], 'L2_ffn_Wd1': _L2_ffn_in['Wd1'], 'L2_ffn_Wu1': _L2_ffn_in['Wu1'], 'L2_ffn_Wd2': _L2_ffn_in['Wd2'], 'L2_ffn_Wu2': _L2_ffn_in['Wu2'], 'L2_ffn_Wd3': _L2_ffn_in['Wd3'], 'L2_ffn_Wu3': _L2_ffn_in['Wu3'], 'L3_attn_input_weights': _L3_attn_in['input_weights'], 'L3_attn_output_weight': _L3_attn_in['output_weight'], 'L3_ffn_W_in': _L3_ffn_in['W_in'], 'L3_ffn_keys_a': _L3_ffn_in['keys_a'], 'L3_ffn_keys_b': _L3_ffn_in['keys_b'], 'L3_ffn_u_shared': _L3_ffn_in['u_shared'], 'L3_ffn_expert_v': _L3_ffn_in['expert_v'], 'L3_ffn_W_out': _L3_ffn_in['W_out'], 'L3_ffn_ln_w': _L3_ffn_in['ln_w'], 'L3_ffn_ln_b': _L3_ffn_in['ln_b']}
    _x0 = _d['L0_attn_x']
    _d['L0_attn_x'] = jax.random.normal(jax.random.fold_in(jax.random.key(seed), 1), (4, 1024, 256), dtype=_x0.dtype)
    del _x0
    return _d

def reference(L0_attn_x, L0_attn_Wq, L0_attn_bq, L0_attn_Wk, L0_attn_bk, L0_attn_Wv, L0_attn_bv, L0_attn_Wo, L0_attn_bo, L0_ffn_cn_w1, L0_ffn_cn_b1, L0_ffn_cn_w2, L0_ffn_cn_b2, L0_ffn_cn_w3, L0_ffn_cn_b3, L0_ffn_cn_w4, L0_ffn_cn_b4, L0_ffn_gc_w1, L0_ffn_gc_b1, L0_ffn_gc_w2, L0_ffn_gc_b2, L0_ffn_gc_w3, L0_ffn_gc_b3, L0_ffn_adaptive_range, L1_attn_wq, L1_attn_bq, L1_attn_wk, L1_attn_bk, L1_attn_wv, L1_attn_bv, L1_attn_wo, L1_attn_bo, L1_attn_cos, L1_attn_sin, L1_ffn_router_w, L1_ffn_router_b, L1_ffn_W1, L1_ffn_b1, L1_ffn_W2, L1_ffn_b2, L2_attn_qkv_w, L2_attn_qkv_b, L2_attn_out_w, L2_attn_out_b, L2_attn_decay_alpha, L2_ffn_W, L2_ffn_Wp, L2_ffn_bp, L2_ffn_sim, L2_ffn_temp, L2_ffn_Wd0, L2_ffn_Wu0, L2_ffn_Wd1, L2_ffn_Wu1, L2_ffn_Wd2, L2_ffn_Wu2, L2_ffn_Wd3, L2_ffn_Wu3, L3_attn_input_weights, L3_attn_output_weight, L3_ffn_W_in, L3_ffn_keys_a, L3_ffn_keys_b, L3_ffn_u_shared, L3_ffn_expert_v, L3_ffn_W_out, L3_ffn_ln_w, L3_ffn_ln_b):

    def _L0_attn_ref(x, Wq, bq, Wk, bk, Wv, bv, Wo, bo):
        import jax, jax.numpy as jnp
        import numpy as np
        D_MODEL = 256
        N_HEADS = 16
        D_K = D_MODEL // N_HEADS
        WINDOW = 128
        NEG_INF = -1e+30
        B, L, D = x.shape
        H, dk, W = (N_HEADS, D_K, WINDOW)

        def proj(Wm, bm):
            y = jnp.einsum('bld,ed->ble', x, Wm) + bm
            return y.reshape(B, L, H, dk).transpose(0, 2, 1, 3)
        q = proj(Wq, bq)
        k = proj(Wk, bk)
        v = proj(Wv, bv)
        scores = jnp.einsum('bhid,bhjd->bhij', q, k) / jnp.sqrt(jnp.asarray(dk, x.dtype))
        if W < L:
            im = jnp.arange(L) % W
            tile_mask = im[:, None] >= im[None, :]
            scores = jnp.where(tile_mask, scores, NEG_INF)
        probs = jax.nn.softmax(scores, axis=-1)
        attn = jnp.einsum('bhij,bhjd->bhid', probs, v)
        out = attn.transpose(0, 2, 1, 3).reshape(B, L, D)
        out = jnp.einsum('bld,ed->ble', out, Wo) + bo
        return out

    def _L0_ffn_ref(x, cn_w1, cn_b1, cn_w2, cn_b2, cn_w3, cn_b3, cn_w4, cn_b4, gc_w1, gc_b1, gc_w2, gc_b2, gc_w3, gc_b3, adaptive_range):
        import jax, jax.numpy as jnp
        import numpy as np
        B, S, DIM = (4, 1024, 256)
        BASE_COUPLING = 0.1
        NUM_CYCLES = 3

        def _gelu(x):
            return jax.nn.gelu(x, approximate=False)

        def _coupling_net(h, w1, b1, w2, b2, w3, b3, w4, b4):
            h = _gelu(h @ w1 + b1)
            h = _gelu(h @ w2 + b2)
            h = _gelu(h @ w3 + b3)
            return jax.nn.sigmoid(h @ w4 + b4)

        def _global_net(h, w1, b1, w2, b2, w3, b3):
            h = _gelu(h @ w1 + b1)
            h = _gelu(h @ w2 + b2)
            return jax.nn.sigmoid(h @ w3 + b3)

        def _twist(x):
            o_r, o_i, p_r, p_i = jnp.split(x, 4, axis=-1)
            return jnp.concatenate([p_r, -p_i, -o_r, o_i], axis=-1)
        global_context = x.mean(axis=1, keepdims=True)
        gf = _global_net(global_context, gc_w1, gc_b1, gc_w2, gc_b2, gc_w3, gc_b3)
        out = x
        for _ in range(NUM_CYCLES):
            tf = _coupling_net(out, cn_w1, cn_b1, cn_w2, cn_b2, cn_w3, cn_b3, cn_w4, cn_b4)
            combined = 0.7 * gf + 0.3 * tf
            coupling = BASE_COUPLING + adaptive_range * (combined - 0.5) * 2.0
            out = out + coupling * _twist(out)
        return out

    def _L1_attn_ref(x, wq, bq, wk, bk, wv, bv, wo, bo, cos, sin):
        import jax, jax.numpy as jnp
        import numpy as np
        MODEL_DIM = 256
        NUM_HEADS = 16
        D_K = MODEL_DIM // NUM_HEADS
        MAX_SEQ_LEN = 800
        B, T = (2, 512)
        THETA_BASE = 10000.0
        b, t, dm = x.shape
        h, d = (NUM_HEADS, dm // NUM_HEADS)
        xq = (x @ wq.T + bq).reshape(b, h, t, d)
        xk = (x @ wk.T + bk).reshape(b, h, t, d)
        xv = (x @ wv.T + bv).reshape(b, h, t, d)

        def rot_half(q):
            q2 = q.reshape(b, h, t, d // 2, 2)
            return jnp.stack([-q2[..., 1], q2[..., 0]], axis=-1).reshape(b, h, t, d)
        c = cos[t]
        s = sin[t]
        xq = xq * c + rot_half(xq) * s
        xk = xk * c + rot_half(xk) * s
        scores = jnp.einsum('bhqd,bhkd->bhqk', xq, xk) / np.sqrt(d)
        p = jax.nn.softmax(scores, axis=-1)
        o = jnp.einsum('bhqk,bhkd->bhqd', p, xv)
        o = o.transpose(0, 2, 1, 3).reshape(b, t, dm)
        return o @ wo.T + bo

    def _L1_ffn_ref(x, router_w, router_b, W1, b1, W2, b2):
        import jax, jax.numpy as jnp
        import numpy as np
        D_MODEL = 256
        D_FF = 1024
        N_EXPERTS = 8
        TOP_K = 2
        D_FF_PER = D_FF // N_EXPERTS
        B, T = (4, 512)
        router_logits = x @ router_w + router_b
        routing_weights = jax.nn.softmax(router_logits, axis=-1)
        top_k_weights, top_k_indices = jax.lax.top_k(routing_weights, TOP_K)
        top_k_weights = top_k_weights / jnp.sum(top_k_weights, axis=-1, keepdims=True)
        routing_mask = jnp.zeros_like(routing_weights)
        routing_mask = jnp.take_along_axis(routing_mask, top_k_indices, axis=-1)
        b_idx = jnp.arange(x.shape[0])[:, None, None]
        t_idx = jnp.arange(x.shape[1])[None, :, None]
        routing_mask = jnp.zeros_like(routing_weights).at[b_idx, t_idx, top_k_indices].set(top_k_weights)
        h1 = jnp.einsum('btd,nde->btne', x, W1) + b1
        h1 = jax.nn.gelu(h1, approximate=False)
        out_per_expert = jnp.einsum('btne,nef->btnf', h1, W2) + b2
        output = jnp.sum(out_per_expert * routing_mask[..., None], axis=-2)
        return output

    def _L2_attn_ref(x, qkv_w, qkv_b, out_w, out_b, decay_alpha):
        import jax, jax.numpy as jnp
        import numpy as np
        D_MODEL = 256
        NHEAD = 16
        HEAD_DIM = D_MODEL // NHEAD
        SCALE = float(np.sqrt(HEAD_DIM))
        B, T, D = x.shape
        qkv = x @ qkv_w.T + qkv_b
        qkv = qkv.reshape(B, T, 3, NHEAD, HEAD_DIM).transpose(2, 0, 3, 1, 4)
        q, k, v = (qkv[0], qkv[1], qkv[2])
        logits = jnp.einsum('bhqd,bhkd->bhqk', q, k) / SCALE
        pos = jnp.arange(T, dtype=jnp.float32)
        dist = jnp.abs(pos[None, :] - pos[:, None])
        alpha = jax.nn.softplus(decay_alpha)
        logits = logits - alpha[:, None, None] * dist[None]
        attn = jax.nn.softmax(logits, axis=-1)
        out = jnp.einsum('bhqk,bhkd->bhqd', attn, v)
        out = out.transpose(0, 2, 1, 3).reshape(B, T, D)
        out = out @ out_w.T + out_b
        return out

    def _L2_ffn_ref(x, W, Wp, bp, sim, temp, Wd0, Wu0, Wd1, Wu1, Wd2, Wu2, Wd3, Wu3):
        import jax, jax.numpy as jnp
        import numpy as np
        B, C, D, O = (4, 1024, 256, 256)
        PROJ = 64
        RANKS = [1, 2, 4, 8]
        E = len(RANKS)
        CLAMP_MAX = float(np.log(1.0 / 0.01))

        def _l2norm(v, axis):
            return v / jnp.maximum(jnp.linalg.norm(v, axis=axis, keepdims=True), 1e-12)
        base = jnp.einsum('bcd,od->bco', x, W)
        xf = x.reshape(-1, x.shape[-1])
        proj = _l2norm(xf @ Wp.T + bp, axis=1)
        simn = _l2norm(sim, axis=0)
        scale = jnp.exp(jnp.minimum(temp, CLAMP_MAX))
        logits = proj @ simn * scale
        lw = jax.nn.softmax(logits, axis=1)
        top1 = jnp.argmax(lw, axis=1)
        ret = jnp.where(jnp.arange(E)[None, :] == top1[:, None], lw, 0.0)
        ret = ret.reshape(x.shape[0], x.shape[1], E)
        downs = (Wd0, Wd1, Wd2, Wd3)
        ups = (Wu0, Wu1, Wu2, Wu3)
        l = jnp.stack([jnp.einsum('bcr,or->bco', jnp.einsum('bcd,rd->bcr', x, d), u) for d, u in zip(downs, ups)], axis=2)
        res = jnp.sum(ret[..., None] * l, axis=2)
        return base + res

    def _L3_attn_ref(values, input_weights, output_weight):
        import math
        import jax, jax.numpy as jnp
        import numpy as np
        NUM_HEADS = 8
        ATTN_STD = np.array([1.0, 2.0, 4.0, 8.0, 1.0, 2.0, 4.0, 8.0], dtype=np.float32)
        ATTN_OFFSET = np.array([-1.0, -2.0, -4.0, -8.0, -1.0, -2.0, -4.0, -8.0], dtype=np.float32)

        def _gaussian_attn_weights(qlen, dtype):
            stds = jnp.asarray(ATTN_STD, dtype=dtype)[:, None, None]
            offs = jnp.asarray(ATTN_OFFSET, dtype=dtype)[:, None, None]
            q = jnp.arange(qlen, dtype=dtype)[None, :, None]
            k = jnp.arange(qlen, dtype=dtype)[None, None, :]
            dist = k - q - offs
            inv_norm = 1.0 / (stds * math.sqrt(2.0 * math.pi))
            return inv_norm * jnp.exp(-0.5 * (dist / stds) ** 2)
        B, L, D = values.shape
        H = NUM_HEADS
        pd = D // H
        v = values @ input_weights.T
        v = v.reshape(B, L, H, pd).transpose(0, 2, 1, 3)
        probs = _gaussian_attn_weights(L, values.dtype)
        attended = jnp.einsum('hqk,bhkd->bhqd', probs, v)
        attended = attended.transpose(0, 2, 1, 3).reshape(B, L, D)
        return attended @ output_weight.T

    def _L3_ffn_ref(x, W_in, keys_a, keys_b, u_shared, expert_v, W_out, ln_w, ln_b):
        import jax, jax.numpy as jnp
        import numpy as np
        D, H, K, S = (256, 8, 16, 128)
        HD = D // H
        N_TOTAL = S * S
        LN_EPS = 1e-05
        B, T, Dm = x.shape
        h = (x @ W_in.T).reshape(B, T, H, HD)
        scores_a = jnp.einsum('bthd,hsd->bths', h, keys_a)
        scores_b = jnp.einsum('bthd,hsd->bths', h, keys_b)
        top_a_s, top_a_i = jax.lax.top_k(scores_a, K)
        top_b_s, top_b_i = jax.lax.top_k(scores_b, K)
        prod_s = top_a_s[..., :, None] + top_b_s[..., None, :]
        prod_i = top_a_i[..., :, None] * S + top_b_i[..., None, :]
        prod_s_flat = prod_s.reshape(B, T, H, K * K)
        prod_i_flat = prod_i.reshape(B, T, H, K * K)
        top_scores, top_pos = jax.lax.top_k(prod_s_flat, K)
        top_expert_idx = jnp.take_along_axis(prod_i_flat, top_pos, axis=-1)
        top_weights = jax.nn.softmax(top_scores, axis=-1)
        sel_v = expert_v[top_expert_idx]
        activation = jax.nn.sigmoid(jnp.einsum('bthd,d->bth', h, u_shared))[..., None]
        weighted_v = jnp.einsum('bthk,bthkd->bthd', top_weights, sel_v)
        expert_out = activation * weighted_v
        merged = expert_out.reshape(B, T, Dm)
        proj = merged @ W_out.T
        mu = jnp.mean(proj, axis=-1, keepdims=True)
        var = jnp.mean(jnp.square(proj - mu), axis=-1, keepdims=True)
        out = (proj - mu) * jax.lax.rsqrt(var + LN_EPS) * ln_w + ln_b
        return out
    x = L0_attn_x
    x = x + 0.5 * _L0_ffn_ref(_layernorm(x, axis=-1), L0_ffn_cn_w1, L0_ffn_cn_b1, L0_ffn_cn_w2, L0_ffn_cn_b2, L0_ffn_cn_w3, L0_ffn_cn_b3, L0_ffn_cn_w4, L0_ffn_cn_b4, L0_ffn_gc_w1, L0_ffn_gc_b1, L0_ffn_gc_w2, L0_ffn_gc_b2, L0_ffn_gc_w3, L0_ffn_gc_b3, L0_ffn_adaptive_range)
    x = x + _L0_attn_ref(_layernorm(x, axis=-1), L0_attn_Wq, L0_attn_bq, L0_attn_Wk, L0_attn_bk, L0_attn_Wv, L0_attn_bv, L0_attn_Wo, L0_attn_bo)
    x = x + 0.5 * _L0_ffn_ref(_layernorm(x, axis=-1), L0_ffn_cn_w1, L0_ffn_cn_b1, L0_ffn_cn_w2, L0_ffn_cn_b2, L0_ffn_cn_w3, L0_ffn_cn_b3, L0_ffn_cn_w4, L0_ffn_cn_b4, L0_ffn_gc_w1, L0_ffn_gc_b1, L0_ffn_gc_w2, L0_ffn_gc_b2, L0_ffn_gc_w3, L0_ffn_gc_b3, L0_ffn_adaptive_range)
    x = x + 0.5 * _L1_ffn_ref(_layernorm(x, axis=-1), L1_ffn_router_w, L1_ffn_router_b, L1_ffn_W1, L1_ffn_b1, L1_ffn_W2, L1_ffn_b2)
    x = x + _L1_attn_ref(_layernorm(x, axis=-1), L1_attn_wq, L1_attn_bq, L1_attn_wk, L1_attn_bk, L1_attn_wv, L1_attn_bv, L1_attn_wo, L1_attn_bo, L1_attn_cos, L1_attn_sin)
    x = x + 0.5 * _L1_ffn_ref(_layernorm(x, axis=-1), L1_ffn_router_w, L1_ffn_router_b, L1_ffn_W1, L1_ffn_b1, L1_ffn_W2, L1_ffn_b2)
    x = x + 0.5 * _L2_ffn_ref(_layernorm(x, axis=-1), L2_ffn_W, L2_ffn_Wp, L2_ffn_bp, L2_ffn_sim, L2_ffn_temp, L2_ffn_Wd0, L2_ffn_Wu0, L2_ffn_Wd1, L2_ffn_Wu1, L2_ffn_Wd2, L2_ffn_Wu2, L2_ffn_Wd3, L2_ffn_Wu3)
    x = x + _L2_attn_ref(_layernorm(x, axis=-1), L2_attn_qkv_w, L2_attn_qkv_b, L2_attn_out_w, L2_attn_out_b, L2_attn_decay_alpha)
    x = x + 0.5 * _L2_ffn_ref(_layernorm(x, axis=-1), L2_ffn_W, L2_ffn_Wp, L2_ffn_bp, L2_ffn_sim, L2_ffn_temp, L2_ffn_Wd0, L2_ffn_Wu0, L2_ffn_Wd1, L2_ffn_Wu1, L2_ffn_Wd2, L2_ffn_Wu2, L2_ffn_Wd3, L2_ffn_Wu3)
    x = x + 0.5 * _L3_ffn_ref(_layernorm(x, axis=-1), L3_ffn_W_in, L3_ffn_keys_a, L3_ffn_keys_b, L3_ffn_u_shared, L3_ffn_expert_v, L3_ffn_W_out, L3_ffn_ln_w, L3_ffn_ln_b)
    x = x + _L3_attn_ref(_layernorm(x, axis=-1), L3_attn_input_weights, L3_attn_output_weight)
    x = x + 0.5 * _L3_ffn_ref(_layernorm(x, axis=-1), L3_ffn_W_in, L3_ffn_keys_a, L3_ffn_keys_b, L3_ffn_u_shared, L3_ffn_expert_v, L3_ffn_W_out, L3_ffn_ln_w, L3_ffn_ln_b)
    return x

_drawn_inputs = setup_inputs


def setup_inputs(seed=0):
    import zlib

    import numpy as np

    out = dict(_drawn_inputs(seed))
    spreads = {'L0_ffn_cn_b1': (0.0, 0.713),
     'L0_ffn_cn_b2': (0.0, 0.669),
     'L0_ffn_cn_b3': (0.0, 0.492),
     'L0_ffn_gc_b1': (0.0, 0.495),
     'L0_ffn_gc_b2': (0.0, 0.412),
     'L1_attn_bq': (0.0, 0.475),
     'L1_attn_bk': (0.0, 0.458),
     'L1_attn_bv': (0.0, 0.1),
     'L1_attn_bo': (0.0, 0.1),
     'L2_attn_decay_alpha': (0.10000000149011612, 0.6),
     'L2_ffn_bp': (0.0, 0.8),
     'L3_ffn_ln_w': (1.0, 0.2),
     'L3_ffn_ln_b': (0.0, 0.1)}
    factors = {'L0_attn_Wq': 8.0,
     'L0_attn_bq': 8.0,
     'L0_attn_Wk': 8.0,
     'L0_attn_bk': 64.0,
     'L0_attn_Wv': 3.647,
     'L0_attn_bv': 3.417,
     'L0_attn_Wo': 2.993,
     'L0_ffn_cn_w1': 2.749,
     'L0_ffn_cn_w2': 2.823,
     'L0_ffn_gc_w1': 6.284,
     'L0_ffn_gc_w2': 4.425,
     'L1_ffn_router_b': 2.903,
     'L1_ffn_b1': 3.534,
     'L2_ffn_Wd0': 3.293,
     'L2_ffn_Wu0': 3.154,
     'L2_ffn_Wd1': 4.015,
     'L2_ffn_Wu1': 3.981,
     'L2_ffn_Wd2': 5.156,
     'L2_ffn_Wu2': 5.058,
     'L2_ffn_Wd3': 4.933,
     'L2_ffn_Wu3': 4.911,
     'L3_ffn_u_shared': 7.377,
     'L3_attn_input_weights': 2.73,
     'L3_attn_output_weight': 2.682}
    for name, (base, spread) in spreads.items():
        noise = np.random.default_rng([zlib.crc32(name.encode()), seed]).standard_normal(out[name].shape)
        drawn = base * np.exp(spread * noise) if base else spread * noise
        out[name] = jnp.asarray(drawn.astype(out[name].dtype))
    for name, factor in factors.items():
        out[name] = (out[name] * factor).astype(out[name].dtype)
    return out
```

```python
import concourse.bass as bass
from concourse import mybir
from contextlib import ExitStack

F32 = mybir.dt.float32
BF16 = mybir.dt.bfloat16
U32 = mybir.dt.uint32
I32 = mybir.dt.int32
ALU = mybir.AluOpType
ACT = mybir.ActivationFunctionType
AX = mybir.AxisListType

P = 128
B, S, D = 4, 1024, 256
T = S // P
C = D // P
H = 16
DK = D // H
G = 4
NG = H // G
PAD = 32
HALF = S // 2
LOWEST = -3.0e38
MASKED = -1.0e30
EPS = 1e-5
E1 = 8
F1 = 128
PR = 64
RANKS = (1, 2, 4, 8)
RT = sum(RANKS)
HP, KP, NS = 8, 16, 128
HD = D // HP
ROWS = [KP // (i + 1) for i in range(KP)]
NC_ = sum(ROWS)
STARTS = [sum(ROWS[:i]) for i in range(KP)]
TERMS = ((0, 0), (0, 1), (1, 0), (1, 1), (0, 2), (2, 0))
KT = len(TERMS) * DK
STD = (1.0, 2.0, 4.0, 8.0)

SEMS = ("loaded", "stored", "bounced", "mbounced", "vector_step", "pool_step", "scalar_step", "variance_ready",
        "std_ready", "normalized", "transposed", "multiplied", "activated", "state_updated", "sums_ready",
        "columns_ready", "split_ready", "v_ready", "max_scored", "max_taken", "max_turned", "max_split",
        "scored", "biased", "exponentiated", "weighted", "heads_copied", "denominators_ready", "heads_done",
        "routed", "cleared", "indices_ready", "gathered_even", "gathered_odd", "gathers_used", "merged_ready",
        "results_ready", "halfway", "rows_ready", "probs_ready", "bounced0", "bounced1", "v_bounced", "v_loaded",
        "heads_loaded0", "heads_loaded1", "heads_loaded2", "heads_loaded3", "max_combined", "max_loaded", "rotated",
        "table_ready", "v_scored")


class Core:

    def __init__(self, nc, ctx, a):
        self.nc, self.a, self.stage = nc, a, 0
        self.sem = {n: ctx.enter_context(nc.semaphore(n)) for n in SEMS}
        nums = [s.num for s in self.sem.values()]
        self.span = range(min(nums), max(nums) + 1)
        assert len(self.span) == len(nums)

        def sb(name, shape, dt=F32):
            return ctx.enter_context(nc.sbuf_tensor(name, shape, dt))

        self.ps = ctx.enter_context(nc.psum_tensor("ps", [P, 8, 512], F32))
        self.ident = sb("ident", [P, P])
        self.ones = sb("ones", [P, P])
        self.sel = sb("sel", [P, P])
        self.residue = sb("residue", [16, 2, P], BF16)
        self.qk_parts = nc.dram_tensor("qk_parts", (2, 3, D, S), BF16).ap()
        self.max_parts = nc.dram_tensor("max_parts", (3, G * S), BF16).ap()
        self.v_rows = nc.dram_tensor("v_rows", (S, D), F32).ap()
        self.ones_rows = nc.dram_tensor("ones_rows", (4, H * S), BF16).ap()
        self.x = sb("x", [P, T, D])
        self.y = sb("y", [P, T, D])
        self.yT = sb("yT", [P, C, S])

    def unique(self, name):
        return f"{name}_{self.stage}"

    def end_stage(self, gathers=False):
        self.stage += 1
        self.nc.all_engine_barrier(sem_only=True)
        if gathers:
            first = self.sem["gathered_even"].num
            assert self.sem["gathered_odd"].num == first + 1
            self.nc.gpsimd.dma_reset(range(first, first + 2))
        self.nc.gpsimd.sem_clear(self.span)
        self.nc.all_engine_barrier(sem_only=True)


def stepper(eng, sem):
    count = [0]

    def link(ins):
        count[0] += 1
        ins.then_inc(sem, 1)
        eng.wait_ge(sem, count[0])
    return link


def constants(k):
    nc, s = k.nc, k.sem
    with ExitStack() as ctx:
        ones_b = ctx.enter_context(nc.sbuf_tensor("ones_b", [P, 4 * H * S // P], BF16))
        block = ctx.enter_context(nc.Block())

        @block.gpsimd
        def _(pool):
            link = stepper(pool, s["pool_step"])
            pool.memset(ones_b[:, :], 1.0).then_inc(s["cleared"], 1)
            pool.memset(k.ones[:, :], 1.0)
            pool.memset(k.sel[:, :], 0.0)
            pool.memset(k.residue[:, 0, :], 0.0)
            pool.memset(k.residue[:, 1, :], 1.0)
            link(pool.memset(k.ident[:, :], 0.0))
            pool.affine_select(out=k.ident[:, :], in_=k.ident[:, :], compare_op=ALU.not_equal, fill=1.0,
                               base=0, pattern=[[-1, P]], channel_multiplier=1)
            pool.affine_select(out=k.sel[:, :], in_=k.sel[:, :], compare_op=ALU.not_equal, fill=1.0,
                               base=-DK, pattern=[[-PAD, G], [0, PAD]], channel_multiplier=1)
            pool.affine_select(out=k.residue[:, 0, :], in_=k.residue[:, 0, :], compare_op=ALU.is_ge, fill=MASKED,
                               base=0, pattern=[[1, P]], channel_multiplier=-T)
            link(pool.affine_select(out=k.residue[:, 1, :], in_=k.residue[:, 1, :], compare_op=ALU.is_ge, fill=0.0,
                                    base=0, pattern=[[1, P]], channel_multiplier=-T))
            link(pool.affine_select(out=k.residue[:, 1, :], in_=k.residue[:, 1, :], compare_op=ALU.is_ge, fill=0.0,
                                    base=T - 1, pattern=[[-1, P]], channel_multiplier=T))

        @block.sync
        def _(sp):
            sp.wait_ge(s["cleared"], 1)
            sp.dma_start(k.ones_rows.rearrange("a (b n) -> (a b) n", b=P // 4), ones_b[:, :]).then_inc(s["stored"], 16)
            sp.wait_ge(s["stored"], 16)
    k.end_stage()


def load_batch(k, x, b):
    nc, s = k.nc, k.sem
    with nc.Block() as block:
        @block.sync
        def _(sp):
            sp.dma_start(k.x[:, :, :], x[bass.ds(b, 1)].rearrange("o (t p) n -> p (o t) n", p=P)).then_inc(s["loaded"], 16)
            sp.wait_ge(s["loaded"], 16)
    k.end_stage()


def store_batch(k, out, b):
    nc, s = k.nc, k.sem
    with nc.Block() as block:
        @block.sync
        def _(sp):
            sp.dma_start(out[bass.ds(b, 1)].rearrange("o (t p) n -> p (o t) n", p=P), k.x[:, :, :]).then_inc(s["stored"], 16)
            sp.wait_ge(s["stored"], 16)
    k.end_stage()


def layer_norm(k):
    nc, s, ps = k.nc, k.sem, k.ps
    with ExitStack() as ctx:
        stats = ctx.enter_context(nc.sbuf_tensor(k.unique("ln_stats"), [P, T, 6], F32))
        mv = ctx.enter_context(nc.sbuf_tensor(k.unique("ln_mv"), [P, T, 2], F32))
        var = ctx.enter_context(nc.sbuf_tensor(k.unique("ln_var"), [P, T], F32))
        std = ctx.enter_context(nc.sbuf_tensor(k.unique("ln_std"), [P, T], F32))
        rstd = ctx.enter_context(nc.sbuf_tensor(k.unique("ln_rstd"), [P, T], F32))
        block = ctx.enter_context(nc.Block())

        @block.vector
        def _(dve):
            link = stepper(dve, s["vector_step"])
            for t in range(T):
                last = dve.bn_stats(stats[:, t, :], k.x[:, t, :])
            link(last)
            for t in range(T):
                last = dve.bn_aggr(mv[:, t, :], stats[:, t, :])
            link(last)
            dve.tensor_scalar(var[:, :], mv[:, :, 1], EPS, None, ALU.add).then_inc(s["variance_ready"], 1)
            dve.wait_ge(s["std_ready"], 1)
            link(dve.reciprocal(rstd[:, :], std[:, :]))
            for t in range(T):
                dve.tensor_scalar(k.y[:, t, :], k.x[:, t, :], mv[:, t, 0:1], rstd[:, t:t + 1],
                                  ALU.subtract, ALU.mult).then_inc(s["normalized"], 1)

        @block.tensor
        def _(pe):
            for t in range(T):
                pe.wait_ge(s["normalized"], t + 1)
                for c in range(C):
                    last = pe.transpose(ps[:, 2 * c + t // 4, (t % 4) * P:(t % 4 + 1) * P],
                                        k.y[:, t, c * P:(c + 1) * P], k.ident[:, :])
                last.then_inc(s["transposed"], 1)

        @block.scalar
        def _(act):
            act.wait_ge(s["variance_ready"], 1)
            act.activation(std[:, :], var[:, :], ACT.Sqrt).then_inc(s["std_ready"], 1)
            for half in range(2):
                act.wait_ge(s["transposed"], 4 * (half + 1))
                for c in range(C):
                    act.activation(k.yT[:, c, half * HALF:(half + 1) * HALF], ps[:, 2 * c + half, :], ACT.Copy)
    k.end_stage()


def coupling_ffn(k):
    nc, s, ps, a = k.nc, k.sem, k.ps, k.a
    with ExitStack() as ctx:
        def sb(name, shape, dt=F32):
            return ctx.enter_context(nc.sbuf_tensor(k.unique(name), shape, dt))

        w1 = sb("cn_w1", [P, C, D])
        w2 = sb("cn_w2", [P, C, 128])
        w3 = sb("cn_w3", [P, 64])
        w4 = sb("cn_w4", [64, 1])
        w4r = sb("cn_w4r", [64, P])
        v1 = sb("gc_w1", [P, C, 128])
        v2 = sb("gc_w2", [P, 64])
        v3 = sb("gc_w3", [64, 1])
        v3r = sb("gc_w3r", [64, P])
        b1 = sb("cn_b1", [P, C])
        cols = sb("cn_cols", [P, 8])
        hb = sb("cn_hb", [P, 2])
        sign = sb("cn_sign", [P, 1])
        base = sb("cn_base", [P, 2])
        g = sb("cn_g", [P, 8])
        oT = [k.yT, sb("cn_oT0", [P, C, S]), sb("cn_oT1", [P, C, S])]
        h1 = sb("cn_h1", [P, C, S])
        h2 = sb("cn_h2", [P, S])
        h3 = sb("cn_h3", [64, S])
        th = sb("cn_th", [P, S])
        cs = sb("cn_cs", [P, S])
        tw = sb("cn_tw", [P, C, S])
        block = ctx.enter_context(nc.Block())
        state = [oT[0], oT[1], oT[2], oT[1]]
        @block.sync
        def _(sp):
            ld = s["loaded"]
            sp.dma_start(w1[:, :, :], a["L0_ffn_cn_w1"].rearrange("(c p) n -> p c n", p=P)).then_inc(ld, 16)
            sp.dma_start(w2[:, :, :], a["L0_ffn_cn_w2"].rearrange("(c p) n -> p c n", p=P)).then_inc(ld, 16)
            sp.dma_start(w3[:, :], a["L0_ffn_cn_w3"]).then_inc(ld, 16)
            sp.dma_start(w4[:, :], a["L0_ffn_cn_w4"]).then_inc(ld, 16)
            sp.dma_start(v1[:, :, :], a["L0_ffn_gc_w1"].rearrange("(c p) n -> p c n", p=P)).then_inc(ld, 16)
            sp.dma_start(v2[:, :], a["L0_ffn_gc_w2"]).then_inc(ld, 16)
            sp.dma_start(v3[:, :], a["L0_ffn_gc_w3"]).then_inc(ld, 16)
            sp.dma_start(b1[:, :], a["L0_ffn_cn_b1"].rearrange("(c p) -> p c", p=P)).then_inc(ld, 16)
            sp.dma_start(cols[:, 0:1], a["L0_ffn_cn_b2"].rearrange("(p o) -> p o", o=1)).then_inc(ld, 16)
            sp.dma_start(cols[0:64, 1:2], a["L0_ffn_cn_b3"].rearrange("(p o) -> p o", o=1)).then_inc(ld, 16)
            sp.dma_start(cols[:, 2:3], a["L0_ffn_cn_b4"].partition_broadcast(P)).then_inc(ld, 16)
            sp.dma_start(cols[:, 3:4], a["L0_ffn_gc_b1"].rearrange("(p o) -> p o", o=1)).then_inc(ld, 16)
            sp.dma_start(cols[0:64, 4:5], a["L0_ffn_gc_b2"].rearrange("(p o) -> p o", o=1)).then_inc(ld, 16)
            sp.dma_start(cols[:, 5:6], a["L0_ffn_gc_b3"].partition_broadcast(P)).then_inc(ld, 16)
            sp.dma_start(cols[:, 6:7], a["L0_ffn_adaptive_range"].partition_broadcast(P)).then_inc(ld, 16)

        NL = 15

        @block.vector
        def _(dve):
            link = stepper(dve, s["vector_step"])
            dve.memset(sign[0:64, :], 1.0)
            dve.memset(sign[64:128, :], -1.0)
            dve.tensor_reduce(g[:, 0:2], k.yT[:, :, :], AX.X, ALU.add)
            dve.wait_ge(s["loaded"], 16 * NL)
            dve.tensor_copy(w4r[:, :], w4[:, :].broadcast_to([64, P]))
            dve.tensor_copy(v3r[:, :], v3[:, :].broadcast_to([64, P]))
            dve.tensor_scalar(hb[:, 0:1], cols[:, 2:3], 0.5, None, ALU.mult)
            link(dve.tensor_scalar(hb[:, 1:2], cols[:, 5:6], 0.5, None, ALU.mult))
            dve.tensor_scalar(g[:, 2:4], g[:, 0:2], 1.0 / S, None, ALU.mult).then_inc(s["sums_ready"], 1)
            dve.wait_ge(s["columns_ready"], 1)
            link(dve.tensor_tensor(g[:, 7:8], g[:, 6:7], cols[:, 6:7], ALU.mult))
            link(dve.tensor_scalar(g[:, 7:8], g[:, 7:8], 0.7, 0.1, ALU.mult, ALU.add))
            dve.tensor_tensor(base[:, 0:1], g[:, 7:8], sign[:, :], ALU.mult)
            link(dve.scalar_tensor_tensor(out=base[:, 1:2], in0=cols[:, 6:7], scalar=0.3, in1=sign[:, :],
                                          op0=ALU.mult, op1=ALU.mult))
            for n in range(3):
                o, new = state[n], state[n + 1]
                for half in range(2):
                    q = slice(half * HALF, (half + 1) * HALF)
                    dve.wait_ge(s["activated"], 10 * n + 9 + half)
                    link(dve.tensor_scalar(cs[:, q], th[:, q], base[:, 1:2], base[:, 0:1], ALU.mult, ALU.add))
                    dve.tensor_tensor(tw[:, 0, q], cs[:, q], o[:, 1, q], ALU.mult)
                    link(dve.tensor_tensor(tw[:, 1, q], cs[:, q], o[:, 0, q], ALU.mult))
                    dve.tensor_tensor(new[:, 0, q], o[:, 0, q], tw[:, 0, q], ALU.add)
                    link(dve.tensor_tensor(new[:, 1, q], o[:, 1, q], tw[:, 1, q], ALU.subtract))
                    dve.sem_inc(s["state_updated"], 1)
            for j in range(4):
                dve.wait_ge(s["transposed"], j + 1)
                xv = k.x[:, 2 * j:2 * j + 2, :].rearrange("p t n -> p (t n)")
                dve.scalar_tensor_tensor(out=xv, in0=ps[:, j, :], scalar=0.5, in1=xv, op0=ALU.mult, op1=ALU.add)

        @block.tensor
        def _(pe):
            pe.wait_ge(s["sums_ready"], 1)
            for c in range(C):
                last = pe.matmul(ps[:, 7, 0:1], v1[:, c, :], g[:, 2 + c:3 + c], start=(c == 0), stop=(c == C - 1))
            last.then_inc(s["halfway"], 1)
            pe.wait_ge(s["rows_ready"], 1)
            pe.matmul(ps[0:64, 7, 1:2], v2[:, :], g[:, 4:5], start=True, stop=True).then_inc(s["halfway"], 1)
            pe.wait_ge(s["rows_ready"], 2)
            pe.matmul(ps[:, 7, 2:3], v3r[:, :], g[0:64, 5:6], start=True, stop=True).then_inc(s["halfway"], 1)
            pe.wait_ge(s["columns_ready"], 1)
            for n in range(3):
                o = state[n]
                for half in range(2):
                    if n:
                        pe.wait_ge(s["state_updated"], 2 * (n - 1) + half + 1)
                    for m in range(C):
                        for c in range(C):
                            last = pe.matmul(ps[:, 4 * half + m, :], w1[:, c, m * P:(m + 1) * P],
                                             o[:, c, half * HALF:(half + 1) * HALF], start=(c == 0), stop=(c == C - 1))
                    last.then_inc(s["multiplied"], 1)
                for half in range(2):
                    pe.wait_ge(s["activated"], 10 * n + 2 * (half + 1))
                    for c in range(C):
                        last = pe.matmul(ps[:, 4 * half + 2, :], w2[:, c, :], h1[:, c, half * HALF:(half + 1) * HALF],
                                         start=(c == 0), stop=(c == C - 1))
                    last.then_inc(s["multiplied"], 1)
                for half in range(2):
                    pe.wait_ge(s["activated"], 10 * n + 4 + half + 1)
                    pe.matmul(ps[0:64, 4 * half + 3, :], w3[:, :], h2[:, half * HALF:(half + 1) * HALF],
                              start=True, stop=True).then_inc(s["multiplied"], 1)
                for half in range(2):
                    pe.wait_ge(s["activated"], 10 * n + 6 + half + 1)
                    pe.matmul(ps[:, 4 * half, :], w4r[:, :], h3[:, half * HALF:(half + 1) * HALF],
                              start=True, stop=True).then_inc(s["multiplied"], 1)
            o = state[3]
            for t in range(T):
                pe.wait_ge(s["state_updated"], 5 + t // 4)
                for c in range(C):
                    last = pe.transpose(ps[:, t // 2, (t % 2) * D + c * P:(t % 2) * D + (c + 1) * P],
                                        o[:, c, t * P:(t + 1) * P], k.ident[:, :])
                if t % 2:
                    last.then_inc(s["transposed"], 1)

        @block.scalar
        def _(act):
            act.wait_ge(s["halfway"], 1)
            act.activation(g[:, 4:5], ps[:, 7, 0:1], ACT.Gelu, bias=cols[:, 3:4]).then_inc(s["rows_ready"], 1)
            act.wait_ge(s["halfway"], 2)
            act.activation(g[0:64, 5:6], ps[0:64, 7, 1:2], ACT.Gelu, bias=cols[0:64, 4:5]).then_inc(s["rows_ready"], 1)
            act.wait_ge(s["halfway"], 3)
            act.activation(g[:, 6:7], ps[:, 7, 2:3], ACT.Tanh, bias=hb[:, 1:2], scale=0.5).then_inc(s["columns_ready"], 1)
            for n in range(3):
                for half in range(2):
                    q = slice(half * HALF, (half + 1) * HALF)
                    act.wait_ge(s["multiplied"], 8 * n + half + 1)
                    for m in range(C):
                        act.activation(h1[:, m, q], ps[:, 4 * half + m, :], ACT.Gelu,
                                       bias=b1[:, m:m + 1]).then_inc(s["activated"], 1)
                for half in range(2):
                    q = slice(half * HALF, (half + 1) * HALF)
                    act.wait_ge(s["multiplied"], 8 * n + 3 + half)
                    act.activation(h2[:, q], ps[:, 4 * half + 2, :], ACT.Gelu, bias=cols[:, 0:1]).then_inc(s["activated"], 1)
                for half in range(2):
                    q = slice(half * HALF, (half + 1) * HALF)
                    act.wait_ge(s["multiplied"], 8 * n + 5 + half)
                    act.activation(h3[:, q], ps[0:64, 4 * half + 3, :], ACT.Gelu,
                                   bias=cols[0:64, 1:2]).then_inc(s["activated"], 1)
                for half in range(2):
                    q = slice(half * HALF, (half + 1) * HALF)
                    act.wait_ge(s["multiplied"], 8 * n + 7 + half)
                    act.activation(th[:, q], ps[:, 4 * half, :], ACT.Tanh, bias=hb[:, 0:1], scale=0.5).then_inc(s["activated"], 1)
    k.end_stage()


def expert_ffn(k):
    nc, s, ps, a = k.nc, k.sem, k.ps, k.a
    with ExitStack() as ctx:
        def sb(name, shape, dt=F32):
            return ctx.enter_context(nc.sbuf_tensor(k.unique(name), shape, dt))

        rw = sb("e_rw", [P, C, E1])
        rb = sb("e_rb", [P, E1])
        w1 = sb("e_w1", [P, E1, C, F1])
        w2 = sb("e_w2", [P, E1, D])
        b1 = sb("e_b1", [P, E1])
        b2 = sb("e_b2", [E1, D])
        logit = sb("e_logit", [P, T, E1])
        best = sb("e_best", [P, T, 8])
        bi = sb("e_bi", [P, T, 8], U32)
        bf = sb("e_bf", [P, T, 8])
        number = sb("e_number", [P, T, E1])
        gap = sb("e_gap", [P, T])
        wt = sb("e_wt", [P, 3, T])
        mask = sb("e_mask", [P, T, E1])
        pick = sb("e_pick", [P, T, E1])
        maskT = sb("e_maskT", [E1, S])
        h1 = sb("e_h1", [P, 2, S])
        acc = sb("e_acc", [P, T, D])
        block = ctx.enter_context(nc.Block())

        @block.sync
        def _(sp):
            ld = s["loaded"]
            sp.dma_start(rw[:, :, :], a["L1_ffn_router_w"].rearrange("(c p) n -> p c n", p=P)).then_inc(ld, 16)
            sp.dma_start(rb[:, :], a["L1_ffn_router_b"].partition_broadcast(P)).then_inc(ld, 16)
            for e in range(E1):
                sp.dma_start(w1[:, e, :, :], a["L1_ffn_W1"][e].rearrange("(c p) n -> p c n", p=P)).then_inc(ld, 16)
            sp.dma_start(b1[:, :], a["L1_ffn_b1"].rearrange("e p -> p e")).then_inc(ld, 16)
            sp.dma_start(w2[:, :, :], a["L1_ffn_W2"].rearrange("e p n -> p e n")).then_inc(ld, 16)
            sp.dma_start(b2[:, :], a["L1_ffn_b2"]).then_inc(ld, 16)

        NL = 5 + E1

        @block.gpsimd
        def _(pool):
            pool.iota(number[:, :, :], pattern=[[0, T], [1, E1]], base=0, channel_multiplier=0,
                      allow_small_or_imprecise_dtypes=True).then_inc(s["pool_step"], 1)

        @block.tensor
        def _(pe):
            pe.wait_ge(s["loaded"], 16 * NL)
            for t in range(T):
                for c in range(C):
                    last = pe.matmul(ps[:, 7, t * E1:(t + 1) * E1], k.yT[:, c, t * P:(t + 1) * P], rw[:, c, :],
                                     start=(c == 0), stop=(c == C - 1))
            last.then_inc(s["scored"], 1)

            def up(e):
                if e >= 2:
                    pe.wait_ge(s["activated"], 2 * (e - 1))
                for half in range(2):
                    for c in range(C):
                        last = pe.matmul(ps[:, 2 * (e % 2) + half, :], w1[:, e, c, :],
                                         k.yT[:, c, half * HALF:(half + 1) * HALF], start=(c == 0), stop=(c == C - 1))
                    last.then_inc(s["multiplied"], 1)

            def down(e):
                for j in range(T // 2):
                    n = (T // 2) * e + j
                    if n >= 3:
                        pe.wait_ge(s["weighted"], n - 2)
                    pe.wait_ge(s["activated"], 2 * e + j // 2 + 1)
                    for i in range(2):
                        t = 2 * j + i
                        last = pe.matmul(ps[:, 4 + n % 3, i * D:(i + 1) * D], h1[:, e % 2, t * P:(t + 1) * P],
                                         w2[:, e, :], start=True, stop=True)
                    last.then_inc(s["merged_ready"], 1)

            up(0)
            for e in range(E1):
                if e + 1 < E1:
                    up(e + 1)
                down(e)
            pe.wait_ge(s["routed"], 1)
            pe.wait_ge(s["weighted"], (T // 2) * E1)
            for t in range(T):
                last = pe.transpose(ps[0:E1, t // 4, (t % 4) * P:(t % 4 + 1) * P], mask[:, t, :], k.ident[:, :])
            last.then_inc(s["transposed"], 1)
            pe.wait_ge(s["columns_ready"], 1)
            for t in range(T):
                last = pe.matmul(ps[:, 4 + t // 2, (t % 2) * D:(t % 2 + 1) * D], maskT[:, t * P:(t + 1) * P], b2[:, :],
                                 start=True, stop=True)
            last.then_inc(s["results_ready"], 1)

        @block.scalar
        def _(act):
            for e in range(E1):
                if e == 1:
                    act.wait_ge(s["sums_ready"], 1)
                    act.activation(wt[:, 0, :], gap[:, :], ACT.Exp).then_inc(s["exponentiated"], 1)
                if e >= 2:
                    act.wait_ge(s["merged_ready"], (T // 2) * (e - 1))
                for half in range(2):
                    act.wait_ge(s["multiplied"], 2 * e + half + 1)
                    act.activation(h1[:, e % 2, half * HALF:(half + 1) * HALF], ps[:, 2 * (e % 2) + half, :], ACT.Gelu,
                                   bias=b1[:, e:e + 1]).then_inc(s["activated"], 1)
            act.wait_ge(s["transposed"], 1)
            act.activation(maskT[:, :].rearrange("p (a b) -> p a b", a=2), ps[0:E1, 0:2, :], ACT.Copy).then_inc(s["columns_ready"], 1)

        @block.vector
        def _(dve):
            link = stepper(dve, s["vector_step"])
            dve.wait_ge(s["scored"], 1)
            link(dve.tensor_tensor(logit[:, :, :], ps[:, 7, 0:T * E1].rearrange("p (t e) -> p t e", t=T),
                                   rb[:, :].unsqueeze(1).broadcast_to([P, T, E1]), ALU.add))
            for t in range(T):
                last = dve.max(best[:, t, :], logit[:, t, :])
            link(last)
            for t in range(T):
                last = dve.max_index(bi[:, t, :], best[:, t, :], logit[:, t, :])
            link(last)
            dve.tensor_tensor(gap[:, :], best[:, :, 1], best[:, :, 0], ALU.subtract).then_inc(s["sums_ready"], 1)
            link(dve.tensor_copy(bf[:, :, :], bi[:, :, :]))
            dve.wait_ge(s["exponentiated"], 1)
            link(dve.tensor_scalar(wt[:, 2, :], wt[:, 0, :], 1.0, None, ALU.add))
            link(dve.reciprocal(wt[:, 1, :], wt[:, 2, :]))
            link(dve.tensor_tensor(wt[:, 2, :], wt[:, 0, :], wt[:, 1, :], ALU.mult))
            dve.wait_ge(s["pool_step"], 1)
            for i, m in ((0, mask), (1, pick)):
                link(dve.tensor_tensor(m[:, :, :], number[:, :, :], bf[:, :, i:i + 1].broadcast_to([P, T, E1]), ALU.is_equal))
                link(dve.tensor_tensor(m[:, :, :], m[:, :, :], wt[:, 1 + i, :].unsqueeze(2).broadcast_to([P, T, E1]), ALU.mult))
            dve.tensor_tensor(mask[:, :, :], mask[:, :, :], pick[:, :, :], ALU.add).then_inc(s["routed"], 1)
            dve.wait_ge(s["routed"], 1)
            for e in range(E1):
                for j in range(T // 2):
                    n = (T // 2) * e + j
                    dve.wait_ge(s["merged_ready"], n + 1)
                    for i in range(2):
                        t = 2 * j + i
                        src = ps[:, 4 + n % 3, i * D:(i + 1) * D]
                        if e == 0:
                            last = dve.tensor_scalar(acc[:, t, :], src, mask[:, t, e:e + 1], None, ALU.mult)
                        else:
                            last = dve.scalar_tensor_tensor(out=acc[:, t, :], in0=src, scalar=mask[:, t, e:e + 1],
                                                            in1=acc[:, t, :], op0=ALU.mult, op1=ALU.add)
                    last.then_inc(s["weighted"], 1)
                dve.wait_ge(s["weighted"], (T // 2) * (e + 1))
            dve.wait_ge(s["results_ready"], 1)
            av = acc[:, :, :].rearrange("p (j t) n -> p j (t n)", t=2)
            xv = k.x[:, :, :].rearrange("p (j t) n -> p j (t n)", t=2)
            link(dve.tensor_tensor(av, av, ps[:, 4:8, :], ALU.add))
            dve.scalar_tensor_tensor(out=xv, in0=av, scalar=0.5, in1=xv, op0=ALU.mult, op1=ALU.add)
    k.end_stage()


def lora_ffn(k):
    nc, s, ps, a = k.nc, k.sem, k.ps, k.a
    NE = len(RANKS)
    with ExitStack() as ctx:
        def sb(name, shape, dt=F32):
            return ctx.enter_context(nc.sbuf_tensor(k.unique(name), shape, dt))

        w = sb("r_w", [P, C, D])
        wp = sb("r_wp", [P, C, PR])
        wd = sb("r_wd", [P, C, RT])
        wu = sb("r_wu", [RT, D])
        bp = sb("r_bp", [PR, 1])
        sim = sb("r_sim", [PR, NE])
        simq = sb("r_simq", [PR, 4, NE])
        temp = sb("r_temp", [P, 2])
        proj = sb("r_proj", [PR, S])
        projq = sb("r_projq", [PR, S])
        norm = sb("r_norm", [P, T])
        inv = sb("r_inv", [P, T])
        logit = sb("r_logit", [P, T, 8])
        prob = sb("r_prob", [P, T, 8])
        best = sb("r_best", [P, T, 8])
        bi = sb("r_bi", [P, T, 8], U32)
        bf = sb("r_bf", [P, T, 8])
        total = sb("r_total", [P, 2, T])
        number = sb("r_number", [P, T, NE])
        ret = sb("r_ret", [P, T, NE])
        down = sb("r_down", [P, T, RT])
        downT = sb("r_downT", [RT, S])
        block = ctx.enter_context(nc.Block())

        @block.sync
        def _(sp):
            ld = s["loaded"]
            sp.dma_start(w[:, :, :], a["L2_ffn_WT"].rearrange("(c p) n -> p c n", p=P)).then_inc(ld, 16)
            sp.dma_start(wp[:, :, :], a["L2_ffn_WpT"].rearrange("(c p) n -> p c n", p=P)).then_inc(ld, 16)
            sp.dma_start(wd[:, :, :], a["L2_ffn_WdT"].rearrange("(c p) n -> p c n", p=P)).then_inc(ld, 16)
            sp.dma_start(wu[:, :], a["L2_ffn_WuT"]).then_inc(ld, 16)
            sp.dma_start(bp[:, :], a["L2_ffn_bp"].rearrange("(p o) -> p o", o=1)).then_inc(ld, 16)
            sp.dma_start(sim[:, :], a["L2_ffn_sim"]).then_inc(ld, 16)
            sp.dma_start(temp[:, 0:1], a["L2_ffn_temp"].partition_broadcast(P)).then_inc(ld, 16)

        NL = 7

        @block.gpsimd
        def _(pool):
            pool.iota(number[:, :, :], pattern=[[0, T], [1, NE]], base=0, channel_multiplier=0,
                      allow_small_or_imprecise_dtypes=True).then_inc(s["pool_step"], 1)

        @block.tensor
        def _(pe):
            pe.wait_ge(s["loaded"], 16 * NL)
            for half in range(2):
                for c in range(C):
                    last = pe.matmul(ps[0:PR, half, :], wp[:, c, :], k.yT[:, c, half * HALF:(half + 1) * HALF],
                                     start=(c == 0), stop=(c == C - 1))
                last.then_inc(s["multiplied"], 1)
            for t in range(T):
                for c in range(C):
                    last = pe.matmul(ps[:, 3, t * RT:(t + 1) * RT], k.yT[:, c, t * P:(t + 1) * P], wd[:, c, :],
                                     start=(c == 0), stop=(c == C - 1))
            last.then_inc(s["columns_ready"], 1)
            pe.wait_ge(s["sums_ready"], 1)
            pe.matmul(ps[0:PR, 2, 0:NE], k.ones[0:PR, 0:PR], simq[:, 0, :], start=True, stop=True).then_inc(s["rows_ready"], 1)
            pe.wait_ge(s["activated"], 4)
            pe.wait_ge(s["split_ready"], 1)
            for t in range(T):
                pe.matmul(ps[:, 2, 64 + t * NE:64 + (t + 1) * NE], proj[:, t * P:(t + 1) * P], simq[:, 3, :], start=True, stop=True)
                last = pe.matmul(ps[:, 2, 128 + t:129 + t], projq[:, t * P:(t + 1) * P], k.ones[0:PR, 0:1], start=True, stop=True)
            last.then_inc(s["scored"], 1)
            for t in range(T):
                for c in range(C):
                    pe.matmul(ps[:, 4 + t // 2, (t % 2) * D:(t % 2 + 1) * D], k.yT[:, c, t * P:(t + 1) * P], w[:, c, :],
                              start=(c == 0), stop=False)
                if t == 0:
                    pe.wait_ge(s["weighted"], 1)
                    for u in range(T):
                        last = pe.transpose(ps[0:RT, u // 4, (u % 4) * P:(u % 4 + 1) * P], down[:, u, :], k.ident[:, :])
                    last.then_inc(s["transposed"], 1)
                    pe.wait_ge(s["halfway"], 1)
                last = pe.matmul(ps[:, 4 + t // 2, (t % 2) * D:(t % 2 + 1) * D], downT[:, t * P:(t + 1) * P], wu[:, :],
                                 start=False, stop=True)
                if t % 2:
                    last.then_inc(s["results_ready"], 1)

        @block.scalar
        def _(act):
            for half in range(2):
                act.wait_ge(s["multiplied"], half + 1)
                q = slice(half * HALF, (half + 1) * HALF)
                act.activation(proj[:, q], ps[0:PR, half, :], ACT.Identity, bias=bp[:, :]).then_inc(s["activated"], 1)
                act.activation(projq[:, q], ps[0:PR, half, :], ACT.Square, bias=bp[:, :]).then_inc(s["activated"], 1)
            act.wait_ge(s["rows_ready"], 1)
            act.activation(simq[:, 1, :], ps[0:PR, 2, 0:NE], ACT.Sqrt).then_inc(s["std_ready"], 1)
            act.wait_ge(s["scored"], 1)
            act.activation(norm[:, :], ps[:, 2, 128:128 + T], ACT.Sqrt).then_inc(s["std_ready"], 1)
            act.wait_ge(s["variance_ready"], 1)
            act.activation(temp[:, 1:2], temp[:, 1:2], ACT.Exp).then_inc(s["exponentiated"], 1)
            act.wait_ge(s["max_taken"], 1)
            act.activation(prob[:, :, :], prob[:, :, :], ACT.Exp).then_inc(s["exponentiated"], 1)
            act.wait_ge(s["transposed"], 1)
            act.activation(downT[:, :].rearrange("p (a b) -> p a b", a=2), ps[0:RT, 0:2, :], ACT.Copy).then_inc(s["halfway"], 1)

        @block.vector
        def _(dve):
            link = stepper(dve, s["vector_step"])
            dve.memset(logit[:, :, :], LOWEST)
            dve.wait_ge(s["loaded"], 16 * NL)
            dve.tensor_tensor(simq[:, 0, :], sim[:, :], sim[:, :], ALU.mult).then_inc(s["sums_ready"], 1)
            dve.tensor_scalar(temp[:, 1:2], temp[:, 0:1], float(np_log100()), None, ALU.min).then_inc(s["variance_ready"], 1)
            dve.wait_ge(s["std_ready"], 1)
            link(dve.tensor_scalar(simq[:, 1, :], simq[:, 1, :], 1e-12, None, ALU.max))
            link(dve.reciprocal(simq[:, 2, :], simq[:, 1, :]))
            dve.tensor_tensor(simq[:, 3, :], sim[:, :], simq[:, 2, :], ALU.mult).then_inc(s["split_ready"], 1)
            dve.wait_ge(s["std_ready"], 2)
            link(dve.tensor_scalar(norm[:, :], norm[:, :], 1e-12, None, ALU.max))
            link(dve.reciprocal(inv[:, :], norm[:, :]))
            dve.wait_ge(s["exponentiated"], 1)
            link(dve.tensor_scalar(inv[:, :], inv[:, :], temp[:, 1:2], None, ALU.mult))
            link(dve.tensor_tensor(logit[:, :, 0:NE], ps[:, 2, 64:64 + T * NE].rearrange("p (t e) -> p t e", t=T),
                                   inv[:, :].unsqueeze(2).broadcast_to([P, T, NE]), ALU.mult))
            for t in range(T):
                last = dve.max(best[:, t, :], logit[:, t, :])
            link(last)
            for t in range(T):
                last = dve.max_index(bi[:, t, :], best[:, t, :], logit[:, t, :])
            link(last)
            dve.tensor_tensor(prob[:, :, :], logit[:, :, :], best[:, :, 0:1].broadcast_to([P, T, 8]),
                              ALU.subtract).then_inc(s["max_taken"], 1)
            link(dve.tensor_copy(bf[:, :, :], bi[:, :, :]))
            dve.wait_ge(s["exponentiated"], 2)
            link(dve.tensor_reduce(total[:, 0, :], prob[:, :, 0:NE], AX.X, ALU.add))
            dve.reciprocal(total[:, 1, :], total[:, 0, :])
            dve.wait_ge(s["pool_step"], 1)
            link(dve.tensor_tensor(ret[:, :, :], number[:, :, :], bf[:, :, 0:1].broadcast_to([P, T, NE]), ALU.is_equal))
            link(dve.tensor_tensor(ret[:, :, :], ret[:, :, :], total[:, 1, :].unsqueeze(2).broadcast_to([P, T, NE]), ALU.mult))
            dve.wait_ge(s["columns_ready"], 1)
            r0 = 0
            for e, r in enumerate(RANKS):
                last = dve.tensor_tensor(down[:, :, r0:r0 + r],
                                         ps[:, 3, 0:T * RT].rearrange("p (t r) -> p t r", t=T)[:, :, r0:r0 + r],
                                         ret[:, :, e:e + 1].broadcast_to([P, T, r]), ALU.mult)
                r0 += r
            last.then_inc(s["weighted"], 1)
            for j in range(T // 2):
                dve.wait_ge(s["results_ready"], j + 1)
                xv = k.x[:, 2 * j:2 * j + 2, :].rearrange("p t n -> p (t n)")
                dve.scalar_tensor_tensor(out=xv, in0=ps[:, 4 + j, :], scalar=0.5, in1=xv, op0=ALU.mult, op1=ALU.add)
    k.end_stage()


def np_log100():
    import numpy as np
    return np.log(1.0 / 0.01)


def gaussian_attention(k):
    import math
    nc, s, ps, a = k.nc, k.sem, k.ps, k.a
    NB = len(STD)
    reach = math.sqrt(2 * 104.0)
    assert max(sd * reach + off for sd, off in zip(STD, STD)) < P
    with ExitStack() as ctx:
        def sb(name, shape, dt=F32):
            return ctx.enter_context(nc.sbuf_tensor(k.unique(name), shape, dt))

        wi = sb("g_wi", [P, C, D])
        wo = sb("g_wo", [P, C, D])
        dist = sb("g_dist", [P, 3 * P])
        sq = sb("g_sq", [P, NB, 3 * P])
        band = sb("g_band", [P, NB, 3 * P])
        v = sb("g_v", [P, T, D])
        at = sb("g_at", [P, C, S])
        block = ctx.enter_context(nc.Block())

        @block.sync
        def _(sp):
            sp.dma_start(wi[:, :, :], a["L3_attn_input_weightsT"].rearrange("(c p) n -> p c n", p=P)).then_inc(s["loaded"], 16)
            sp.dma_start(wo[:, :, :], a["L3_attn_output_weightT"].rearrange("(c p) n -> p c n", p=P)).then_inc(s["loaded"], 16)

        @block.gpsimd
        def _(pool):
            pool.iota(dist[:, :], pattern=[[-1, 3 * P]], base=P, channel_multiplier=1,
                      allow_small_or_imprecise_dtypes=True).then_inc(s["pool_step"], 1)

        @block.vector
        def _(dve):
            link = stepper(dve, s["vector_step"])
            dve.wait_ge(s["pool_step"], 1)
            for i, sd in enumerate(STD):
                last = dve.tensor_scalar(sq[:, i, :], dist[:, :], sd, 1.0 / sd, ALU.add, ALU.mult)
            link(last)
            dve.tensor_tensor(sq[:, :, :], sq[:, :, :], sq[:, :, :], ALU.mult).then_inc(s["sums_ready"], 1)
            dve.wait_ge(s["exponentiated"], 1)
            for i, sd in enumerate(STD):
                last = dve.tensor_scalar(band[:, i, :], sq[:, i, :], 1.0 / (sd * math.sqrt(2.0 * math.pi)), None, ALU.mult)
            last.then_inc(s["probs_ready"], 1)
            for j in range(T // 2):
                dve.wait_ge(s["results_ready"], j + 1)
                xv = k.x[:, 2 * j:2 * j + 2, :].rearrange("p t n -> p (t n)")
                dve.tensor_tensor(xv, ps[:, 4 + j, :], xv, ALU.add)

        @block.scalar
        def _(act):
            act.wait_ge(s["sums_ready"], 1)
            act.activation(sq[:, :, :], sq[:, :, :], ACT.Exp, scale=-0.5).then_inc(s["exponentiated"], 1)
            for j in range(T // 2):
                act.wait_ge(s["multiplied"], j + 1)
                act.activation(v[:, 2 * j:2 * j + 2, :].rearrange("p t n -> p (t n)"), ps[:, 4 + j, :], ACT.Copy).then_inc(s["v_ready"], 1)
            for c in range(C):
                for half in range(2):
                    act.wait_ge(s["weighted"], 2 * c + half + 1)
                    act.activation(at[:, c, half * HALF:(half + 1) * HALF], ps[:, 2 * c + half, :], ACT.Copy).then_inc(s["heads_done"], 1)

        @block.tensor
        def _(pe):
            pe.wait_ge(s["loaded"], 32)
            for t in range(T):
                for c in range(C):
                    last = pe.matmul(ps[:, 4 + t // 2, (t % 2) * D:(t % 2 + 1) * D], k.yT[:, c, t * P:(t + 1) * P], wi[:, c, :],
                                     start=(c == 0), stop=(c == C - 1))
                if t % 2:
                    last.then_inc(s["multiplied"], 1)
            pe.wait_ge(s["v_ready"], T // 2)
            pe.wait_ge(s["probs_ready"], 1)
            for c in range(C):
                for qt in range(T):
                    near = [kt for kt in (qt - 1, qt, qt + 1) if 0 <= kt < T]
                    for kt in near:
                        for hh in range(G):
                            last = pe.matmul(ps[32 * hh:32 * hh + 32, 2 * c + qt // 4, (qt % 4) * P:(qt % 4 + 1) * P],
                                             v[:, kt, c * P + 32 * hh:c * P + 32 * hh + 32],
                                             band[:, hh, (qt - kt + 1) * P:(qt - kt + 2) * P],
                                             start=(kt == near[0]), stop=(kt == near[-1]), tile_position=(0, 32 * hh))
                    if qt % 4 == 3:
                        last.then_inc(s["weighted"], 1)
            pe.wait_ge(s["heads_done"], 4)
            for t in range(T):
                for c in range(C):
                    last = pe.matmul(ps[:, 4 + t // 2, (t % 2) * D:(t % 2 + 1) * D], at[:, c, t * P:(t + 1) * P], wo[:, c, :],
                                     start=(c == 0), stop=(c == C - 1))
                if t % 2:
                    last.then_inc(s["results_ready"], 1)
    k.end_stage()


def attention_plan(variant):
    def maxima(g):
        return [(g, hh, qt, ch) for hh in range(G) for qt in range(T)
                for ch in range(2 if variant else qt // 4 + 1)]

    plan, nmax, nscore = [], 0, 0

    def take(steps):
        nonlocal nmax
        for st in steps:
            plan.append(("max", nmax) + st)
            nmax += 1
    take(maxima(0))
    plan.append(("turn", 0))
    late = []
    for g in range(NG):
        steps = [(half, kt) for half in range(2) for kt in range(T if variant else 4 * half + 4)]
        todo = maxima(g + 1) if g + 1 < NG else []
        done, turned = 0, not todo
        for i, (half, kt) in enumerate(steps):
            for pair in range(2):
                plan.append(("score", nscore, g, half, kt, pair))
                nscore += 1
            upto = min(len(todo), -(-len(todo) * (i + 1) // (len(steps) - 2)))
            take(todo[done:upto])
            done = upto
            plan.extend(late)
            late = [("weigh", nscore // 2 - 1, g, half, kt)]
            if (half, kt) == steps[-1] or steps[i + 1][0] != half:
                late.append(("finish", 2 * g + half))
            if done == len(todo) and not turned:
                plan.append(("turn", g + 1))
                turned = True
    plan.extend(late)
    return plan


def attention(k, variant):
    nc, s, ps, a = k.nc, k.sem, k.ps, k.a
    plan = attention_plan(variant)
    name = ("L0_attn_", "L1_attn_", "L2_attn_")[variant]
    TABLE = 2 * S - P
    ROWS_ = 16 * NG
    with ExitStack() as outer:
        def osb(n, shape, dt=F32):
            return outer.enter_context(nc.sbuf_tensor(k.unique(n), shape, dt))

        va = osb("a_va", [P, T, H, PAD])
        qa = osb("a_qa", [P, H, S], BF16)
        ka = osb("a_ka", [P, H, S], BF16)
        bo = osb("a_bo", [P, D])
        wo = osb("a_wo", [P, G, D])

        with ExitStack() as ctx:
            def sb(n, shape, dt=F32):
                return ctx.enter_context(nc.sbuf_tensor(k.unique(n), shape, dt))

            w = [sb("a_wq", [P, C, D]), sb("a_wk", [P, C, D])]
            wr = [sb("a_wqr", [P, C, D]), sb("a_wkr", [P, C, D])] if variant == 1 else w
            tmp = sb("a_tmp", [P, C * D]) if variant == 1 else None
            wv = sb("a_wv", [P, C, D])
            brow = sb("a_brow", [1, 2, D])
            browr = sb("a_browr", [1, 2, D]) if variant == 1 else brow
            bcol = sb("a_bcol", [P, 2 * C])
            bv = sb("a_bv", [P, D])
            turnc = sb("a_turnc", [P, 2, DK]) if variant == 1 else None
            yo = k.yT if variant else sb("a_yo", [P, C, S])
            qf = sb("a_qf", [P, 2, C, S])
            parts = sb("a_parts", [P, 2, 3, C, S], BF16)
            vn = sb("a_vn", [P, T, D]) if variant == 1 else None
            block = ctx.enter_context(nc.Block())
            NL = 8 + G + (2 if variant == 1 else 0)
            bounced = [s["bounced0"], s["bounced1"]]
            NBOUNCE = 2 * T if variant == 1 else 2

            @block.sync
            def _(sp):
                ld = s["loaded"]
                if variant == 2:
                    wT, b = a["L2_attn_qkv_wT"], a["L2_attn_qkv_b"]
                    src = [wT[:, i * D:(i + 1) * D] for i in range(3)] + [b[i * D:(i + 1) * D] for i in range(3)]
                    src += [a["L2_attn_out_wT"], a["L2_attn_out_b"]]
                elif variant == 1:
                    src = [a[name + n] for n in ("wqT", "wkT", "wvT", "bq", "bk", "bv", "woT", "bo")]
                else:
                    src = [a[name + n] for n in ("WqT", "WkT", "WvT", "bq", "bk", "bv", "WoT", "bo")]
                for i, dst in enumerate((w[0], w[1], wv)):
                    sp.dma_start(dst[:, :, :], src[i].rearrange("(c p) n -> p c n", p=P)).then_inc(ld, 16)
                for i in range(2):
                    sp.dma_start(brow[:, i, :], src[3 + i].rearrange("(o n) -> o n", o=1)).then_inc(ld, 16)
                sp.dma_start(bv[:, :], src[5].partition_broadcast(P)).then_inc(ld, 16)
                sp.dma_start(bo[:, :], src[7].partition_broadcast(P)).then_inc(ld, 16)
                sp.dma_start(ka[KT:KT + 3, :, :], k.ones_rows[0:3].rearrange("a (h n) -> a h n", h=H)).then_inc(ld, 16)
                if variant == 1:
                    for i, n in enumerate(("cos", "sin")):
                        sp.dma_start(turnc[:, i, :], a[name + n][a[name + n].shape[0] - 1].partition_broadcast(P)).then_inc(ld, 16)
                sp.wait_ge(s["cleared"], 1)
                for hh in range(G):
                    sp.dma_start(wo[PAD * hh:PAD * hh + DK, :, :],
                                 src[6].rearrange("(g h d) n -> h d g n", h=G, d=DK)[hh]).then_inc(ld, 16)

                def bring(g):
                    for r, pair in enumerate(TERMS):
                        for qk, dst in ((0, qa), (1, ka)):
                            sp.dma_start(dst[DK * r:DK * r + DK, G * g:G * g + G, :],
                                         k.qk_parts[qk, pair[qk], G * DK * g:G * DK * (g + 1), :]
                                         .rearrange("(h d) n -> d h n", d=DK)).then_inc(s[f"heads_loaded{g}"], 16)

                for m in range(C):
                    for qk in range(2):
                        sp.wait_ge(s["split_ready"], 2 * m + qk + 1)
                        if variant == 1:
                            for c in range(T):
                                dst = k.qk_parts[qk].rearrange("x (h d) (c l) -> c d x h l", d=DK, c=H)[T * m + c]
                                for x in range(3):
                                    sp.dma_start(dst[:, x], parts[DK * c:DK * c + DK, qk, x, m, :]
                                                 .rearrange("d (h l) -> d h l", h=H)).then_inc(bounced[m], 16)
                        else:
                            sp.dma_start(k.qk_parts[qk, :, m * P:(m + 1) * P, :].rearrange("x f n -> f x n"),
                                         parts[:, qk, :, m, :]).then_inc(bounced[m], 16)
                    if variant != 1:
                        sp.wait_ge(bounced[m], 16 * NBOUNCE)
                        bring(2 * m)
                        bring(2 * m + 1)
                if variant == 1:
                    for m in range(C):
                        sp.wait_ge(bounced[m], 16 * 3 * NBOUNCE)
                    for g in range(NG):
                        bring(g)
                    sp.wait_ge(s["v_ready"], T // 2)
                    sp.dma_start(k.v_rows.rearrange("(t p) n -> p t n", p=P), vn[:, :, :]).then_inc(s["v_bounced"], 16)
                    sp.wait_ge(s["v_bounced"], 16)
                    for kt in range(T):
                        for c in range(2):
                            sp.dma_start(va[64 * c:64 * c + 64, kt, :, 0:DK],
                                         k.v_rows.rearrange("(h l) (c d) -> c l h d", h=H, d=DK)[2 * kt + c])\
                              .then_inc(s["v_loaded"], 16)
                    sp.wait_ge(s["v_loaded"], 16 * 2 * T)
                for g in range(NG):
                    sp.wait_ge(s[f"heads_loaded{g}"], 16 * 2 * len(TERMS))
                sp.wait_ge(ld, 16 * NL)

            @block.tensor
            def _(pe):
                pe.wait_ge(s["loaded"], 16 * NL)
                if variant == 1:
                    pe.wait_ge(s["rotated"], 1)
                for i in range(2):
                    for m in range(C):
                        last = pe.matmul(ps[:, 7, 2 * i + m:2 * i + m + 1], browr[0:1, i, m * P:(m + 1) * P], k.ones[0:1, 0:1],
                                         start=True, stop=True)
                last.then_inc(s["rows_ready"], 1)
                if not variant:
                    pe.wait_ge(s["transposed"], C)
                n = 0
                for m in range(C):
                    for qk in range(2):
                        for half in range(2):
                            if n >= 6:
                                pe.wait_ge(s["activated"], n - 5)
                            for c in range(C):
                                last = pe.matmul(ps[:, n % 6, :], wr[qk][:, c, m * P:(m + 1) * P],
                                                 yo[:, c, half * HALF:(half + 1) * HALF], start=(c == 0), stop=(c == C - 1))
                            last.then_inc(s["multiplied"], 1)
                            n += 1
                pe.wait_ge(s["columns_ready"], 1)
                for t in range(T):
                    if t >= 4 and t % 2 == 0:
                        pe.wait_ge(s["v_ready"], t // 2 - 1)
                    for c in range(C):
                        last = pe.matmul(ps[:, 6 + t // 2 % 2, (t % 2) * D:(t % 2 + 1) * D], yo[:, c, t * P:(t + 1) * P], wv[:, c, :],
                                         start=(c == 0), stop=(c == C - 1))
                    if t % 2:
                        last.then_inc(s["v_scored"], 1)

            @block.scalar
            def _(act):
                n = 0
                if not variant:
                    for c in range(C):
                        act.activation(yo[:, c, :].rearrange("p (r t) -> p t r", t=T),
                                       k.yT[:, c, :].rearrange("p (t r) -> p t r", t=T), ACT.Copy).then_inc(s["transposed"], 1)
                act.wait_ge(s["columns_ready"], 1)
                for m in range(C):
                    for qk in range(2):
                        for half in range(2):
                            act.wait_ge(s["multiplied"], n + 1)
                            act.activation(qf[:, qk, m, half * HALF:(half + 1) * HALF], ps[:, n % 6, :], ACT.Identity, bias=bcol[:, 2 * qk + m:2 * qk + m + 1]).then_inc(s["activated"], 1)
                            n += 1

            @block.vector
            def _(dve):
                link = stepper(dve, s["vector_step"])
                dve.memset(wo[:, :, :], 0.0).then_inc(s["cleared"], 1)
                dve.memset(va[:, :, :, DK + 1:PAD], 0.0)
                dve.memset(va[:, :, :, DK:DK + 1], 1.0)
                if variant == 1:
                    dve.wait_ge(s["loaded"], 16 * (NL - G))
                    dve.wait_ge(s["loaded"], 16 * NL)
                    for src, dst, np_, nr in ((w[0], wr[0], P, C * H), (w[1], wr[1], P, C * H), (brow, browr, 1, 2 * H)):
                        sv = src[:, :, :].rearrange("p c (h e o) -> p (c h) e o", o=2, e=DK // 2)
                        dv = dst[:, :, :].rearrange("p c (h e o) -> p (c h) e o", o=2, e=DK // 2)
                        tv = tmp[0:np_, 0:nr * DK // 2].rearrange("p (b e) -> p b e", e=DK // 2)
                        for o in range(2):
                            cs = [turnc[0:np_, i, :].rearrange("p (e o) -> p e o", o=2)[:, :, o].unsqueeze(1)
                                  .broadcast_to([np_, nr, DK // 2]) for i in range(2)]
                            dve.tensor_tensor(tv, sv[:, :, :, 1 - o], cs[1], ALU.mult)
                            link(dve.tensor_tensor(dv[:, :, :, o], sv[:, :, :, o], cs[0], ALU.mult))
                            link(dve.tensor_tensor(dv[:, :, :, o], dv[:, :, :, o], tv, ALU.add if o else ALU.subtract))
                    dve.sem_inc(s["rotated"], 1)
                dve.wait_ge(s["rows_ready"], 1)
                dve.tensor_copy(bcol[:, :], ps[:, 7, 0:2 * C]).then_inc(s["columns_ready"], 1)
                for j in range(C * 2):
                    m, qk = j // 2, j % 2
                    dve.wait_ge(s["activated"], 2 * j + 2)
                    q = qf[:, qk, m, :]
                    link(dve.tensor_copy(parts[:, qk, 0, m, :], q))
                    link(dve.tensor_tensor(q, q, parts[:, qk, 0, m, :], ALU.subtract))
                    link(dve.tensor_copy(parts[:, qk, 1, m, :], q))
                    dve.tensor_tensor(parts[:, qk, 2, m, :], q, parts[:, qk, 1, m, :], ALU.subtract).then_inc(s["split_ready"], 1)
                for j in range(T // 2):
                    dve.wait_ge(s["v_scored"], j + 1)
                    src = ps[:, 6 + j % 2, :]
                    if variant == 1:
                        dve.tensor_tensor(vn[:, 2 * j:2 * j + 2, :], src.rearrange("p (t n) -> p t n", t=2),
                                          bv[:, :].unsqueeze(1).broadcast_to([P, 2, D]), ALU.add).then_inc(s["v_ready"], 1)
                    else:
                        dve.tensor_tensor(va[:, 2 * j:2 * j + 2, :, 0:DK],
                                          src.rearrange("p (t h d) -> p t h d", t=2, h=H),
                                          bv[:, :].rearrange("p (h d) -> p h d", h=H).unsqueeze(1).broadcast_to([P, 2, H, DK]),
                                          ALU.add).then_inc(s["v_ready"], 1)
        k.end_stage()

        with ExitStack() as ctx:
            def sb(n, shape, dt=F32):
                return ctx.enter_context(nc.sbuf_tensor(k.unique(n), shape, dt))

            ex = sb("a_ex", [P, 4, 2, HALF])
            part = sb("a_part", [P, 2, G * T, 2])
            mx = sb("a_mx", [P, 2, G * T])
            mf = sb("a_mf", [G * T, P])
            mp = sb("a_mp", [G * T, 3, P], BF16)
            ot = sb("a_ot", [P, NG, S])
            on = sb("a_on", [P, NG, S]) if variant == 1 else ot
            rd = sb("a_rd", [P, HALF])
            if variant == 2:
                dist = sb("a_dist", [P, TABLE])
                neg = sb("a_neg", [P, TABLE])
                table = sb("a_table", [P, 2, TABLE])
                al = sb("a_al", [P, 4, H])
            block = ctx.enter_context(nc.Block())
            last_weigh = {}
            for e in plan:
                if e[0] == "weigh":
                    last_weigh[2 * e[2] + e[3]] = e[1] + 1
            maxima_of = [1 + max(e[1] for e in plan if e[0] == "max" and e[2] == g) for g in range(NG)]

            def columns(half, kt):
                q0 = half * HALF if variant else max(half * HALF, kt * P)
                return q0, (half + 1) * HALF - q0

            @block.sync
            def _(sp):
                if variant == 2:
                    sp.dma_start(al[:, 0, :], a["L2_attn_decay_alpha"].partition_broadcast(P)).then_inc(s["loaded"], 16)
                for g in range(NG):
                    sp.wait_ge(s["max_split"], g + 1)
                    sp.dma_start(k.max_parts.rearrange("x (b n) -> b x n", n=P), mp[:, :, :]).then_inc(s["mbounced"], 16)
                    sp.wait_ge(s["mbounced"], 16 * (g + 1))
                    sp.dma_start(qa[KT:KT + 3, G * g:G * g + G, :],
                                 k.max_parts.rearrange("x (h n) -> x h n", h=G)).then_inc(s["max_loaded"], 16)
                    sp.wait_ge(s["max_loaded"], 16 * (g + 1))

            if variant == 2:
                @block.gpsimd
                def _(pool):
                    pool.iota(dist[:, :], pattern=[[1, TABLE]], base=-(S - P), channel_multiplier=-1,
                              allow_small_or_imprecise_dtypes=True).then_inc(s["pool_step"], 1)

            @block.tensor
            def _(pe):
                for e in plan:
                    if e[0] == "max":
                        _, n, g, hh, qt, ch = e
                        h = G * g + hh
                        width = HALF if variant else min(HALF, (qt + 1) * P - ch * HALF)
                        if n >= 2:
                            pe.wait_ge(s["max_taken"], n - 1)
                        if g and hh == 0 and qt == 0 and ch == 0:
                            pe.wait_ge(s["max_split"], g)
                        bank = ps[:, 6 + n % 2, :]
                        last = pe.matmul(bank[:, 0:width], qa[0:KT, h, qt * P:(qt + 1) * P],
                                         ka[0:KT, h, ch * HALF:ch * HALF + width], start=True, stop=True)
                        if not variant and ch == qt // 4:
                            last = pe.matmul(bank[:, width - P:width], k.residue[:, 0, :], k.residue[:, 1, :],
                                             start=False, stop=True, skip_group_check=True)
                        last.then_inc(s["max_scored"], 1)
                    elif e[0] == "turn":
                        g = e[1]
                        pe.wait_ge(s["max_combined"], g + 1)
                        pe.transpose(ps[0:G * T, 6, 0:P], mx[:, g % 2, :], k.ident[:, :]).then_inc(s["max_turned"], 1)
                    elif e[0] == "score":
                        _, n, g, half, kt, pair = e
                        q0, width = columns(half, kt)
                        if n >= 2:
                            pe.wait_ge(s["exponentiated"], n - 1)
                        if half == 0 and kt == 0 and pair == 0:
                            pe.wait_ge(s["max_loaded"], 16 * (g + 1))
                        for j in range(2):
                            h = G * g + 2 * pair + j
                            bank = ps[:, 2 * (n % 2) + j, :]
                            last = pe.matmul(bank[:, 0:width], ka[0:KT + 3, h, kt * P:(kt + 1) * P],
                                             qa[0:KT + 3, h, q0:q0 + width], start=True, stop=True)
                            if not variant and q0 == kt * P:
                                last = pe.matmul(bank[:, 0:P], k.residue[:, 1, :], k.residue[:, 0, :],
                                                 start=False, stop=True, skip_group_check=True)
                        last.then_inc(s["scored"], 1)
                    elif e[0] == "weigh":
                        _, i, g, half, kt = e
                        q0, width = columns(half, kt)
                        pe.wait_ge(s["exponentiated"], 2 * i + 2)
                        f = 2 * g + half
                        if kt == 0 and f >= 2:
                            pe.wait_ge(s["heads_done"], f - 1)
                        final = kt == (T - 1 if variant else 4 * half + 3)
                        for hh in range(G):
                            last = pe.matmul(ps[PAD * hh:PAD * hh + PAD, 4 + half, q0 - half * HALF:q0 - half * HALF + width],
                                             va[:, kt, G * g + hh, :], ex[:, 2 * (i % 2) + hh // 2, hh % 2, 0:width],
                                             start=(kt == 0), stop=final, tile_position=(0, PAD * hh), skip_group_check=True)
                        last.then_inc(s["weighted"], 1)
                    else:
                        f = e[1]
                        pe.wait_ge(s["heads_copied"], f + 1)
                        pe.matmul(ps[:, 4 + f % 2, :], k.sel[:, :], ot[:, f // 2, (f % 2) * HALF:(f % 2 + 1) * HALF],
                                  start=True, stop=True).then_inc(s["denominators_ready"], 1)
                pe.wait_ge(s["heads_done"], 2 * NG)
                for t in range(T):
                    for g in range(NG):
                        o = on[:, g, :]
                        if variant == 0:
                            o = o.rearrange("p (r t) -> p t r", t=T)[:, t, :]
                        else:
                            o = o[:, t * P:(t + 1) * P]
                        last = pe.matmul(ps[:, t // 2, (t % 2) * D:(t % 2 + 1) * D], o, wo[:, g, :],
                                         start=(g == 0), stop=(g == NG - 1))
                    if t % 2:
                        last.then_inc(s["results_ready"], 1)

            @block.scalar
            def _(act):
                if variant == 2:
                    act.wait_ge(s["sums_ready"], 1)
                    act.activation(al[:, 1, :], al[:, 1, :], ACT.Exp).then_inc(s["scalar_step"], 1)
                    act.wait_ge(s["scalar_step"], 1)
                    act.activation(al[:, 1, :], al[:, 1, :], ACT.Ln, bias=1.0).then_inc(s["columns_ready"], 1)
                for e in plan:
                    if e[0] != "score":
                        continue
                    _, n, g, half, kt, pair = e
                    width = columns(half, kt)[1]
                    act.wait_ge(s["biased"] if variant == 2 else s["scored"], n + 1)
                    if n >= 4:
                        act.wait_ge(s["weighted"], (n - 4) // 2 + 1)
                    act.activation(ex[:, 2 * (n // 2 % 2) + pair, :, 0:width], ps[:, 2 * (n % 2):2 * (n % 2) + 2, 0:width],
                                   ACT.Exp, scale=0.25).then_inc(s["exponentiated"], 1)

            @block.vector
            def _(dve):
                link = stepper(dve, s["vector_step"])
                dve.memset(part[:, :, :, :], LOWEST)
                if variant == 2:
                    dve.wait_ge(s["loaded"], 16)
                    dve.scalar_tensor_tensor(out=al[:, 1, :], in0=al[:, 0, :], scalar=-1.0, in1=al[:, 0, :],
                                             op0=ALU.mult, op1=ALU.min).then_inc(s["sums_ready"], 1)
                    link(dve.tensor_scalar(al[:, 2, :], al[:, 0, :], 0.0, None, ALU.max))
                    dve.wait_ge(s["columns_ready"], 1)
                    link(dve.tensor_tensor(al[:, 3, :], al[:, 1, :], al[:, 2, :], ALU.add))
                    link(dve.tensor_scalar(al[:, 3, :], al[:, 3, :], -4.0, None, ALU.mult))
                    dve.wait_ge(s["pool_step"], 1)
                    link(dve.tensor_scalar(neg[:, :], dist[:, :], -1.0, None, ALU.mult))
                    link(dve.tensor_tensor(dist[:, :], dist[:, :], neg[:, :], ALU.max))
                else:
                    link(dve.memset(rd[:, 0:1], 0.0))
                for e in plan:
                    if e[0] == "max":
                        _, n, g, hh, qt, ch = e
                        width = HALF if variant else min(HALF, (qt + 1) * P - ch * HALF)
                        h = G * g + hh
                        if variant == 2 and qt == 0 and ch == 0:
                            link(dve.tensor_scalar(table[:, h % 2, :], dist[:, :], al[:, 3, h:h + 1], None, ALU.mult))
                        dve.wait_ge(s["max_scored"], n + 1)
                        bank = ps[:, 6 + n % 2, 0:width]
                        dst = part[:, g % 2, T * hh + qt, ch:ch + 1]
                        if variant == 2:
                            u = ch * HALF - qt * P + S - P
                            dve.tensor_tensor_reduce(bank, bank, table[:, h % 2, u:u + HALF], 1.0, LOWEST, ALU.add, ALU.max,
                                                     dst).then_inc(s["max_taken"], 1)
                        else:
                            dve.tensor_reduce(dst, bank, AX.X, ALU.max).then_inc(s["max_taken"], 1)
                    elif e[0] == "turn":
                        g = e[1]
                        dve.wait_ge(s["max_taken"], maxima_of[g])
                        dve.tensor_tensor(mx[:, g % 2, :], part[:, g % 2, :, 0], part[:, g % 2, :, 1],
                                          ALU.max).then_inc(s["max_combined"], 1)
                        dve.wait_ge(s["max_turned"], g + 1)
                        if g:
                            dve.wait_ge(s["mbounced"], 16 * g)
                        link(dve.tensor_scalar(mf[:, :], ps[0:G * T, 6, 0:P], -1.0, None, ALU.mult))
                        link(dve.tensor_copy(mp[:, 0, :], mf[:, :]))
                        link(dve.tensor_tensor(mf[:, :], mf[:, :], mp[:, 0, :], ALU.subtract))
                        link(dve.tensor_copy(mp[:, 1, :], mf[:, :]))
                        dve.tensor_tensor(mp[:, 2, :], mf[:, :], mp[:, 1, :], ALU.subtract).then_inc(s["max_split"], 1)
                    elif e[0] == "score" and variant == 2:
                        _, n, g, half, kt, pair = e
                        dve.wait_ge(s["scored"], n + 1)
                        u = half * HALF - kt * P + S - P
                        for j in range(2):
                            h = G * g + 2 * pair + j
                            bank = ps[:, 2 * (n % 2) + j, :]
                            last = dve.scalar_tensor_tensor(out=bank, in0=dist[:, u:u + HALF], scalar=al[:, 3, h:h + 1],
                                                            in1=bank, op0=ALU.mult, op1=ALU.add)
                        last.then_inc(s["biased"], 1)
                    elif e[0] == "finish":
                        f = e[1]
                        o = ot[:, f // 2, (f % 2) * HALF:(f % 2 + 1) * HALF]
                        dve.wait_ge(s["weighted"], last_weigh[f])
                        dve.tensor_copy(o, ps[:, 4 + f % 2, :]).then_inc(s["heads_copied"], 1)
                        dve.wait_ge(s["denominators_ready"], f + 1)
                        link(dve.reciprocal(rd[:, :], ps[:, 4 + f % 2, :]))
                        on_f = on[:, f // 2, (f % 2) * HALF:(f % 2 + 1) * HALF]
                        if variant == 1:
                            on_f = on[:, f // 2, :].rearrange("p (l c) -> p c l", c=H)[:, 8 * (f % 2):8 * (f % 2) + 8, :]
                            o, r = o.rearrange("p (c l) -> p c l", c=8), rd[:, :].rearrange("p (c l) -> p c l", c=8)
                        else:
                            r = rd[:, :]
                        dve.tensor_tensor(on_f, o, r, ALU.mult).then_inc(s["heads_done"], 1)
                for j in range(T // 2):
                    dve.wait_ge(s["results_ready"], j + 1)
                    xv = k.x[:, 2 * j:2 * j + 2, :]
                    link(dve.tensor_tensor(xv, ps[:, j, :].rearrange("p (t n) -> p t n", t=2), xv, ALU.add))
                    dve.tensor_tensor(xv, xv, bo[:, :].unsqueeze(1).broadcast_to([P, 2, D]), ALU.add)
        k.end_stage()


def product_key_ffn(k):
    nc, s, ps, a = k.nc, k.sem, k.ps, k.a
    HK = HP * KP
    with ExitStack() as ctx:
        def sb(name, shape, dt=F32):
            return ctx.enter_context(nc.sbuf_tensor(k.unique(name), shape, dt))

        wi = sb("p_wi", [P, C, D])
        wo = sb("p_wo", [P, C, D])
        keys = sb("p_keys", [P, C, 2, NS])
        u = sb("p_u", [P, G])
        lnw = sb("p_lnw", [P, D])
        lnb = sb("p_lnb", [P, D])
        hT = sb("p_hT", [P, C, S])
        score = sb("p_score", [P, 2, HP * 2, NS])
        rest = sb("p_rest", [P, HP * 2, NS])
        top = sb("p_top", [P, HP, 2, KP])
        topi = sb("p_topi", [P, HP, 2, KP], U32)
        topf = sb("p_topf", [P, HP, 2, KP])
        cand = sb("p_cand", [P, HP, NC_])
        cande = sb("p_cande", [P, HP, NC_])
        crest = sb("p_crest", [P, HP, NC_])
        best = sb("p_best", [P, HP, KP])
        besti = sb("p_besti", [P, HP, KP], U32)
        bestf = sb("p_bestf", [P, HP, KP])
        number = sb("p_number", [P, NC_])
        hot = sb("p_hot", [P, HP // 2, KP, NC_])
        expf = sb("p_expf", [P, HP, KP])
        expert = sb("p_expert", [P, 2, HK], U32)
        wt = sb("p_wt", [P, 2, HP, KP])
        z = sb("p_z", [P, 2, 4, HP])
        got = [sb("p_got0", [P, HK, HD]), sb("p_got1", [P, HK, HD])]
        merged = sb("p_merged", [P, D])
        mT = sb("p_mT", [P, C, P])
        proj = sb("p_proj", [P, T, D])
        stats = sb("p_stats", [P, T, 6])
        mv = sb("p_mv", [P, T, 2])
        var = sb("p_var", [P, 3, T])
        block = ctx.enter_context(nc.Block())
        arrived = [s["gathered_even"], s["gathered_odd"]]

        @block.sync
        def _(sp):
            ld = s["loaded"]
            sp.dma_start(wi[:, :, :], a["L3_ffn_W_inT"].rearrange("(c p) n -> p c n", p=P)).then_inc(ld, 16)
            sp.dma_start(wo[:, :, :], a["L3_ffn_W_outT"].rearrange("(c p) n -> p c n", p=P)).then_inc(ld, 16)
            sp.dma_start(keys[:, :, 0, :], a["L3_ffn_keys_aT"].rearrange("(c p) n -> p c n", p=P)).then_inc(ld, 16)
            sp.dma_start(keys[:, :, 1, :], a["L3_ffn_keys_bT"].rearrange("(c p) n -> p c n", p=P)).then_inc(ld, 16)
            sp.dma_start(lnw[:, :], a["L3_ffn_ln_w"].partition_broadcast(P)).then_inc(ld, 16)
            sp.dma_start(lnb[:, :], a["L3_ffn_ln_b"].partition_broadcast(P)).then_inc(ld, 16)
            sp.wait_ge(s["cleared"], 1)
            for hh in range(G):
                sp.dma_start(u[HD * hh:HD * hh + HD, hh:hh + 1], a["L3_ffn_u_shared"].rearrange("(p o) -> p o", o=1)).then_inc(ld, 16)

        NL = 6 + G

        @block.gpsimd
        def _(pool):
            pool.memset(u[:, :], 0.0).then_inc(s["cleared"], 1)
            pool.iota(number[:, :], pattern=[[1, NC_]], base=0, channel_multiplier=0,
                      allow_small_or_imprecise_dtypes=True).then_inc(s["pool_step"], 1)
            for t in range(T):
                pool.wait_ge(s["indices_ready"], t + 1)
                if t >= 2:
                    pool.wait_ge(s["gathers_used"], t - 1)
                for j in range(HK):
                    pool.indirect_dma_start(got[t % 2][:, j, :], None, a["L3_ffn_expert_v"],
                                            bass.IndirectOffsetOnAxis(expert[:, t % 2, j:j + 1], 0)).then_inc(arrived[t % 2], 16)
            for n in range(2):
                pool.wait_ge(arrived[n], 16 * HK * T // 2)

        @block.tensor
        def _(pe):
            pe.wait_ge(s["loaded"], 16 * NL)
            for m in range(C):
                for half in range(2):
                    for c in range(C):
                        last = pe.matmul(ps[:, 2 * m + half, :], wi[:, c, m * P:(m + 1) * P],
                                         k.yT[:, c, half * HALF:(half + 1) * HALF], start=(c == 0), stop=(c == C - 1))
                    last.then_inc(s["multiplied"], 1)
            pe.wait_ge(s["activated"], 4)

            def project(t):
                pe.wait_ge(s["merged_ready"], t + 1)
                for c in range(C):
                    last = pe.transpose(ps[:, 5, c * P:(c + 1) * P], merged[:, c * P:(c + 1) * P], k.ident[:, :])
                last.then_inc(s["transposed"], 1)
                pe.wait_ge(s["columns_ready"], t + 1)
                if t:
                    pe.wait_ge(s["results_ready"], t)
                for c in range(C):
                    last = pe.matmul(ps[:, 6, 0:D], mT[:, c, :], wo[:, c, :], start=(c == 0), stop=(c == C - 1))
                last.then_inc(s["weighted"], 1)

            for t in range(T):
                if t:
                    pe.wait_ge(s["probs_ready"], t)
                for h in range(HP):
                    c, hh = h // G, h % G
                    last = pe.matmul(ps[:, hh, c * 2 * NS:(c + 1) * 2 * NS],
                                     hT[HD * hh:HD * hh + HD, c, t * P:(t + 1) * P],
                                     keys[HD * hh:HD * hh + HD, c, :, :].rearrange("p a b -> p (a b)"), start=True, stop=True)
                for c in range(C):
                    last = pe.matmul(ps[:, 4, c * G:(c + 1) * G], hT[:, c, t * P:(t + 1) * P], u[:, :], start=True, stop=True)
                last.then_inc(s["scored"], 1)
                if t:
                    project(t - 1)
            project(T - 1)

        @block.scalar
        def _(act):
            for m in range(C):
                for half in range(2):
                    act.wait_ge(s["multiplied"], 2 * m + half + 1)
                    act.activation(hT[:, m, half * HALF:(half + 1) * HALF], ps[:, 2 * m + half, :], ACT.Copy).then_inc(s["activated"], 1)

            def out_copies(t):
                act.wait_ge(s["transposed"], t + 1)
                act.activation(mT[:, :, :].rearrange("p c n -> p (c n)"), ps[:, 5, 0:D], ACT.Copy).then_inc(s["columns_ready"], 1)
                act.wait_ge(s["weighted"], t + 1)
                act.activation(proj[:, t, :], ps[:, 6, 0:D], ACT.Copy).then_inc(s["results_ready"], 1)

            for t in range(T):
                act.wait_ge(s["scored"], t + 1)
                if t >= 2:
                    act.wait_ge(s["indices_ready"], t - 1)
                    act.wait_ge(s["gathers_used"], t - 1)
                act.activation(z[:, t % 2, 0, :], ps[:, 4, 0:HP], ACT.Exp, scale=-1.0)
                act.activation(score[:, t % 2, :, :].rearrange("p (c g a) n -> p g c (a n)", c=C, g=G),
                               ps[:, 0:G, :].rearrange("p g (c n) -> p g c n", c=C), ACT.Copy).then_inc(s["probs_ready"], 1)
                act.wait_ge(s["max_taken"], t + 1)
                act.activation(wt[:, t % 2, :, :], wt[:, t % 2, :, :], ACT.Exp).then_inc(s["exponentiated"], 1)
                if t:
                    out_copies(t - 1)
            out_copies(T - 1)
            act.wait_ge(s["variance_ready"], 1)
            act.activation(var[:, 1, :], var[:, 0, :], ACT.Sqrt).then_inc(s["std_ready"], 1)

        @block.vector
        def _(dve):
            link = stepper(dve, s["vector_step"])

            def top16(values, indices, score_of, rest_of, n):
                for i in range(n):
                    last = dve.max(values(i)[:, 0:8], score_of(i))
                link(last)
                for i in range(n):
                    last = dve.match_replace(rest_of(i), values(i)[:, 0:8], score_of(i), LOWEST)
                link(last)
                for i in range(n):
                    dve.max_index(indices(i)[:, 0:8], values(i)[:, 0:8], score_of(i))
                    last = dve.max(values(i)[:, 8:16], rest_of(i))
                link(last)
                for i in range(n):
                    last = dve.max_index(indices(i)[:, 8:16], values(i)[:, 8:16], rest_of(i))
                link(last)

            def choose(t):
                dve.wait_ge(s["probs_ready"], t + 1)
                top16(lambda i: top[:, i // 2, i % 2, :], lambda i: topi[:, i // 2, i % 2, :],
                      lambda i: score[:, t % 2, i, :], lambda i: rest[:, i, :], 2 * HP)
                link(dve.tensor_copy(topf[:, :, :, :], topi[:, :, :, :]))
                link(dve.tensor_scalar(topf[:, :, 0, :], topf[:, :, 0, :], float(NS), None, ALU.mult))
                i = 0
                while i < KP:
                    m = sum(1 for r in ROWS[i:] if r == ROWS[i])
                    for of, to in ((top, cand), (topf, cande)):
                        last = dve.tensor_tensor(to[:, :, STARTS[i]:STARTS[i] + m * ROWS[i]].rearrange("p h (m n) -> p h m n", m=m),
                                                 of[:, :, 0, i:i + m].unsqueeze(3).broadcast_to([P, HP, m, ROWS[i]]),
                                                 of[:, :, 1, 0:ROWS[i]].unsqueeze(2).broadcast_to([P, HP, m, ROWS[i]]), ALU.add)
                    i += m
                link(last)
                top16(lambda i: best[:, i, :], lambda i: besti[:, i, :], lambda i: cand[:, i, :], lambda i: crest[:, i, :], HP)
                dve.tensor_tensor(wt[:, t % 2, :, :], best[:, :, :], best[:, :, 0:1].broadcast_to([P, HP, KP]),
                                  ALU.subtract).then_inc(s["max_taken"], 1)
                link(dve.tensor_copy(bestf[:, :, :], besti[:, :, :]))
                if t == 0:
                    dve.wait_ge(s["pool_step"], 1)
                Q = HP // 2
                for q in range(2):
                    hs = slice(Q * q, Q * q + Q)
                    link(dve.tensor_tensor(hot[:, :, :, :].rearrange("p h k n -> p (h k) n"),
                                           number[:, :].unsqueeze(1).broadcast_to([P, Q * KP, NC_]),
                                           bestf[:, hs, :].rearrange("p h k -> p (h k)").unsqueeze(2).broadcast_to([P, Q * KP, NC_]),
                                           ALU.is_equal))
                    link(dve.tensor_tensor(hot[:, :, :, :], hot[:, :, :, :],
                                           cande[:, hs, :].unsqueeze(2).broadcast_to([P, Q, KP, NC_]), ALU.mult))
                    link(dve.tensor_reduce(expf[:, hs, :], hot[:, :, :, :], AX.X, ALU.add))
                if t >= 2:
                    dve.wait_ge(arrived[t % 2], 16 * HK * (t // 2))
                dve.tensor_copy(expert[:, t % 2, :], expf[:, :, :].rearrange("p h k -> p (h k)")).then_inc(s["indices_ready"], 1)
                dve.wait_ge(s["exponentiated"], t + 1)
                zt = z[:, t % 2, :, :]
                dve.tensor_scalar(zt[:, 1, :], zt[:, 0, :], 1.0, None, ALU.add)
                link(dve.tensor_reduce(zt[:, 2, :], wt[:, t % 2, :, :], AX.X, ALU.add))
                link(dve.tensor_tensor(zt[:, 2, :], zt[:, 2, :], zt[:, 1, :], ALU.mult))
                link(dve.reciprocal(zt[:, 3, :], zt[:, 2, :]))
                link(dve.tensor_tensor(wt[:, t % 2, :, :], wt[:, t % 2, :, :],
                                       zt[:, 3, :].unsqueeze(2).broadcast_to([P, HP, KP]), ALU.mult))

            def weigh(t):
                dve.wait_ge(arrived[t % 2], 16 * HK * (t // 2 + 1))
                gt = got[t % 2]
                link(dve.tensor_tensor(gt[:, :, :], gt[:, :, :], wt[:, t % 2, :, :].rearrange("p h k -> p (h k)").unsqueeze(2)
                                       .broadcast_to([P, HK, HD]), ALU.mult))
                if t:
                    dve.wait_ge(s["transposed"], t)
                link(dve.tensor_reduce(merged[:, :].rearrange("p (h d) -> p h d", h=HP),
                                       gt[:, :, :].rearrange("p (h k) d -> p h d k", h=HP), AX.X, ALU.add))
                dve.sem_inc(s["merged_ready"], 1)
                dve.sem_inc(s["gathers_used"], 1)

            for t in range(T):
                choose(t)
                if t:
                    weigh(t - 1)
            weigh(T - 1)
            dve.wait_ge(s["results_ready"], T)
            for t in range(T):
                last = dve.bn_stats(stats[:, t, :], proj[:, t, :])
            link(last)
            for t in range(T):
                last = dve.bn_aggr(mv[:, t, :], stats[:, t, :])
            link(last)
            dve.tensor_scalar(var[:, 0, :], mv[:, :, 1], EPS, None, ALU.add).then_inc(s["variance_ready"], 1)
            dve.wait_ge(s["std_ready"], 1)
            link(dve.reciprocal(var[:, 2, :], var[:, 1, :]))
            for t in range(T):
                last = dve.tensor_scalar(proj[:, t, :], proj[:, t, :], mv[:, t, 0:1], var[:, 2, t:t + 1], ALU.subtract, ALU.mult)
            link(last)
            link(dve.tensor_tensor(proj[:, :, :], proj[:, :, :], lnw[:, :].unsqueeze(1).broadcast_to([P, T, D]), ALU.mult))
            link(dve.tensor_tensor(proj[:, :, :], proj[:, :, :], lnb[:, :].unsqueeze(1).broadcast_to([P, T, D]), ALU.add))
            xv = k.x[:, :, :].rearrange("p t n -> p (t n)")
            dve.scalar_tensor_tensor(out=xv, in0=proj[:, :, :].rearrange("p t n -> p (t n)"), scalar=0.5, in1=xv,
                                     op0=ALU.mult, op1=ALU.add)
    k.end_stage(gathers=True)


def layout(inputs):
    import numpy as np
    r = {n: np.ascontiguousarray(v) for n, v in inputs.items()}

    def turn(n):
        r[n + "T"] = np.ascontiguousarray(r.pop(n).T)
    for n in ("L0_attn_Wq", "L0_attn_Wk", "L0_attn_Wv", "L0_attn_Wo", "L1_attn_wq", "L1_attn_wk", "L1_attn_wv",
              "L1_attn_wo", "L2_attn_qkv_w", "L2_attn_out_w", "L2_ffn_W", "L2_ffn_Wp", "L3_attn_input_weights",
              "L3_attn_output_weight", "L3_ffn_W_in", "L3_ffn_W_out"):
        turn(n)
    r["L2_ffn_WdT"] = np.ascontiguousarray(np.concatenate([r.pop(f"L2_ffn_Wd{i}") for i in range(len(RANKS))], axis=0).T)
    r["L2_ffn_WuT"] = np.ascontiguousarray(np.concatenate([r.pop(f"L2_ffn_Wu{i}") for i in range(len(RANKS))], axis=1).T)
    for n in ("L3_ffn_keys_a", "L3_ffn_keys_b"):
        r[n + "T"] = np.ascontiguousarray(r.pop(n).transpose(0, 2, 1).reshape(D, NS))
    return r


def program(nc, x, out, a):
    with ExitStack() as ctx:
        ctx.enter_context(nc.allow_non_contiguous_dma(reason="biases and router weights as columns"))
        k = Core(nc, ctx, a)
        constants(k)
        with nc.Fori(0, B) as b:
            load_batch(k, x, b)
            for stage in (coupling_ffn, lambda k: attention(k, 0), coupling_ffn,
                          expert_ffn, lambda k: attention(k, 1), expert_ffn,
                          lora_ffn, lambda k: attention(k, 2), lora_ffn,
                          product_key_ffn, gaussian_attention, product_key_ffn):
                layer_norm(k)
                stage(k)
            store_batch(k, out, b)


def kernel(**inputs):
    import concourse.bacc as _bacc
    from concourse import mybir as _mybir
    from concourse.bass_utils import run_bass_kernel_spmd as _run

    nc = _bacc.Bacc("TRN2", target_bir_lowering=False, num_devices=1)
    arrays = layout(inputs)
    aps = {n: nc.dram_tensor("in_" + n, v.shape, _mybir.dt.from_np(v.dtype), kind="ExternalInput").ap()
           for n, v in arrays.items()}
    out = nc.dram_tensor("out_0", (B, S, D), F32, kind="ExternalOutput").ap()
    program(nc, aps["L0_attn_x"], out, aps)
    r = _run(nc, [{"in_" + n: v for n, v in arrays.items()}], core_ids=[0])
    return r.results[0]["out_0"]
```

```python
import concourse.bass as bass
from concourse import mybir
from contextlib import ExitStack

F32 = mybir.dt.float32
BF16 = mybir.dt.bfloat16
U32 = mybir.dt.uint32
I32 = mybir.dt.int32
ALU = mybir.AluOpType
ACT = mybir.ActivationFunctionType
AX = mybir.AxisListType

P = 128
B, S, D = 4, 1024, 256
T = S // P
C = D // P
H = 16
DK = D // H
G = 4
NG = H // G
PAD = 32
HALF = S // 2
LOWEST = -3.0e38
MASKED = -1.0e30
EPS = 1e-5
E1 = 8
F1 = 128
PR = 64
RANKS = (1, 2, 4, 8)
RT = sum(RANKS)
HP, KP, NS = 8, 16, 128
HD = D // HP
ROWS = [KP // (i + 1) for i in range(KP)]
NC_ = sum(ROWS)
STARTS = [sum(ROWS[:i]) for i in range(KP)]
UNIT = 64
assert NC_ <= UNIT
ROUND = 1.5 * 2 ** 23 * UNIT
TERMS = ((0, 0), (0, 1), (1, 0), (1, 1), (0, 2), (2, 0))
TABLE = 2 * S - P
KT = len(TERMS) * DK
STD = (1.0, 2.0, 4.0, 8.0)

SEMS = ("stored", "bounced", "mbounced", "vector_step", "pool_step", "scalar_step", "variance_ready",
        "std_ready", "normalized", "transposed", "multiplied", "activated", "state_updated", "sums_ready",
        "columns_ready", "split_ready", "v_ready", "max_scored", "max_taken", "max_turned", "max_split",
        "scored", "biased", "exponentiated", "weighted", "heads_copied", "denominators_ready", "heads_done",
        "routed", "cleared", "merged_ready",
        "results_ready", "halfway", "rows_ready", "probs_ready", "bounced0", "bounced1", "v_bounced", "v_loaded",
        "heads_loaded", "max_combined", "max_loaded", "rotated",
        "table_ready", "v_scored", "weights_ready")


FLIGHT = ("indices_ready", "gathered0", "gathered1", "gathered2", "rows_weighed", "rows_used", "stage_done", "stage_open",
          "loaded")
SLOTS = 3
HT = HP * KP // 2
PACE = 67.0


PLAN_US = (245.0, 325.0, 445.0)


class Core:

    def __init__(self, nc, ctx, a):
        self.nc, self.a, self.stage = nc, a, 0
        self.sem = {n: ctx.enter_context(nc.semaphore(n)) for n in SEMS + FLIGHT}
        nums = [self.sem[n].num for n in SEMS]
        self.span = range(min(nums), max(nums) + 1)
        assert len(self.span) == len(nums)
        self.flight = range(self.sem[FLIGHT[0]].num, self.sem[FLIGHT[-1]].num + 1)
        assert len(self.flight) == len(FLIGHT)

        def sb(name, shape, dt=F32):
            return ctx.enter_context(nc.sbuf_tensor(name, shape, dt))

        self.ps = ctx.enter_context(nc.psum_tensor("ps", [P, 8, 512], F32))
        self.ident = sb("ident", [P, P])
        self.ones = sb("ones", [P, P])
        self.sel = sb("sel", [P, P])
        self.residue = sb("residue", [16, 2, P], BF16)
        self.number = sb("number", [P, KP])
        self.starts = sb("starts", [P, KP])
        self.qk_parts = nc.dram_tensor("qk_parts", (2, 3, D, S), BF16).ap()
        self.max_parts = nc.dram_tensor("max_parts", (3, G * S), BF16).ap()
        self.v_rows = nc.dram_tensor("v_rows", (S, D), F32).ap()
        self.ones_rows = nc.dram_tensor("ones_rows", (4, H * S), BF16).ap()
        self.dist_rows = nc.dram_tensor("dist_rows", (P, TABLE), F32).ap()
        self.x = sb("x", [P, T, D])
        self.xp = sb("xp", [P, T, D])
        self.yT = sb("yT", [P, C, S])
        self.got = [sb(f"got{i}", [P, HT, HD]) for i in range(SLOTS)]
        self.expert = sb("expert", [P, T, HP * KP], U32)
        self.wt = sb("wt", [P, T, HP, KP])
        self.merged = sb("merged", [P, T, D])

    def open(self, block):
        self.block, self.stages_done = block, 0
        self.loads = 0
        self.chosen = self.sent = self.weighed = 0
        self.clock = self.started = 0.0

    def unique(self, name):
        return f"{name}_{self.stage}"

    def end_stage(self):
        self.stage += 1
        self.stages_done += 1
        n, s, block = self.stages_done, self.sem, self.block

        @block.sync
        def _(sp):
            sp.drain().then_inc(s["stage_done"], 1)
            sp.wait_ge(s["stage_done"], 4 * n)
            sp.sem_clear(self.span)
            sp.sem_inc(s["stage_open"], 1)

        @block.scalar
        def _(act):
            act.drain().then_inc(s["stage_done"], 1)
            act.wait_ge(s["stage_open"], n)

        @block.vector
        def _(dve):
            dve.drain().then_inc(s["stage_done"], 1)
            dve.wait_ge(s["stage_open"], n)

        @block.tensor
        def _(pe):
            pe.drain().then_inc(s["stage_done"], 1)
            pe.wait_ge(s["stage_open"], n)

    def end_block(self):
        first = self.sem["gathered0"].num
        self.nc.all_engine_barrier(sem_only=True)
        self.nc.gpsimd.dma_reset(range(first, first + SLOTS))
        self.nc.gpsimd.sem_clear(self.flight)
        self.nc.gpsimd.sem_clear(self.span)
        self.nc.all_engine_barrier(sem_only=True)

    def loading(self, n):
        return self.loads + 16 * n

    def weigh(self, dve):
        n, s = self.weighed, self.sem
        self.weighed += 1
        self.clock += 4.4
        t, half = n // 2 % T, n % 2
        rows = self.got[n % SLOTS][:, :, :]
        hs = slice(HP // 2 * half, HP // 2 * (half + 1))
        dve.wait_ge(s[f"gathered{n % SLOTS}"], 16 * HT * (n // SLOTS + 1))
        if n:
            dve.wait_ge(s["rows_used"], n)
        dve.tensor_tensor(rows, rows, self.wt[:, t, hs, :].rearrange("p h k -> p (h k)").unsqueeze(2)
                          .broadcast_to([P, HT, HD]), ALU.mult).then_inc(s["rows_weighed"], 1)
        dve.wait_ge(s["rows_weighed"], self.weighed)
        dve.tensor_reduce(self.merged[:, t, D // 2 * half:D // 2 * (half + 1)].rearrange("p (h d) -> p h d", d=HD),
                          rows.rearrange("p (h k) d -> p h d k", k=KP), AX.X, ALU.add).then_inc(s["rows_used"], 1)

    def pass_time(self, dve, us):
        self.clock += us
        while self.weighed < self.sent and self.clock >= self.started + PACE * (self.weighed % (2 * T) + 1):
            self.weigh(dve)


def stepper(eng, sem):
    count = [0]

    def link(ins):
        count[0] += 1
        ins.then_inc(sem, 1)
        eng.wait_ge(sem, count[0])
    return link


def constants(k):
    nc, s = k.nc, k.sem
    with ExitStack() as ctx:
        ones_b = ctx.enter_context(nc.sbuf_tensor("ones_b", [P, 4 * H * S // P], BF16))
        dist = ctx.enter_context(nc.sbuf_tensor("dist_b", [P, TABLE], F32))
        block = ctx.enter_context(nc.Block())

        @block.gpsimd
        def _(pool):
            link = stepper(pool, s["pool_step"])
            pool.memset(ones_b[:, :], 1.0).then_inc(s["cleared"], 1)
            pool.iota(dist[:, :], pattern=[[1, TABLE]], base=-(S - P), channel_multiplier=-1,
                      allow_small_or_imprecise_dtypes=True).then_inc(s["cleared"], 1)
            pool.iota(k.number[:, :], pattern=[[1, KP]], base=0, channel_multiplier=0,
                      allow_small_or_imprecise_dtypes=True)
            for i in range(KP):
                pool.memset(k.starts[:, i:i + 1], float(STARTS[i]))
            pool.memset(k.ones[:, :], 1.0)
            pool.memset(k.sel[:, :], 0.0)
            pool.memset(k.residue[:, 0, :], 0.0)
            pool.memset(k.residue[:, 1, :], 1.0)
            link(pool.memset(k.ident[:, :], 0.0))
            pool.affine_select(out=k.ident[:, :], in_=k.ident[:, :], compare_op=ALU.not_equal, fill=1.0,
                               base=0, pattern=[[-1, P]], channel_multiplier=1)
            pool.affine_select(out=k.sel[:, :], in_=k.sel[:, :], compare_op=ALU.not_equal, fill=1.0,
                               base=-DK, pattern=[[-PAD, G], [0, PAD]], channel_multiplier=1)
            pool.affine_select(out=k.residue[:, 0, :], in_=k.residue[:, 0, :], compare_op=ALU.is_ge, fill=MASKED,
                               base=0, pattern=[[1, P]], channel_multiplier=-T)
            link(pool.affine_select(out=k.residue[:, 1, :], in_=k.residue[:, 1, :], compare_op=ALU.is_ge, fill=0.0,
                                    base=0, pattern=[[1, P]], channel_multiplier=-T))
            link(pool.affine_select(out=k.residue[:, 1, :], in_=k.residue[:, 1, :], compare_op=ALU.is_ge, fill=0.0,
                                    base=T - 1, pattern=[[-1, P]], channel_multiplier=T))

        @block.sync
        def _(sp):
            sp.wait_ge(s["cleared"], 2)
            sp.dma_start(k.ones_rows.rearrange("a (b n) -> (a b) n", b=P // 4), ones_b[:, :]).then_inc(s["stored"], 16)
            sp.dma_start(k.dist_rows, dist[:, :]).then_inc(s["stored"], 16)
            sp.wait_ge(s["stored"], 32)
    k.end_block()


def load_batch(k, x, b):
    s, block = k.sem, k.block

    @block.sync
    def _(sp):
        src = x[b] if isinstance(b, int) else x[bass.ds(b, 1)].rearrange("o s n -> (o s) n")
        sp.dma_start(k.x[:, :, :], src.rearrange("(t p) n -> p t n", p=P)).then_inc(s["loaded"], 16)
        sp.wait_ge(s["loaded"], k.loading(1))
    k.loads = k.loading(1)
    k.end_stage()


def store_batch(k, out, b):
    s, block = k.sem, k.block

    @block.sync
    def _(sp):
        dst = out[b] if isinstance(b, int) else out[bass.ds(b, 1)].rearrange("o s n -> (o s) n")
        sp.dma_start(dst.rearrange("(t p) n -> p t n", p=P), k.xp[:, :, :]).then_inc(s["stored"], 16)
        sp.wait_ge(s["stored"], 16)
    k.end_stage()


def hand_over(k):
    block = k.block

    @block.vector
    def _(dve):
        dve.tensor_copy(k.xp[:, :, :], k.x[:, :, :])
    k.end_stage()


def layer_norm(k, x, y=None):
    nc, s, ps = k.nc, k.sem, k.ps
    with ExitStack() as ctx:
        if y is None:
            y = ctx.enter_context(nc.sbuf_tensor(k.unique("ln_y"), [P, T, D], F32))
        stats = ctx.enter_context(nc.sbuf_tensor(k.unique("ln_stats"), [P, T, 6], F32))
        mv = ctx.enter_context(nc.sbuf_tensor(k.unique("ln_mv"), [P, T, 2], F32))
        var = ctx.enter_context(nc.sbuf_tensor(k.unique("ln_var"), [P, T], F32))
        std = ctx.enter_context(nc.sbuf_tensor(k.unique("ln_std"), [P, T], F32))
        rstd = ctx.enter_context(nc.sbuf_tensor(k.unique("ln_rstd"), [P, T], F32))
        block = k.block

        @block.vector
        def _(dve):
            link = stepper(dve, s["vector_step"])
            for t in range(T):
                last = dve.bn_stats(stats[:, t, :], x[:, t, :])
            link(last)
            for t in range(T):
                last = dve.bn_aggr(mv[:, t, :], stats[:, t, :])
            link(last)
            dve.tensor_scalar(var[:, :], mv[:, :, 1], EPS, None, ALU.add).then_inc(s["variance_ready"], 1)
            dve.wait_ge(s["std_ready"], 1)
            link(dve.reciprocal(rstd[:, :], std[:, :]))
            for t in range(T):
                dve.tensor_scalar(y[:, t, :], x[:, t, :], mv[:, t, 0:1], rstd[:, t:t + 1],
                                  ALU.subtract, ALU.mult).then_inc(s["normalized"], 1)

        @block.tensor
        def _(pe):
            for t in range(T):
                pe.wait_ge(s["normalized"], t + 1)
                for c in range(C):
                    last = pe.transpose(ps[:, 2 * c + t // 4, (t % 4) * P:(t % 4 + 1) * P],
                                        y[:, t, c * P:(c + 1) * P], k.ident[:, :])
                last.then_inc(s["transposed"], 1)

        @block.scalar
        def _(act):
            act.wait_ge(s["variance_ready"], 1)
            act.activation(std[:, :], var[:, :], ACT.Sqrt).then_inc(s["std_ready"], 1)
            for half in range(2):
                act.wait_ge(s["transposed"], 4 * (half + 1))
                for c in range(C):
                    act.activation(k.yT[:, c, half * HALF:(half + 1) * HALF], ps[:, 2 * c + half, :], ACT.Copy)
    k.end_stage()


def coupling_ffn(k):
    nc, s, ps, a = k.nc, k.sem, k.ps, k.a
    with ExitStack() as ctx:
        def sb(name, shape, dt=F32):
            return ctx.enter_context(nc.sbuf_tensor(k.unique(name), shape, dt))

        w1 = sb("cn_w1", [P, C, D])
        w2 = sb("cn_w2", [P, C, 128])
        w3 = sb("cn_w3", [P, 64])
        w4 = sb("cn_w4", [64, 1])
        w4r = sb("cn_w4r", [64, P])
        v1 = sb("gc_w1", [P, C, 128])
        v2 = sb("gc_w2", [P, 64])
        v3 = sb("gc_w3", [64, 1])
        v3r = sb("gc_w3r", [64, P])
        b1 = sb("cn_b1", [P, C])
        cols = sb("cn_cols", [P, 8])
        hb = sb("cn_hb", [P, 2])
        sign = sb("cn_sign", [P, 1])
        base = sb("cn_base", [P, 2])
        g = sb("cn_g", [P, 8])
        oT = [k.yT, sb("cn_oT0", [P, C, S]), sb("cn_oT1", [P, C, S])]
        h1 = sb("cn_h1", [P, C, S])
        h2 = sb("cn_h2", [P, S])
        h3 = sb("cn_h3", [64, S])
        th = sb("cn_th", [P, S])
        cs = sb("cn_cs", [P, S])
        tw = sb("cn_tw", [P, C, S])
        block = k.block
        state = [oT[0], oT[1], oT[2], oT[1]]
        @block.sync
        def _(sp):
            ld = s["loaded"]
            sp.dma_start(w1[:, :, :], a["L0_ffn_cn_w1"].rearrange("(c p) n -> p c n", p=P)).then_inc(ld, 16)
            sp.dma_start(w2[:, :, :], a["L0_ffn_cn_w2"].rearrange("(c p) n -> p c n", p=P)).then_inc(ld, 16)
            sp.dma_start(w3[:, :], a["L0_ffn_cn_w3"]).then_inc(ld, 16)
            sp.dma_start(w4[:, :], a["L0_ffn_cn_w4"]).then_inc(ld, 16)
            sp.dma_start(v1[:, :, :], a["L0_ffn_gc_w1"].rearrange("(c p) n -> p c n", p=P)).then_inc(ld, 16)
            sp.dma_start(v2[:, :], a["L0_ffn_gc_w2"]).then_inc(ld, 16)
            sp.dma_start(v3[:, :], a["L0_ffn_gc_w3"]).then_inc(ld, 16)
            sp.dma_start(b1[:, :], a["L0_ffn_cn_b1"].rearrange("(c p) -> p c", p=P)).then_inc(ld, 16)
            sp.dma_start(cols[:, 0:1], a["L0_ffn_cn_b2"].rearrange("(p o) -> p o", o=1)).then_inc(ld, 16)
            sp.dma_start(cols[0:64, 1:2], a["L0_ffn_cn_b3"].rearrange("(p o) -> p o", o=1)).then_inc(ld, 16)
            sp.dma_start(cols[:, 2:3], a["L0_ffn_cn_b4"].partition_broadcast(P)).then_inc(ld, 16)
            sp.dma_start(cols[:, 3:4], a["L0_ffn_gc_b1"].rearrange("(p o) -> p o", o=1)).then_inc(ld, 16)
            sp.dma_start(cols[0:64, 4:5], a["L0_ffn_gc_b2"].rearrange("(p o) -> p o", o=1)).then_inc(ld, 16)
            sp.dma_start(cols[:, 5:6], a["L0_ffn_gc_b3"].partition_broadcast(P)).then_inc(ld, 16)
            sp.dma_start(cols[:, 6:7], a["L0_ffn_adaptive_range"].partition_broadcast(P)).then_inc(ld, 16)

        NL = 15
        layer_norm(k, k.x)

        @block.vector
        def _(dve):
            link = stepper(dve, s["vector_step"])
            dve.memset(sign[0:64, :], 1.0)
            dve.memset(sign[64:128, :], -1.0)
            dve.tensor_reduce(g[:, 0:2], k.yT[:, :, :], AX.X, ALU.add)
            dve.wait_ge(s["loaded"], k.loading(NL))
            dve.tensor_copy(w4r[:, :], w4[:, :].broadcast_to([64, P]))
            dve.tensor_copy(v3r[:, :], v3[:, :].broadcast_to([64, P]))
            dve.tensor_scalar(hb[:, 0:1], cols[:, 2:3], 0.5, None, ALU.mult)
            link(dve.tensor_scalar(hb[:, 1:2], cols[:, 5:6], 0.5, None, ALU.mult))
            dve.tensor_scalar(g[:, 2:4], g[:, 0:2], 1.0 / S, None, ALU.mult).then_inc(s["sums_ready"], 1)
            dve.wait_ge(s["columns_ready"], 1)
            link(dve.tensor_tensor(g[:, 7:8], g[:, 6:7], cols[:, 6:7], ALU.mult))
            link(dve.tensor_scalar(g[:, 7:8], g[:, 7:8], 0.7, 0.1, ALU.mult, ALU.add))
            dve.tensor_tensor(base[:, 0:1], g[:, 7:8], sign[:, :], ALU.mult)
            link(dve.scalar_tensor_tensor(out=base[:, 1:2], in0=cols[:, 6:7], scalar=0.3, in1=sign[:, :],
                                          op0=ALU.mult, op1=ALU.mult))
            for n in range(3):
                o, new = state[n], state[n + 1]
                for half in range(2):
                    q = slice(half * HALF, (half + 1) * HALF)
                    dve.wait_ge(s["activated"], 10 * n + 9 + half)
                    link(dve.tensor_scalar(cs[:, q], th[:, q], base[:, 1:2], base[:, 0:1], ALU.mult, ALU.add))
                    dve.tensor_tensor(tw[:, 0, q], cs[:, q], o[:, 1, q], ALU.mult)
                    link(dve.tensor_tensor(tw[:, 1, q], cs[:, q], o[:, 0, q], ALU.mult))
                    dve.tensor_tensor(new[:, 0, q], o[:, 0, q], tw[:, 0, q], ALU.add)
                    link(dve.tensor_tensor(new[:, 1, q], o[:, 1, q], tw[:, 1, q], ALU.subtract))
                    dve.sem_inc(s["state_updated"], 1)
            for j in range(4):
                dve.wait_ge(s["transposed"], j + 1)
                xv = k.x[:, 2 * j:2 * j + 2, :].rearrange("p t n -> p (t n)")
                dve.scalar_tensor_tensor(out=xv, in0=ps[:, j, :], scalar=0.5, in1=xv, op0=ALU.mult, op1=ALU.add)

        @block.tensor
        def _(pe):
            pe.wait_ge(s["sums_ready"], 1)
            for c in range(C):
                last = pe.matmul(ps[:, 7, 0:1], v1[:, c, :], g[:, 2 + c:3 + c], start=(c == 0), stop=(c == C - 1))
            last.then_inc(s["halfway"], 1)
            pe.wait_ge(s["rows_ready"], 1)
            pe.matmul(ps[0:64, 7, 1:2], v2[:, :], g[:, 4:5], start=True, stop=True).then_inc(s["halfway"], 1)
            pe.wait_ge(s["rows_ready"], 2)
            pe.matmul(ps[:, 7, 2:3], v3r[:, :], g[0:64, 5:6], start=True, stop=True).then_inc(s["halfway"], 1)
            pe.wait_ge(s["columns_ready"], 1)
            for n in range(3):
                o = state[n]
                for half in range(2):
                    if n:
                        pe.wait_ge(s["state_updated"], 2 * (n - 1) + half + 1)
                    for m in range(C):
                        for c in range(C):
                            last = pe.matmul(ps[:, 4 * half + m, :], w1[:, c, m * P:(m + 1) * P],
                                             o[:, c, half * HALF:(half + 1) * HALF], start=(c == 0), stop=(c == C - 1))
                    last.then_inc(s["multiplied"], 1)
                for half in range(2):
                    pe.wait_ge(s["activated"], 10 * n + 2 * (half + 1))
                    for c in range(C):
                        last = pe.matmul(ps[:, 4 * half + 2, :], w2[:, c, :], h1[:, c, half * HALF:(half + 1) * HALF],
                                         start=(c == 0), stop=(c == C - 1))
                    last.then_inc(s["multiplied"], 1)
                for half in range(2):
                    pe.wait_ge(s["activated"], 10 * n + 4 + half + 1)
                    pe.matmul(ps[0:64, 4 * half + 3, :], w3[:, :], h2[:, half * HALF:(half + 1) * HALF],
                              start=True, stop=True).then_inc(s["multiplied"], 1)
                for half in range(2):
                    pe.wait_ge(s["activated"], 10 * n + 6 + half + 1)
                    pe.matmul(ps[:, 4 * half, :], w4r[:, :], h3[:, half * HALF:(half + 1) * HALF],
                              start=True, stop=True).then_inc(s["multiplied"], 1)
            o = state[3]
            for t in range(T):
                pe.wait_ge(s["state_updated"], 5 + t // 4)
                for c in range(C):
                    last = pe.transpose(ps[:, t // 2, (t % 2) * D + c * P:(t % 2) * D + (c + 1) * P],
                                        o[:, c, t * P:(t + 1) * P], k.ident[:, :])
                if t % 2:
                    last.then_inc(s["transposed"], 1)

        @block.scalar
        def _(act):
            act.wait_ge(s["halfway"], 1)
            act.activation(g[:, 4:5], ps[:, 7, 0:1], ACT.Gelu, bias=cols[:, 3:4]).then_inc(s["rows_ready"], 1)
            act.wait_ge(s["halfway"], 2)
            act.activation(g[0:64, 5:6], ps[0:64, 7, 1:2], ACT.Gelu, bias=cols[0:64, 4:5]).then_inc(s["rows_ready"], 1)
            act.wait_ge(s["halfway"], 3)
            act.activation(g[:, 6:7], ps[:, 7, 2:3], ACT.Tanh, bias=hb[:, 1:2], scale=0.5).then_inc(s["columns_ready"], 1)
            for n in range(3):
                for half in range(2):
                    q = slice(half * HALF, (half + 1) * HALF)
                    act.wait_ge(s["multiplied"], 8 * n + half + 1)
                    for m in range(C):
                        act.activation(h1[:, m, q], ps[:, 4 * half + m, :], ACT.Gelu,
                                       bias=b1[:, m:m + 1]).then_inc(s["activated"], 1)
                for half in range(2):
                    q = slice(half * HALF, (half + 1) * HALF)
                    act.wait_ge(s["multiplied"], 8 * n + 3 + half)
                    act.activation(h2[:, q], ps[:, 4 * half + 2, :], ACT.Gelu, bias=cols[:, 0:1]).then_inc(s["activated"], 1)
                for half in range(2):
                    q = slice(half * HALF, (half + 1) * HALF)
                    act.wait_ge(s["multiplied"], 8 * n + 5 + half)
                    act.activation(h3[:, q], ps[0:64, 4 * half + 3, :], ACT.Gelu,
                                   bias=cols[0:64, 1:2]).then_inc(s["activated"], 1)
                for half in range(2):
                    q = slice(half * HALF, (half + 1) * HALF)
                    act.wait_ge(s["multiplied"], 8 * n + 7 + half)
                    act.activation(th[:, q], ps[:, 4 * half, :], ACT.Tanh, bias=hb[:, 0:1], scale=0.5).then_inc(s["activated"], 1)
    k.loads = k.loading(NL)
    k.end_stage()


def expert_ffn(k):
    nc, s, ps, a = k.nc, k.sem, k.ps, k.a
    with ExitStack() as ctx:
        def sb(name, shape, dt=F32):
            return ctx.enter_context(nc.sbuf_tensor(k.unique(name), shape, dt))

        rw = sb("e_rw", [P, C, E1])
        rb = sb("e_rb", [P, E1])
        w1 = sb("e_w1", [P, E1, C, F1])
        w2 = sb("e_w2", [P, E1, D])
        b1 = sb("e_b1", [P, E1])
        b2 = sb("e_b2", [E1, D])
        logit = sb("e_logit", [P, T, E1])
        best = sb("e_best", [P, T, 8])
        bi = sb("e_bi", [P, T, 8], U32)
        bf = sb("e_bf", [P, T, 8])
        number = k.number[:, 0:E1].unsqueeze(1).broadcast_to([P, T, E1])
        gap = sb("e_gap", [P, T])
        wt = sb("e_wt", [P, 3, T])
        mask = sb("e_mask", [P, T, E1])
        pick = sb("e_pick", [P, T, E1])
        maskT = sb("e_maskT", [E1, S])
        h1 = sb("e_h1", [P, 2, S])
        acc = sb("e_acc", [P, T, D])
        block = k.block

        @block.sync
        def _(sp):
            ld = s["loaded"]
            sp.dma_start(rw[:, :, :], a["L1_ffn_router_w"].rearrange("(c p) n -> p c n", p=P)).then_inc(ld, 16)
            sp.dma_start(rb[:, :], a["L1_ffn_router_b"].partition_broadcast(P)).then_inc(ld, 16)
            for e in range(E1):
                sp.dma_start(w1[:, e, :, :], a["L1_ffn_W1"][e].rearrange("(c p) n -> p c n", p=P)).then_inc(ld, 16)
            sp.dma_start(b1[:, :], a["L1_ffn_b1"].rearrange("e p -> p e")).then_inc(ld, 16)
            sp.dma_start(w2[:, :, :], a["L1_ffn_W2"].rearrange("e p n -> p e n")).then_inc(ld, 16)
            sp.dma_start(b2[:, :], a["L1_ffn_b2"]).then_inc(ld, 16)

        NL = 5 + E1
        layer_norm(k, k.x)

        @block.tensor
        def _(pe):
            pe.wait_ge(s["loaded"], k.loading(NL))
            for t in range(T):
                for c in range(C):
                    last = pe.matmul(ps[:, 7, t * E1:(t + 1) * E1], k.yT[:, c, t * P:(t + 1) * P], rw[:, c, :],
                                     start=(c == 0), stop=(c == C - 1))
            last.then_inc(s["scored"], 1)

            def up(e):
                if e >= 2:
                    pe.wait_ge(s["activated"], 2 * (e - 1))
                for half in range(2):
                    for c in range(C):
                        last = pe.matmul(ps[:, 2 * (e % 2) + half, :], w1[:, e, c, :],
                                         k.yT[:, c, half * HALF:(half + 1) * HALF], start=(c == 0), stop=(c == C - 1))
                    last.then_inc(s["multiplied"], 1)

            def down(e):
                for j in range(T // 2):
                    n = (T // 2) * e + j
                    if n >= 3:
                        pe.wait_ge(s["weighted"], n - 2)
                    pe.wait_ge(s["activated"], 2 * e + j // 2 + 1)
                    for i in range(2):
                        t = 2 * j + i
                        last = pe.matmul(ps[:, 4 + n % 3, i * D:(i + 1) * D], h1[:, e % 2, t * P:(t + 1) * P],
                                         w2[:, e, :], start=True, stop=True)
                    last.then_inc(s["merged_ready"], 1)

            up(0)
            for e in range(E1):
                if e + 1 < E1:
                    up(e + 1)
                down(e)
            pe.wait_ge(s["routed"], 1)
            pe.wait_ge(s["weighted"], (T // 2) * E1)
            for t in range(T):
                last = pe.transpose(ps[0:E1, t // 4, (t % 4) * P:(t % 4 + 1) * P], mask[:, t, :], k.ident[:, :])
            last.then_inc(s["transposed"], 1)
            pe.wait_ge(s["columns_ready"], 1)
            for t in range(T):
                last = pe.matmul(ps[:, 4 + t // 2, (t % 2) * D:(t % 2 + 1) * D], maskT[:, t * P:(t + 1) * P], b2[:, :],
                                 start=True, stop=True)
            last.then_inc(s["results_ready"], 1)

        @block.scalar
        def _(act):
            for e in range(E1):
                if e == 1:
                    act.wait_ge(s["sums_ready"], 1)
                    act.activation(wt[:, 0, :], gap[:, :], ACT.Exp).then_inc(s["exponentiated"], 1)
                if e >= 2:
                    act.wait_ge(s["merged_ready"], (T // 2) * (e - 1))
                for half in range(2):
                    act.wait_ge(s["multiplied"], 2 * e + half + 1)
                    act.activation(h1[:, e % 2, half * HALF:(half + 1) * HALF], ps[:, 2 * (e % 2) + half, :], ACT.Gelu,
                                   bias=b1[:, e:e + 1]).then_inc(s["activated"], 1)
            act.wait_ge(s["transposed"], 1)
            act.activation(maskT[:, :].rearrange("p (a b) -> p a b", a=2), ps[0:E1, 0:2, :], ACT.Copy).then_inc(s["columns_ready"], 1)

        @block.vector
        def _(dve):
            link = stepper(dve, s["vector_step"])
            dve.wait_ge(s["scored"], 1)
            link(dve.tensor_tensor(logit[:, :, :], ps[:, 7, 0:T * E1].rearrange("p (t e) -> p t e", t=T),
                                   rb[:, :].unsqueeze(1).broadcast_to([P, T, E1]), ALU.add))
            for t in range(T):
                last = dve.max(best[:, t, :], logit[:, t, :])
            link(last)
            for t in range(T):
                last = dve.max_index(bi[:, t, :], best[:, t, :], logit[:, t, :])
            link(last)
            dve.tensor_tensor(gap[:, :], best[:, :, 1], best[:, :, 0], ALU.subtract).then_inc(s["sums_ready"], 1)
            link(dve.tensor_copy(bf[:, :, :], bi[:, :, :]))
            dve.wait_ge(s["exponentiated"], 1)
            link(dve.tensor_scalar(wt[:, 2, :], wt[:, 0, :], 1.0, None, ALU.add))
            link(dve.reciprocal(wt[:, 1, :], wt[:, 2, :]))
            link(dve.tensor_tensor(wt[:, 2, :], wt[:, 0, :], wt[:, 1, :], ALU.mult))
            for i, m in ((0, mask), (1, pick)):
                link(dve.tensor_tensor(m[:, :, :], number, bf[:, :, i:i + 1].broadcast_to([P, T, E1]), ALU.is_equal))
                link(dve.tensor_tensor(m[:, :, :], m[:, :, :], wt[:, 1 + i, :].unsqueeze(2).broadcast_to([P, T, E1]), ALU.mult))
            dve.tensor_tensor(mask[:, :, :], mask[:, :, :], pick[:, :, :], ALU.add).then_inc(s["routed"], 1)
            dve.wait_ge(s["routed"], 1)
            for e in range(E1):
                for j in range(T // 2):
                    n = (T // 2) * e + j
                    dve.wait_ge(s["merged_ready"], n + 1)
                    for i in range(2):
                        t = 2 * j + i
                        src = ps[:, 4 + n % 3, i * D:(i + 1) * D]
                        if e == 0:
                            last = dve.tensor_scalar(acc[:, t, :], src, mask[:, t, e:e + 1], None, ALU.mult)
                        else:
                            last = dve.scalar_tensor_tensor(out=acc[:, t, :], in0=src, scalar=mask[:, t, e:e + 1],
                                                            in1=acc[:, t, :], op0=ALU.mult, op1=ALU.add)
                    last.then_inc(s["weighted"], 1)
                dve.wait_ge(s["weighted"], (T // 2) * (e + 1))
            dve.wait_ge(s["results_ready"], 1)
            av = acc[:, :, :].rearrange("p (j t) n -> p j (t n)", t=2)
            xv = k.x[:, :, :].rearrange("p (j t) n -> p j (t n)", t=2)
            link(dve.tensor_tensor(av, av, ps[:, 4:8, :], ALU.add))
            dve.scalar_tensor_tensor(out=xv, in0=av, scalar=0.5, in1=xv, op0=ALU.mult, op1=ALU.add)
    k.loads = k.loading(NL)
    k.end_stage()


def lora_ffn(k):
    nc, s, ps, a = k.nc, k.sem, k.ps, k.a
    NE = len(RANKS)
    with ExitStack() as ctx:
        def sb(name, shape, dt=F32):
            return ctx.enter_context(nc.sbuf_tensor(k.unique(name), shape, dt))

        w = sb("r_w", [P, C, D])
        wp = sb("r_wp", [P, C, PR])
        wd = sb("r_wd", [P, C, RT])
        wu = sb("r_wu", [RT, D])
        bp = sb("r_bp", [PR, 1])
        sim = sb("r_sim", [PR, NE])
        simq = sb("r_simq", [PR, 4, NE])
        temp = sb("r_temp", [P, 2])
        proj = sb("r_proj", [PR, S])
        projq = sb("r_projq", [PR, S])
        norm = sb("r_norm", [P, T])
        inv = sb("r_inv", [P, T])
        logit = sb("r_logit", [P, T, 8])
        prob = sb("r_prob", [P, T, 8])
        best = sb("r_best", [P, T, 8])
        bi = sb("r_bi", [P, T, 8], U32)
        bf = sb("r_bf", [P, T, 8])
        total = sb("r_total", [P, 2, T])
        number = k.number[:, 0:NE].unsqueeze(1).broadcast_to([P, T, NE])
        ret = sb("r_ret", [P, T, NE])
        down = sb("r_down", [P, T, RT])
        downT = sb("r_downT", [RT, S])
        block = k.block

        @block.sync
        def _(sp):
            ld = s["loaded"]
            sp.dma_start(w[:, :, :], a["L2_ffn_WT"].rearrange("(c p) n -> p c n", p=P)).then_inc(ld, 16)
            sp.dma_start(wp[:, :, :], a["L2_ffn_WpT"].rearrange("(c p) n -> p c n", p=P)).then_inc(ld, 16)
            sp.dma_start(wd[:, :, :], a["L2_ffn_WdT"].rearrange("(c p) n -> p c n", p=P)).then_inc(ld, 16)
            sp.dma_start(wu[:, :], a["L2_ffn_WuT"]).then_inc(ld, 16)
            sp.dma_start(bp[:, :], a["L2_ffn_bp"].rearrange("(p o) -> p o", o=1)).then_inc(ld, 16)
            sp.dma_start(sim[:, :], a["L2_ffn_sim"]).then_inc(ld, 16)
            sp.dma_start(temp[:, 0:1], a["L2_ffn_temp"].partition_broadcast(P)).then_inc(ld, 16)

        NL = 7
        layer_norm(k, k.x)

        @block.tensor
        def _(pe):
            pe.wait_ge(s["loaded"], k.loading(NL))
            for half in range(2):
                for c in range(C):
                    last = pe.matmul(ps[0:PR, half, :], wp[:, c, :], k.yT[:, c, half * HALF:(half + 1) * HALF],
                                     start=(c == 0), stop=(c == C - 1))
                last.then_inc(s["multiplied"], 1)
            for t in range(T):
                for c in range(C):
                    last = pe.matmul(ps[:, 3, t * RT:(t + 1) * RT], k.yT[:, c, t * P:(t + 1) * P], wd[:, c, :],
                                     start=(c == 0), stop=(c == C - 1))
            last.then_inc(s["columns_ready"], 1)
            pe.wait_ge(s["sums_ready"], 1)
            pe.matmul(ps[0:PR, 2, 0:NE], k.ones[0:PR, 0:PR], simq[:, 0, :], start=True, stop=True).then_inc(s["rows_ready"], 1)
            pe.wait_ge(s["activated"], 4)
            pe.wait_ge(s["split_ready"], 1)
            for t in range(T):
                pe.matmul(ps[:, 2, 64 + t * NE:64 + (t + 1) * NE], proj[:, t * P:(t + 1) * P], simq[:, 3, :], start=True, stop=True)
                last = pe.matmul(ps[:, 2, 128 + t:129 + t], projq[:, t * P:(t + 1) * P], k.ones[0:PR, 0:1], start=True, stop=True)
            last.then_inc(s["scored"], 1)
            for t in range(T):
                for c in range(C):
                    pe.matmul(ps[:, 4 + t // 2, (t % 2) * D:(t % 2 + 1) * D], k.yT[:, c, t * P:(t + 1) * P], w[:, c, :],
                              start=(c == 0), stop=False)
                if t == 0:
                    pe.wait_ge(s["weighted"], 1)
                    for u in range(T):
                        last = pe.transpose(ps[0:RT, u // 4, (u % 4) * P:(u % 4 + 1) * P], down[:, u, :], k.ident[:, :])
                    last.then_inc(s["transposed"], 1)
                    pe.wait_ge(s["halfway"], 1)
                last = pe.matmul(ps[:, 4 + t // 2, (t % 2) * D:(t % 2 + 1) * D], downT[:, t * P:(t + 1) * P], wu[:, :],
                                 start=False, stop=True)
                if t % 2:
                    last.then_inc(s["results_ready"], 1)

        @block.scalar
        def _(act):
            for half in range(2):
                act.wait_ge(s["multiplied"], half + 1)
                q = slice(half * HALF, (half + 1) * HALF)
                act.activation(proj[:, q], ps[0:PR, half, :], ACT.Identity, bias=bp[:, :]).then_inc(s["activated"], 1)
                act.activation(projq[:, q], ps[0:PR, half, :], ACT.Square, bias=bp[:, :]).then_inc(s["activated"], 1)
            act.wait_ge(s["rows_ready"], 1)
            act.activation(simq[:, 1, :], ps[0:PR, 2, 0:NE], ACT.Sqrt).then_inc(s["std_ready"], 1)
            act.wait_ge(s["scored"], 1)
            act.activation(norm[:, :], ps[:, 2, 128:128 + T], ACT.Sqrt).then_inc(s["std_ready"], 1)
            act.wait_ge(s["variance_ready"], 1)
            act.activation(temp[:, 1:2], temp[:, 1:2], ACT.Exp).then_inc(s["exponentiated"], 1)
            act.wait_ge(s["max_taken"], 1)
            act.activation(prob[:, :, :], prob[:, :, :], ACT.Exp).then_inc(s["exponentiated"], 1)
            act.wait_ge(s["transposed"], 1)
            act.activation(downT[:, :].rearrange("p (a b) -> p a b", a=2), ps[0:RT, 0:2, :], ACT.Copy).then_inc(s["halfway"], 1)

        @block.vector
        def _(dve):
            link = stepper(dve, s["vector_step"])
            dve.memset(logit[:, :, :], LOWEST)
            dve.wait_ge(s["loaded"], k.loading(NL))
            dve.tensor_tensor(simq[:, 0, :], sim[:, :], sim[:, :], ALU.mult).then_inc(s["sums_ready"], 1)
            dve.tensor_scalar(temp[:, 1:2], temp[:, 0:1], float(np_log100()), None, ALU.min).then_inc(s["variance_ready"], 1)
            dve.wait_ge(s["std_ready"], 1)
            link(dve.tensor_scalar(simq[:, 1, :], simq[:, 1, :], 1e-12, None, ALU.max))
            link(dve.reciprocal(simq[:, 2, :], simq[:, 1, :]))
            dve.tensor_tensor(simq[:, 3, :], sim[:, :], simq[:, 2, :], ALU.mult).then_inc(s["split_ready"], 1)
            dve.wait_ge(s["std_ready"], 2)
            link(dve.tensor_scalar(norm[:, :], norm[:, :], 1e-12, None, ALU.max))
            link(dve.reciprocal(inv[:, :], norm[:, :]))
            dve.wait_ge(s["exponentiated"], 1)
            link(dve.tensor_scalar(inv[:, :], inv[:, :], temp[:, 1:2], None, ALU.mult))
            link(dve.tensor_tensor(logit[:, :, 0:NE], ps[:, 2, 64:64 + T * NE].rearrange("p (t e) -> p t e", t=T),
                                   inv[:, :].unsqueeze(2).broadcast_to([P, T, NE]), ALU.mult))
            for t in range(T):
                last = dve.max(best[:, t, :], logit[:, t, :])
            link(last)
            for t in range(T):
                last = dve.max_index(bi[:, t, :], best[:, t, :], logit[:, t, :])
            link(last)
            dve.tensor_tensor(prob[:, :, :], logit[:, :, :], best[:, :, 0:1].broadcast_to([P, T, 8]),
                              ALU.subtract).then_inc(s["max_taken"], 1)
            link(dve.tensor_copy(bf[:, :, :], bi[:, :, :]))
            dve.wait_ge(s["exponentiated"], 2)
            link(dve.tensor_reduce(total[:, 0, :], prob[:, :, 0:NE], AX.X, ALU.add))
            dve.reciprocal(total[:, 1, :], total[:, 0, :])
            link(dve.tensor_tensor(ret[:, :, :], number, bf[:, :, 0:1].broadcast_to([P, T, NE]), ALU.is_equal))
            link(dve.tensor_tensor(ret[:, :, :], ret[:, :, :], total[:, 1, :].unsqueeze(2).broadcast_to([P, T, NE]), ALU.mult))
            dve.wait_ge(s["columns_ready"], 1)
            r0 = 0
            for e, r in enumerate(RANKS):
                last = dve.tensor_tensor(down[:, :, r0:r0 + r],
                                         ps[:, 3, 0:T * RT].rearrange("p (t r) -> p t r", t=T)[:, :, r0:r0 + r],
                                         ret[:, :, e:e + 1].broadcast_to([P, T, r]), ALU.mult)
                r0 += r
            last.then_inc(s["weighted"], 1)
            for j in range(T // 2):
                dve.wait_ge(s["results_ready"], j + 1)
                xv = k.x[:, 2 * j:2 * j + 2, :].rearrange("p t n -> p (t n)")
                dve.scalar_tensor_tensor(out=xv, in0=ps[:, 4 + j, :], scalar=0.5, in1=xv, op0=ALU.mult, op1=ALU.add)
    k.loads = k.loading(NL)
    k.end_stage()


def np_log100():
    import numpy as np
    return np.log(1.0 / 0.01)


def gaussian_attention(k):
    import math
    nc, s, ps, a = k.nc, k.sem, k.ps, k.a
    NB = len(STD)
    reach = math.sqrt(2 * 104.0)
    assert max(sd * reach + off for sd, off in zip(STD, STD)) < P
    with ExitStack() as ctx:
        def sb(name, shape, dt=F32):
            return ctx.enter_context(nc.sbuf_tensor(k.unique(name), shape, dt))

        wi = sb("g_wi", [P, C, D])
        wo = sb("g_wo", [P, C, D])
        dist = sb("g_dist", [P, 3 * P])
        sq = sb("g_sq", [P, NB, 3 * P])
        band = sb("g_band", [P, NB, 3 * P])
        v = sb("g_v", [P, T, D])
        at = sb("g_at", [P, C, S])
        block = k.block

        @block.sync
        def _(sp):
            sp.dma_start(dist[:, :], k.dist_rows[:, S - 2 * P:S + P]).then_inc(s["loaded"], 16)
            sp.dma_start(wi[:, :, :], a["L3_attn_input_weightsT"].rearrange("(c p) n -> p c n", p=P)).then_inc(s["loaded"], 16)
            sp.dma_start(wo[:, :, :], a["L3_attn_output_weightT"].rearrange("(c p) n -> p c n", p=P)).then_inc(s["loaded"], 16)
            sp.wait_ge(s["loaded"], k.loading(3))

        layer_norm(k, k.xp)

        @block.vector
        def _(dve):
            link = stepper(dve, s["vector_step"])
            dve.wait_ge(s["loaded"], k.loading(3))
            for i, sd in enumerate(STD):
                last = dve.tensor_scalar(sq[:, i, :], dist[:, :], sd, 1.0 / sd, ALU.subtract, ALU.mult)
            link(last)
            dve.tensor_tensor(sq[:, :, :], sq[:, :, :], sq[:, :, :], ALU.mult).then_inc(s["sums_ready"], 1)
            dve.wait_ge(s["exponentiated"], 1)
            for i, sd in enumerate(STD):
                last = dve.tensor_scalar(band[:, i, :], sq[:, i, :], 1.0 / (sd * math.sqrt(2.0 * math.pi)), None, ALU.mult)
            last.then_inc(s["probs_ready"], 1)
            for j in range(T // 2):
                dve.wait_ge(s["results_ready"], j + 1)
                xv = k.xp[:, 2 * j:2 * j + 2, :].rearrange("p t n -> p (t n)")
                dve.tensor_tensor(xv, ps[:, 4 + j, :], xv, ALU.add)

        @block.scalar
        def _(act):
            act.wait_ge(s["sums_ready"], 1)
            act.activation(sq[:, :, :], sq[:, :, :], ACT.Exp, scale=-0.5).then_inc(s["exponentiated"], 1)
            for j in range(T // 2):
                act.wait_ge(s["multiplied"], j + 1)
                act.activation(v[:, 2 * j:2 * j + 2, :].rearrange("p t n -> p (t n)"), ps[:, 4 + j, :], ACT.Copy).then_inc(s["v_ready"], 1)
            for c in range(C):
                for half in range(2):
                    act.wait_ge(s["weighted"], 2 * c + half + 1)
                    act.activation(at[:, c, half * HALF:(half + 1) * HALF], ps[:, 2 * c + half, :], ACT.Copy).then_inc(s["heads_done"], 1)

        @block.tensor
        def _(pe):
            pe.wait_ge(s["loaded"], k.loading(3))
            for t in range(T):
                for c in range(C):
                    last = pe.matmul(ps[:, 4 + t // 2, (t % 2) * D:(t % 2 + 1) * D], k.yT[:, c, t * P:(t + 1) * P], wi[:, c, :],
                                     start=(c == 0), stop=(c == C - 1))
                if t % 2:
                    last.then_inc(s["multiplied"], 1)
            pe.wait_ge(s["v_ready"], T // 2)
            pe.wait_ge(s["probs_ready"], 1)
            for c in range(C):
                for qt in range(T):
                    near = [kt for kt in (qt - 1, qt, qt + 1) if 0 <= kt < T]
                    for kt in near:
                        for hh in range(G):
                            last = pe.matmul(ps[32 * hh:32 * hh + 32, 2 * c + qt // 4, (qt % 4) * P:(qt % 4 + 1) * P],
                                             v[:, kt, c * P + 32 * hh:c * P + 32 * hh + 32],
                                             band[:, hh, (qt - kt + 1) * P:(qt - kt + 2) * P],
                                             start=(kt == near[0]), stop=(kt == near[-1]), tile_position=(0, 32 * hh))
                    if qt % 4 == 3:
                        last.then_inc(s["weighted"], 1)
            pe.wait_ge(s["heads_done"], 4)
            for t in range(T):
                for c in range(C):
                    last = pe.matmul(ps[:, 4 + t // 2, (t % 2) * D:(t % 2 + 1) * D], at[:, c, t * P:(t + 1) * P], wo[:, c, :],
                                     start=(c == 0), stop=(c == C - 1))
                if t % 2:
                    last.then_inc(s["results_ready"], 1)
    k.loads = k.loading(3)
    k.end_stage()


def attention_plan(variant):
    def maxima(g):
        return [(g, hh, qt, ch) for hh in range(G) for qt in range(T)
                for ch in range(2 if variant else qt // 4 + 1)]

    plan, nmax, nscore = [], 0, 0

    def take(steps):
        nonlocal nmax
        for st in steps:
            plan.append(("max", nmax) + st)
            nmax += 1
    take(maxima(0))
    plan.append(("turn", 0))
    late = []
    for g in range(NG):
        steps = [(half, kt) for half in range(2) for kt in range(T if variant else 4 * half + 4)]
        todo = maxima(g + 1) if g + 1 < NG else []
        done, turned = 0, not todo
        for i, (half, kt) in enumerate(steps):
            upto = max(done, min(len(todo), -(-len(todo) * (i + 1) // (len(steps) - 3))))
            q = [done + (upto - done) * j // 4 for j in range(5)]
            a, b = (2, 3) if variant == 0 else (1, 3)
            plan.append(("score", nscore, g, half, kt, 0))
            take(todo[q[0]:q[a]])
            plan.append(("score", nscore + 1, g, half, kt, 1))
            take(todo[q[a]:q[b]])
            plan.extend(late)
            take(todo[q[b]:q[4]])
            nscore += 2
            done = upto
            late = [("weigh", nscore // 2 - 1, g, half, kt)]
            if (half, kt) == steps[-1] or steps[i + 1][0] != half:
                late.append(("finish", 2 * g + half))
            if done == len(todo) and not turned:
                plan.append(("turn", g + 1))
                turned = True
    plan.extend(late)
    return plan


def attention(k, variant):
    nc, s, ps, a = k.nc, k.sem, k.ps, k.a
    plan = attention_plan(variant)
    name = ("L0_attn_", "L1_attn_", "L2_attn_")[variant]
    with ExitStack() as outer:
        def osb(n, shape, dt=F32):
            return outer.enter_context(nc.sbuf_tensor(k.unique(n), shape, dt))

        va = osb("a_va", [P, T, H, PAD])
        qa = osb("a_qa", [P, H, S], BF16)
        ka = osb("a_ka", [P, H, S], BF16)
        bo = osb("a_bo", [P, D])
        wo = osb("a_wo", [P, G, D])

        with ExitStack() as ctx:
            def sb(n, shape, dt=F32):
                return ctx.enter_context(nc.sbuf_tensor(k.unique(n), shape, dt))

            w = [sb("a_wq", [P, C, D]), sb("a_wk", [P, C, D])]
            wr = [sb("a_wqr", [P, C, D]), sb("a_wkr", [P, C, D])] if variant == 1 else w
            tmp = sb("a_tmp", [P, C * D]) if variant == 1 else None
            wv = sb("a_wv", [P, C, D])
            brow = sb("a_brow", [1, 2, D])
            browr = sb("a_browr", [1, 2, D]) if variant == 1 else brow
            bcol = sb("a_bcol", [P, 2 * C])
            bv = sb("a_bv", [P, D])
            turnc = sb("a_turnc", [P, 2, DK]) if variant == 1 else None
            yo = k.yT if variant else sb("a_yo", [P, C, S])
            qf = sb("a_qf", [P, 2, S])
            parts = sb("a_parts", [P, 2, C, 3, S], BF16)
            vn = qf[:, :, :].rearrange("p a n -> p (a n)").rearrange("p (t n) -> p t n", t=T)
            block = k.block
            NL = 8 + G + (2 if variant == 1 else 0)
            bounced = [s["bounced0"], s["bounced1"]]
            NBOUNCE = 2 * T if variant == 1 else 2

            @block.vector
            def _(dve):
                dve.memset(wo[:, :, :], 0.0).then_inc(s["cleared"], 1)
                dve.memset(va[:, :, :, DK + 1:PAD], 0.0)
                dve.memset(va[:, :, :, DK:DK + 1], 1.0)

            @block.sync
            def _(sp):
                ld = s["loaded"]
                if variant == 2:
                    wT, b = a["L2_attn_qkv_wT"], a["L2_attn_qkv_b"]
                    src = [wT[:, i * D:(i + 1) * D] for i in range(3)] + [b[i * D:(i + 1) * D] for i in range(3)]
                    src += [a["L2_attn_out_wT"], a["L2_attn_out_b"]]
                elif variant == 1:
                    src = [a[name + n] for n in ("wqT", "wkT", "wvT", "bq", "bk", "bv", "woT", "bo")]
                else:
                    src = [a[name + n] for n in ("WqT", "WkT", "WvT", "bq", "bk", "bv", "WoT", "bo")]
                for i, dst in enumerate((w[0], w[1], wv)):
                    sp.dma_start(dst[:, :, :], src[i].rearrange("(c p) n -> p c n", p=P)).then_inc(ld, 16)
                for i in range(2):
                    sp.dma_start(brow[:, i, :], src[3 + i].rearrange("(o n) -> o n", o=1)).then_inc(ld, 16)
                sp.dma_start(bv[:, :], src[5].partition_broadcast(P)).then_inc(ld, 16)
                sp.dma_start(bo[:, :], src[7].partition_broadcast(P)).then_inc(ld, 16)
                sp.dma_start(ka[KT:KT + 3, :, :], k.ones_rows[0:3].rearrange("a (h n) -> a h n", h=H)).then_inc(ld, 16)
                if variant == 1:
                    for i, n in enumerate(("cos", "sin")):
                        sp.dma_start(turnc[:, i, :], a[name + n][a[name + n].shape[0] - 1].partition_broadcast(P)).then_inc(ld, 16)
                sp.wait_ge(s["cleared"], 1)
                for hh in range(G):
                    sp.dma_start(wo[PAD * hh:PAD * hh + DK, :, :],
                                 src[6].rearrange("(g h d) n -> h d g n", h=G, d=DK)[hh]).then_inc(ld, 16)
                sp.wait_ge(ld, k.loading(NL))

            layer_norm(k, k.x, qf[:, :, :].rearrange("p a n -> p (a n)").rearrange("p (t n) -> p t n", t=T))

            @block.sync
            def _(sp):
                def bring(g, n=2):
                    for r, pair in enumerate(TERMS):
                        for qk, dst in ((0, qa), (1, ka)):
                            sp.dma_start(dst[DK * r:DK * r + DK, G * g:G * (g + n), :],
                                         k.qk_parts[qk, pair[qk], G * DK * g:G * DK * (g + n), :]
                                         .rearrange("(h d) n -> d h n", d=DK)).then_inc(s["heads_loaded"], 16)

                for m in range(C):
                    for qk in range(2):
                        sp.wait_ge(s["split_ready"], 2 * m + qk + 1)
                        if variant == 1:
                            for c in range(T):
                                dst = k.qk_parts[qk].rearrange("x (h d) (c l) -> c d x h l", d=DK, c=H)[T * m + c]
                                sp.dma_start(dst, parts[DK * c:DK * c + DK, qk, m, :, :]
                                             .rearrange("d x (h l) -> d x h l", h=H)).then_inc(bounced[m], 16)
                        else:
                            sp.dma_start(k.qk_parts[qk, :, m * P:(m + 1) * P, :].rearrange("x f n -> f x n"),
                                         parts[:, qk, m, :, :]).then_inc(bounced[m], 16)
                    if variant != 1:
                        sp.wait_ge(bounced[m], 16 * NBOUNCE)
                        bring(2 * m)
                if variant == 1:
                    for m in range(C):
                        sp.wait_ge(bounced[m], 16 * NBOUNCE)
                    bring(0, NG)
                    sp.wait_ge(s["v_ready"], T // 2)
                    sp.dma_start(k.v_rows.rearrange("(t p) n -> p t n", p=P), vn[:, :, :]).then_inc(s["v_bounced"], 16)
                    sp.wait_ge(s["v_bounced"], 16)
                    for kt in range(T):
                        for c in range(2):
                            sp.dma_start(va[64 * c:64 * c + 64, kt, :, 0:DK],
                                         k.v_rows.rearrange("(h l) (c d) -> c l h d", h=H, d=DK)[2 * kt + c])\
                              .then_inc(s["v_loaded"], 16)
                    sp.wait_ge(s["v_loaded"], 16 * 2 * T)
                sp.wait_ge(s["heads_loaded"], 16 * 2 * len(TERMS) * (1 if variant == 1 else C))

            @block.tensor
            def _(pe):
                pe.wait_ge(s["loaded"], k.loading(NL))
                if variant == 1:
                    pe.wait_ge(s["rotated"], 1)
                for i in range(2):
                    for m in range(C):
                        last = pe.matmul(ps[:, 7, 2 * i + m:2 * i + m + 1], browr[0:1, i, m * P:(m + 1) * P], k.ones[0:1, 0:1],
                                         start=True, stop=True)
                last.then_inc(s["rows_ready"], 1)
                if not variant:
                    pe.wait_ge(s["transposed"], C)
                n = 0
                for m in range(C):
                    for qk in range(2):
                        for half in range(2):
                            if n >= 6:
                                pe.wait_ge(s["activated"], n - 5)
                            for c in range(C):
                                last = pe.matmul(ps[:, n % 6, :], wr[qk][:, c, m * P:(m + 1) * P],
                                                 yo[:, c, half * HALF:(half + 1) * HALF], start=(c == 0), stop=(c == C - 1))
                            last.then_inc(s["multiplied"], 1)
                            n += 1
                pe.wait_ge(s["columns_ready"], 1)
                for t in range(T):
                    if t >= 4 and t % 2 == 0:
                        pe.wait_ge(s["v_ready"], t // 2 - 1)
                    for c in range(C):
                        last = pe.matmul(ps[:, 6 + t // 2 % 2, (t % 2) * D:(t % 2 + 1) * D], yo[:, c, t * P:(t + 1) * P], wv[:, c, :],
                                         start=(c == 0), stop=(c == C - 1))
                    if t % 2:
                        last.then_inc(s["v_scored"], 1)

            @block.scalar
            def _(act):
                n = 0
                if not variant:
                    for c in range(C):
                        act.activation(yo[:, c, :].rearrange("p (r t) -> p t r", t=T),
                                       k.yT[:, c, :].rearrange("p (t r) -> p t r", t=T), ACT.Copy).then_inc(s["transposed"], 1)
                act.wait_ge(s["columns_ready"], 1)
                for m in range(C):
                    for qk in range(2):
                        if m:
                            act.wait_ge(s["split_ready"], qk + 1)
                        for half in range(2):
                            act.wait_ge(s["multiplied"], n + 1)
                            act.activation(qf[:, qk, half * HALF:(half + 1) * HALF], ps[:, n % 6, :], ACT.Identity, bias=bcol[:, 2 * qk + m:2 * qk + m + 1]).then_inc(s["activated"], 1)
                            n += 1

            @block.vector
            def _(dve):
                link = stepper(dve, s["vector_step"])
                if variant == 1:
                    dve.wait_ge(s["loaded"], k.loading(NL))
                    for src, dst, np_, nr in ((w[0], wr[0], P, C * H), (w[1], wr[1], P, C * H), (brow, browr, 1, 2 * H)):
                        sv = src[:, :, :].rearrange("p c (h e o) -> p (c h) e o", o=2, e=DK // 2)
                        dv = dst[:, :, :].rearrange("p c (h e o) -> p (c h) e o", o=2, e=DK // 2)
                        tv = tmp[0:np_, 0:nr * DK // 2].rearrange("p (b e) -> p b e", e=DK // 2)
                        for o in range(2):
                            cs = [turnc[0:np_, i, :].rearrange("p (e o) -> p e o", o=2)[:, :, o].unsqueeze(1)
                                  .broadcast_to([np_, nr, DK // 2]) for i in range(2)]
                            dve.tensor_tensor(tv, sv[:, :, :, 1 - o], cs[1], ALU.mult)
                            link(dve.tensor_tensor(dv[:, :, :, o], sv[:, :, :, o], cs[0], ALU.mult))
                            link(dve.tensor_tensor(dv[:, :, :, o], dv[:, :, :, o], tv, ALU.add if o else ALU.subtract))
                    dve.sem_inc(s["rotated"], 1)
                dve.wait_ge(s["rows_ready"], 1)
                dve.tensor_copy(bcol[:, :], ps[:, 7, 0:2 * C]).then_inc(s["columns_ready"], 1)
                for j in range(C * 2):
                    m, qk = j // 2, j % 2
                    dve.wait_ge(s["activated"], 2 * j + 2)
                    q = qf[:, qk, :]
                    link(dve.tensor_copy(parts[:, qk, m, 0, :], q))
                    link(dve.tensor_tensor(q, q, parts[:, qk, m, 0, :], ALU.subtract))
                    link(dve.tensor_copy(parts[:, qk, m, 1, :], q))
                    dve.tensor_tensor(parts[:, qk, m, 2, :], q, parts[:, qk, m, 1, :], ALU.subtract).then_inc(s["split_ready"], 1)
                if variant == 1:
                    dve.wait_ge(s["split_ready"], 2 * C)
                for j in range(T // 2):
                    dve.wait_ge(s["v_scored"], j + 1)
                    src = ps[:, 6 + j % 2, :]
                    if variant == 1:
                        dve.tensor_tensor(vn[:, 2 * j:2 * j + 2, :], src.rearrange("p (t n) -> p t n", t=2),
                                          bv[:, :].unsqueeze(1).broadcast_to([P, 2, D]), ALU.add).then_inc(s["v_ready"], 1)
                    else:
                        dve.tensor_tensor(va[:, 2 * j:2 * j + 2, :, 0:DK],
                                          src.rearrange("p (t h d) -> p t h d", t=2, h=H),
                                          bv[:, :].rearrange("p (h d) -> p h d", h=H).unsqueeze(1).broadcast_to([P, 2, H, DK]),
                                          ALU.add).then_inc(s["v_ready"], 1)
        k.loads = k.loading(NL)
        k.end_stage()

        with ExitStack() as ctx:
            def sb(n, shape, dt=F32):
                return ctx.enter_context(nc.sbuf_tensor(k.unique(n), shape, dt))

            ex = sb("a_ex", [P, 4, 2, HALF])
            part = sb("a_part", [P, 2, G * T, 2])
            mx = sb("a_mx", [P, 2, G * T])
            mf = sb("a_mf", [G * T, P])
            mp = sb("a_mp", [G * T, 3, P], BF16)
            ot = sb("a_ot", [P, NG, S])
            on = sb("a_on", [P, NG, S]) if variant == 1 else ot
            rd = sb("a_rd", [P, HALF])
            if variant == 2:
                dist = k.yT[:, :, :].rearrange("p c n -> p (c n)")[:, 0:TABLE]
                table = sb("a_table", [P, 2, TABLE])
                al = sb("a_al", [P, 4, H])
            block = k.block
            last_weigh = {}
            for e in plan:
                if e[0] == "weigh":
                    last_weigh[2 * e[2] + e[3]] = e[1] + 1
            maxima_of = [1 + max(e[1] for e in plan if e[0] == "max" and e[2] == g) for g in range(NG)]

            def columns(half, kt):
                q0 = half * HALF if variant else max(half * HALF, kt * P)
                return q0, (half + 1) * HALF - q0

            @block.sync
            def _(sp):
                if variant == 2:
                    sp.dma_start(al[:, 0, :], a["L2_attn_decay_alpha"].partition_broadcast(P)).then_inc(s["loaded"], 16)
                    sp.dma_start(dist, k.dist_rows).then_inc(s["loaded"], 16)
                for g in range(NG):
                    sp.wait_ge(s["max_split"], g + 1)
                    sp.dma_start(k.max_parts.rearrange("x (b n) -> b x n", n=P), mp[:, :, :]).then_inc(s["mbounced"], 16)
                    sp.wait_ge(s["mbounced"], 16 * (g + 1))
                    sp.dma_start(qa[KT:KT + 3, G * g:G * g + G, :],
                                 k.max_parts.rearrange("x (h n) -> x h n", h=G)).then_inc(s["max_loaded"], 16)
                    sp.wait_ge(s["max_loaded"], 16 * (g + 1))

            @block.tensor
            def _(pe):
                for e in plan:
                    if e[0] == "max":
                        _, n, g, hh, qt, ch = e
                        h = G * g + hh
                        width = HALF if variant else min(HALF, (qt + 1) * P - ch * HALF)
                        if n >= 2:
                            pe.wait_ge(s["max_taken"], n - 1)
                        if g and hh == 0 and qt == 0 and ch == 0:
                            pe.wait_ge(s["max_split"], g)
                        bank = ps[:, 6 + n % 2, :]
                        last = pe.matmul(bank[:, 0:width], qa[0:KT, h, qt * P:(qt + 1) * P],
                                         ka[0:KT, h, ch * HALF:ch * HALF + width], start=True, stop=True)
                        if not variant and ch == qt // 4:
                            last = pe.matmul(bank[:, width - P:width], k.residue[:, 0, :], k.residue[:, 1, :],
                                             start=False, stop=True, skip_group_check=True)
                        last.then_inc(s["max_scored"], 1)
                    elif e[0] == "turn":
                        g = e[1]
                        pe.wait_ge(s["max_combined"], g + 1)
                        pe.transpose(ps[0:G * T, 6, 0:P], mx[:, g % 2, :], k.ident[:, :]).then_inc(s["max_turned"], 1)
                    elif e[0] == "score":
                        _, n, g, half, kt, pair = e
                        q0, width = columns(half, kt)
                        if n >= 2:
                            pe.wait_ge(s["exponentiated"], n - 1)
                        if half == 0 and kt == 0 and pair == 0:
                            pe.wait_ge(s["max_loaded"], 16 * (g + 1))
                        for j in range(2):
                            h = G * g + 2 * pair + j
                            bank = ps[:, 2 * (n % 2) + j, :]
                            last = pe.matmul(bank[:, 0:width], ka[0:KT + 3, h, kt * P:(kt + 1) * P],
                                             qa[0:KT + 3, h, q0:q0 + width], start=True, stop=True)
                            if not variant and q0 == kt * P:
                                last = pe.matmul(bank[:, 0:P], k.residue[:, 1, :], k.residue[:, 0, :],
                                                 start=False, stop=True, skip_group_check=True)
                        last.then_inc(s["scored"], 1)
                    elif e[0] == "weigh":
                        _, i, g, half, kt = e
                        q0, width = columns(half, kt)
                        pe.wait_ge(s["exponentiated"], 2 * i + 2)
                        f = 2 * g + half
                        if kt == 0 and f >= 2:
                            pe.wait_ge(s["heads_done"], f - 1)
                        final = kt == (T - 1 if variant else 4 * half + 3)
                        for hh in range(G):
                            last = pe.matmul(ps[PAD * hh:PAD * hh + PAD, 4 + half, q0 - half * HALF:q0 - half * HALF + width],
                                             va[:, kt, G * g + hh, :], ex[:, 2 * (i % 2) + hh // 2, hh % 2, 0:width],
                                             start=(kt == 0), stop=final, tile_position=(0, PAD * hh), skip_group_check=True)
                        last.then_inc(s["weighted"], 1)
                    else:
                        f = e[1]
                        pe.wait_ge(s["heads_copied"], f + 1)
                        pe.matmul(ps[:, 4 + f % 2, :], k.sel[:, :], ot[:, f // 2, (f % 2) * HALF:(f % 2 + 1) * HALF],
                                  start=True, stop=True).then_inc(s["denominators_ready"], 1)
                pe.wait_ge(s["heads_done"], 2 * NG)
                for t in range(T):
                    for g in range(NG):
                        o = on[:, g, :]
                        if variant == 0:
                            o = o.rearrange("p (r t) -> p t r", t=T)[:, t, :]
                        else:
                            o = o[:, t * P:(t + 1) * P]
                        last = pe.matmul(ps[:, t // 2, (t % 2) * D:(t % 2 + 1) * D], o, wo[:, g, :],
                                         start=(g == 0), stop=(g == NG - 1))
                    if t % 2:
                        last.then_inc(s["results_ready"], 1)

            @block.scalar
            def _(act):
                if variant == 2:
                    act.wait_ge(s["sums_ready"], 1)
                    act.activation(al[:, 1, :], al[:, 1, :], ACT.Exp).then_inc(s["scalar_step"], 1)
                    act.wait_ge(s["scalar_step"], 1)
                    act.activation(al[:, 1, :], al[:, 1, :], ACT.Ln, bias=1.0).then_inc(s["columns_ready"], 1)

                def decay(h):
                    act.activation(table[:, h % 2, :], dist, ACT.Copy, scale=al[:, 3, h:h + 1]).then_inc(s["table_ready"], 1)

                if variant == 2:
                    act.wait_ge(s["weights_ready"], 1)
                    decay(0)
                    decay(1)
                for e in plan:
                    if variant == 2 and e[0] == "max" and e[4] == 0 and e[5] == 0:
                        h = G * e[2] + e[3]
                        if 0 < h < H - 1:
                            act.wait_ge(s["max_taken"], 2 * T * h)
                            decay(h + 1)
                    if e[0] != "score":
                        continue
                    _, n, g, half, kt, pair = e
                    width = columns(half, kt)[1]
                    act.wait_ge(s["biased"] if variant == 2 else s["scored"], n + 1)
                    if n >= 4:
                        act.wait_ge(s["weighted"], (n - 4) // 2 + 1)
                    act.activation(ex[:, 2 * (n // 2 % 2) + pair, :, 0:width], ps[:, 2 * (n % 2):2 * (n % 2) + 2, 0:width],
                                   ACT.Exp, scale=0.25).then_inc(s["exponentiated"], 1)

            @block.vector
            def _(dve):
                link = stepper(dve, s["vector_step"])
                dve.memset(part[:, :, :, :], LOWEST)
                if variant == 2:
                    dve.wait_ge(s["loaded"], k.loading(2))
                    dve.scalar_tensor_tensor(out=al[:, 1, :], in0=al[:, 0, :], scalar=-1.0, in1=al[:, 0, :],
                                             op0=ALU.mult, op1=ALU.min).then_inc(s["sums_ready"], 1)
                    link(dve.tensor_scalar(al[:, 2, :], al[:, 0, :], 0.0, None, ALU.max))
                    dve.wait_ge(s["columns_ready"], 1)
                    link(dve.tensor_tensor(al[:, 3, :], al[:, 1, :], al[:, 2, :], ALU.add))
                    link(dve.tensor_scalar(al[:, 3, :], al[:, 3, :], -4.0, None, ALU.mult))
                    link(dve.tensor_scalar(table[:, 0, :], dist, -1.0, None, ALU.mult))
                    dve.tensor_tensor(dist, dist, table[:, 0, :], ALU.max).then_inc(s["weights_ready"], 1)
                    dve.wait_ge(s["weights_ready"], 1)
                else:
                    link(dve.memset(rd[:, 0:1], 0.0))
                for e in plan:
                    k.pass_time(dve, PLAN_US[variant] / len(plan))
                    if e[0] == "max":
                        _, n, g, hh, qt, ch = e
                        width = HALF if variant else min(HALF, (qt + 1) * P - ch * HALF)
                        h = G * g + hh
                        if variant == 2 and qt == 0 and ch == 0:
                            dve.wait_ge(s["table_ready"], h + 1)
                        dve.wait_ge(s["max_scored"], n + 1)
                        bank = ps[:, 6 + n % 2, 0:width]
                        dst = part[:, g % 2, T * hh + qt, ch:ch + 1]
                        if variant == 2:
                            u = ch * HALF - qt * P + S - P
                            dve.tensor_tensor_reduce(bank, bank, table[:, h % 2, u:u + HALF], 1.0, LOWEST, ALU.add, ALU.max,
                                                     dst).then_inc(s["max_taken"], 1)
                        else:
                            dve.tensor_reduce(dst, bank, AX.X, ALU.max).then_inc(s["max_taken"], 1)
                    elif e[0] == "turn":
                        g = e[1]
                        dve.wait_ge(s["max_taken"], maxima_of[g])
                        dve.tensor_tensor(mx[:, g % 2, :], part[:, g % 2, :, 0], part[:, g % 2, :, 1],
                                          ALU.max).then_inc(s["max_combined"], 1)
                        dve.wait_ge(s["max_turned"], g + 1)
                        if g:
                            dve.wait_ge(s["mbounced"], 16 * g)
                        link(dve.tensor_scalar(mf[:, :], ps[0:G * T, 6, 0:P], -1.0, None, ALU.mult))
                        link(dve.tensor_copy(mp[:, 0, :], mf[:, :]))
                        link(dve.tensor_tensor(mf[:, :], mf[:, :], mp[:, 0, :], ALU.subtract))
                        link(dve.tensor_copy(mp[:, 1, :], mf[:, :]))
                        dve.tensor_tensor(mp[:, 2, :], mf[:, :], mp[:, 1, :], ALU.subtract).then_inc(s["max_split"], 1)
                    elif e[0] == "score" and variant == 2:
                        _, n, g, half, kt, pair = e
                        dve.wait_ge(s["scored"], n + 1)
                        u = half * HALF - kt * P + S - P
                        for j in range(2):
                            h = G * g + 2 * pair + j
                            bank = ps[:, 2 * (n % 2) + j, :]
                            last = dve.scalar_tensor_tensor(out=bank, in0=dist[:, u:u + HALF], scalar=al[:, 3, h:h + 1],
                                                            in1=bank, op0=ALU.mult, op1=ALU.add)
                        last.then_inc(s["biased"], 1)
                    elif e[0] == "finish":
                        f = e[1]
                        o = ot[:, f // 2, (f % 2) * HALF:(f % 2 + 1) * HALF]
                        dve.wait_ge(s["weighted"], last_weigh[f])
                        dve.tensor_copy(o, ps[:, 4 + f % 2, :]).then_inc(s["heads_copied"], 1)
                        dve.wait_ge(s["denominators_ready"], f + 1)
                        link(dve.reciprocal(rd[:, :], ps[:, 4 + f % 2, :]))
                        on_f = on[:, f // 2, (f % 2) * HALF:(f % 2 + 1) * HALF]
                        if variant == 1:
                            on_f = on[:, f // 2, :].rearrange("p (l c) -> p c l", c=H)[:, 8 * (f % 2):8 * (f % 2) + 8, :]
                            o, r = o.rearrange("p (c l) -> p c l", c=8), rd[:, :].rearrange("p (c l) -> p c l", c=8)
                        else:
                            r = rd[:, :]
                        dve.tensor_tensor(on_f, o, r, ALU.mult).then_inc(s["heads_done"], 1)
                for j in range(T // 2):
                    dve.wait_ge(s["results_ready"], j + 1)
                    xv = k.x[:, 2 * j:2 * j + 2, :]
                    link(dve.tensor_tensor(xv, ps[:, j, :].rearrange("p (t n) -> p t n", t=2), xv, ALU.add))
                    dve.tensor_tensor(xv, xv, bo[:, :].unsqueeze(1).broadcast_to([P, 2, D]), ALU.add)
        if variant == 2:
            k.loads = k.loading(2)
        k.end_stage()


def choose_experts(k):
    nc, s, ps, a = k.nc, k.sem, k.ps, k.a
    with ExitStack() as ctx:
        def sb(name, shape, dt=F32):
            return ctx.enter_context(nc.sbuf_tensor(k.unique(name), shape, dt))

        wi = sb("p_wi", [P, C, D])
        keys = sb("p_keys", [P, C, 2, NS])
        u = sb("p_u", [P, G])
        hT = sb("p_hT", [P, C, S])
        score = sb("p_score", [P, 2, HP * 2, NS])
        rest = sb("p_rest", [P, HP * 2, NS])
        top = sb("p_top", [P, HP, 2, KP])
        topi = sb("p_topi", [P, HP, 2, KP], U32)
        topf = sb("p_topf", [P, HP, 2, KP])
        cand = sb("p_cand", [P, HP, NC_])
        rise = sb("p_rise", [P, HP, 2, KP])
        crest = sb("p_crest", [P, HP, NC_])
        best = sb("p_best", [P, HP, KP])
        besti = sb("p_besti", [P, HP, KP], U32)
        bestf = sb("p_bestf", [P, HP, KP])
        hot = sb("p_hot", [P, HP * KP, KP])
        first = sb("p_first", [P, 4, HP * KP])
        expf = sb("p_expf", [P, HP, KP])
        z = sb("p_z", [P, 2, 4, HP])
        block = k.block
        tiles0 = k.chosen
        k.chosen += T
        k.started = k.clock + 45.0

        @block.vector
        def _(dve):
            dve.memset(u[:, :], 0.0).then_inc(s["cleared"], 1)

        @block.sync
        def _(sp):
            ld = s["loaded"]
            sp.dma_start(wi[:, :, :], a["L3_ffn_W_inT"].rearrange("(c p) n -> p c n", p=P)).then_inc(ld, 16)
            sp.dma_start(keys[:, :, 0, :], a["L3_ffn_keys_aT"].rearrange("(c p) n -> p c n", p=P)).then_inc(ld, 16)
            sp.dma_start(keys[:, :, 1, :], a["L3_ffn_keys_bT"].rearrange("(c p) n -> p c n", p=P)).then_inc(ld, 16)
            sp.wait_ge(s["cleared"], 1)
            for hh in range(G):
                sp.dma_start(u[HD * hh:HD * hh + HD, hh:hh + 1], a["L3_ffn_u_shared"].rearrange("(p o) -> p o", o=1)).then_inc(ld, 16)

        NL = 3 + G
        layer_norm(k, k.xp)

        @block.gpsimd
        def _(pool):
            for i in range(2 * T):
                n = 2 * tiles0 + i
                pool.wait_ge(s["indices_ready"], n // 2 + 1)
                if n >= SLOTS:
                    pool.wait_ge(s["rows_used"], n - SLOTS + 1)
                for j in range(HT):
                    col = HT * (i % 2) + j
                    pool.indirect_dma_start(k.got[n % SLOTS][:, j, :], None, a["L3_ffn_expert_v"],
                                            bass.IndirectOffsetOnAxis(k.expert[:, i // 2, col:col + 1], 0))\
                        .then_inc(s[f"gathered{n % SLOTS}"], 16)

        @block.tensor
        def _(pe):
            pe.wait_ge(s["loaded"], k.loading(NL))
            for m in range(C):
                for half in range(2):
                    for c in range(C):
                        last = pe.matmul(ps[:, 2 * m + half, :], wi[:, c, m * P:(m + 1) * P],
                                         k.yT[:, c, half * HALF:(half + 1) * HALF], start=(c == 0), stop=(c == C - 1))
                    last.then_inc(s["multiplied"], 1)
            pe.wait_ge(s["activated"], 4)
            for t in range(T):
                if t:
                    pe.wait_ge(s["probs_ready"], t)
                for h in range(HP):
                    c, hh = h // G, h % G
                    pe.matmul(ps[:, hh, c * 2 * NS:(c + 1) * 2 * NS],
                              hT[HD * hh:HD * hh + HD, c, t * P:(t + 1) * P],
                              keys[HD * hh:HD * hh + HD, c, :, :].rearrange("p a b -> p (a b)"), start=True, stop=True)
                for c in range(C):
                    last = pe.matmul(ps[:, 4, c * G:(c + 1) * G], hT[:, c, t * P:(t + 1) * P], u[:, :], start=True, stop=True)
                last.then_inc(s["scored"], 1)

        @block.scalar
        def _(act):
            for m in range(C):
                for half in range(2):
                    act.wait_ge(s["multiplied"], 2 * m + half + 1)
                    act.activation(hT[:, m, half * HALF:(half + 1) * HALF], ps[:, 2 * m + half, :], ACT.Copy).then_inc(s["activated"], 1)

            def copy_scores(t):
                act.wait_ge(s["scored"], t + 1)
                if t >= 2:
                    act.wait_ge(s["weights_ready"], t - 1)
                act.activation(z[:, t % 2, 0, :], ps[:, 4, 0:HP], ACT.Exp, scale=-1.0)
                act.activation(score[:, t % 2, :, :].rearrange("p (c g a) n -> p g c (a n)", c=C, g=G),
                               ps[:, 0:G, :].rearrange("p g (c n) -> p g c n", c=C), ACT.Copy).then_inc(s["probs_ready"], 1)

            copy_scores(0)
            for t in range(T):
                if t + 1 < T:
                    copy_scores(t + 1)
                act.wait_ge(s["max_taken"], t + 1)
                act.activation(k.wt[:, t, :, :], k.wt[:, t, :, :], ACT.Exp).then_inc(s["exponentiated"], 1)

        @block.vector
        def _(dve):
            link = stepper(dve, s["vector_step"])

            def top16(values, indices, score_of, rest_of, n):
                for i in range(n):
                    last = dve.max(values(i)[:, 0:8], score_of(i))
                link(last)
                for i in range(n):
                    last = dve.match_replace(rest_of(i), values(i)[:, 0:8], score_of(i), LOWEST)
                link(last)
                for i in range(n):
                    dve.max_index(indices(i)[:, 0:8], values(i)[:, 0:8], score_of(i))
                    last = dve.max(values(i)[:, 8:16], rest_of(i))
                link(last)
                for i in range(n):
                    last = dve.max_index(indices(i)[:, 8:16], values(i)[:, 8:16], rest_of(i))
                link(last)

            def look_up(value, place, bounds, steps):
                link(dve.tensor_tensor(hot[:, :, :], place.unsqueeze(2).broadcast_to([P, HP * KP, KP]),
                                       bounds[:, :].unsqueeze(1).broadcast_to([P, HP * KP, KP]), ALU.is_ge))
                hv = hot[:, :, :].rearrange("p (h k) r -> p h k r", k=KP)
                link(dve.tensor_tensor(hv, hv, steps.unsqueeze(2).broadcast_to([P, HP, KP, KP]), ALU.mult))
                link(dve.tensor_reduce(value, hot[:, :, :], AX.X, ALU.add))

            def choose(t):
                wt = k.wt[:, t, :, :]
                dve.wait_ge(s["probs_ready"], t + 1)
                top16(lambda i: top[:, i // 2, i % 2, :], lambda i: topi[:, i // 2, i % 2, :],
                      lambda i: score[:, t % 2, i, :], lambda i: rest[:, i, :], 2 * HP)
                link(dve.tensor_copy(topf[:, :, :, :], topi[:, :, :, :]))
                link(dve.scalar_tensor_tensor(out=topf[:, :, 0, :], in0=topf[:, :, 0, :], scalar=float(UNIT),
                                              in1=k.starts[:, :].unsqueeze(1).broadcast_to([P, HP, KP]),
                                              op0=ALU.mult, op1=ALU.add))
                dve.tensor_copy(rise[:, :, :, 0:1], topf[:, :, :, 0:1])
                dve.tensor_tensor(rise[:, :, :, 1:KP], topf[:, :, :, 1:KP], topf[:, :, :, 0:KP - 1], ALU.subtract)
                i = 0
                while i < KP:
                    m = sum(1 for r in ROWS[i:] if r == ROWS[i])
                    last = dve.tensor_tensor(cand[:, :, STARTS[i]:STARTS[i] + m * ROWS[i]].rearrange("p h (m n) -> p h m n", m=m),
                                             top[:, :, 0, i:i + m].unsqueeze(3).broadcast_to([P, HP, m, ROWS[i]]),
                                             top[:, :, 1, 0:ROWS[i]].unsqueeze(2).broadcast_to([P, HP, m, ROWS[i]]), ALU.add)
                    i += m
                link(last)
                top16(lambda i: best[:, i, :], lambda i: besti[:, i, :], lambda i: cand[:, i, :], lambda i: crest[:, i, :], HP)
                if t == 0 and tiles0:
                    dve.wait_ge(s["rows_used"], 2 * tiles0)
                dve.tensor_tensor(wt, best[:, :, :], best[:, :, 0:1].broadcast_to([P, HP, KP]),
                                  ALU.subtract).then_inc(s["max_taken"], 1)
                link(dve.tensor_copy(bestf[:, :, :], besti[:, :, :]))
                place = bestf[:, :, :].rearrange("p h k -> p (h k)")
                look_up(first[:, 0, :], place, k.starts, rise[:, :, 0, :])
                dve.tensor_tensor(first[:, 2, :], place, first[:, 0, :], ALU.subtract)
                link(dve.tensor_scalar(first[:, 1, :], first[:, 0, :], 0.5 - NC_ / 2, ROUND, ALU.add, ALU.add))
                link(dve.tensor_scalar(first[:, 1, :], first[:, 1, :], ROUND, None, ALU.subtract))
                link(dve.tensor_tensor(first[:, 2, :], first[:, 2, :], first[:, 1, :], ALU.add))
                look_up(first[:, 3, :], first[:, 2, :], k.number, rise[:, :, 1, :])
                link(dve.scalar_tensor_tensor(out=expf[:, :, :].rearrange("p h k -> p (h k)"), in0=first[:, 1, :],
                                              scalar=float(NS // UNIT), in1=first[:, 3, :], op0=ALU.mult, op1=ALU.add))
                dve.tensor_copy(k.expert[:, t, :], expf[:, :, :].rearrange("p h k -> p (h k)")).then_inc(s["indices_ready"], 1)
                dve.wait_ge(s["exponentiated"], t + 1)
                zt = z[:, t % 2, :, :]
                dve.tensor_scalar(zt[:, 1, :], zt[:, 0, :], 1.0, None, ALU.add)
                link(dve.tensor_reduce(zt[:, 2, :], wt, AX.X, ALU.add))
                link(dve.tensor_tensor(zt[:, 2, :], zt[:, 2, :], zt[:, 1, :], ALU.mult))
                link(dve.reciprocal(zt[:, 3, :], zt[:, 2, :]))
                link(dve.tensor_tensor(wt, wt, zt[:, 3, :].unsqueeze(2).broadcast_to([P, HP, KP]), ALU.mult))
                dve.sem_inc(s["weights_ready"], 1)

            k.clock += 15.0
            for t in range(T):
                choose(t)
                k.sent += 2
                k.pass_time(dve, 35.0)
    k.loads = k.loading(NL)
    k.end_stage()


def finish_experts(k):
    nc, s, ps, a = k.nc, k.sem, k.ps, k.a
    with ExitStack() as ctx:
        def sb(name, shape, dt=F32):
            return ctx.enter_context(nc.sbuf_tensor(k.unique(name), shape, dt))

        wo = sb("p_wo", [P, C, D])
        lnw = sb("p_lnw", [P, D])
        lnb = sb("p_lnb", [P, D])
        mT = sb("p_mT", [P, T, C, P])
        proj = sb("p_proj", [P, T, D])
        stats = sb("p_stats", [P, T, 6])
        mv = sb("p_mv", [P, T, 2])
        var = sb("p_var", [P, 3, T])
        block = k.block
        after = k.sent

        @block.sync
        def _(sp):
            ld = s["loaded"]
            sp.dma_start(wo[:, :, :], a["L3_ffn_W_outT"].rearrange("(c p) n -> p c n", p=P)).then_inc(ld, 16)
            sp.dma_start(lnw[:, :], a["L3_ffn_ln_w"].partition_broadcast(P)).then_inc(ld, 16)
            sp.dma_start(lnb[:, :], a["L3_ffn_ln_b"].partition_broadcast(P)).then_inc(ld, 16)
            sp.wait_ge(ld, k.loading(3))

        @block.tensor
        def _(pe):
            def project(t):
                pe.wait_ge(s["columns_ready"], t + 1)
                if t >= 4:
                    pe.wait_ge(s["results_ready"], t - 3)
                for c in range(C):
                    last = pe.matmul(ps[:, 4 + t % 4, 0:D], mT[:, t, c, :], wo[:, c, :],
                                     start=(c == 0), stop=(c == C - 1))
                last.then_inc(s["weighted"], 1)

            pe.wait_ge(s["loaded"], k.loading(3))
            for t in range(T):
                pe.wait_ge(s["rows_used"], after - 2 * T + 2 * t + 2)
                for c in range(C):
                    last = pe.transpose(ps[:, t % 4, c * P:(c + 1) * P],
                                        k.merged[:, t, c * P:(c + 1) * P], k.ident[:, :])
                last.then_inc(s["transposed"], 1)
                if t:
                    project(t - 1)
            project(T - 1)

        @block.scalar
        def _(act):
            for t in range(T):
                act.wait_ge(s["transposed"], t + 1)
                act.activation(mT[:, t, :, :].rearrange("p c n -> p (c n)"), ps[:, t % 4, 0:D],
                               ACT.Copy).then_inc(s["columns_ready"], 1)
                if t:
                    act.wait_ge(s["weighted"], t)
                    act.activation(proj[:, t - 1, :], ps[:, 4 + (t - 1) % 4, 0:D],
                                   ACT.Copy).then_inc(s["results_ready"], 1)
            act.wait_ge(s["weighted"], T)
            act.activation(proj[:, T - 1, :], ps[:, 4 + (T - 1) % 4, 0:D], ACT.Copy).then_inc(s["results_ready"], 1)
            act.wait_ge(s["variance_ready"], 1)
            act.activation(var[:, 1, :], var[:, 0, :], ACT.Sqrt).then_inc(s["std_ready"], 1)

        @block.vector
        def _(dve):
            link = stepper(dve, s["vector_step"])
            while k.weighed < after:
                k.weigh(dve)
            k.clock = max(k.clock, k.started + PACE * 2 * T)
            dve.wait_ge(s["results_ready"], T)
            for t in range(T):
                last = dve.bn_stats(stats[:, t, :], proj[:, t, :])
            link(last)
            for t in range(T):
                last = dve.bn_aggr(mv[:, t, :], stats[:, t, :])
            link(last)
            dve.tensor_scalar(var[:, 0, :], mv[:, :, 1], EPS, None, ALU.add).then_inc(s["variance_ready"], 1)
            dve.wait_ge(s["std_ready"], 1)
            link(dve.reciprocal(var[:, 2, :], var[:, 1, :]))
            for t in range(T):
                last = dve.tensor_scalar(proj[:, t, :], proj[:, t, :], mv[:, t, 0:1], var[:, 2, t:t + 1], ALU.subtract, ALU.mult)
            link(last)
            dve.wait_ge(s["loaded"], k.loading(3))
            link(dve.tensor_tensor(proj[:, :, :], proj[:, :, :], lnw[:, :].unsqueeze(1).broadcast_to([P, T, D]), ALU.mult))
            link(dve.tensor_tensor(proj[:, :, :], proj[:, :, :], lnb[:, :].unsqueeze(1).broadcast_to([P, T, D]), ALU.add))
            xv = k.xp[:, :, :].rearrange("p t n -> p (t n)")
            dve.scalar_tensor_tensor(out=xv, in0=proj[:, :, :].rearrange("p t n -> p (t n)"), scalar=0.5, in1=xv,
                                     op0=ALU.mult, op1=ALU.add)
    k.loads = k.loading(3)
    k.end_stage()


def layout(inputs):
    import numpy as np
    r = {n: np.ascontiguousarray(v) for n, v in inputs.items()}

    def turn(n):
        r[n + "T"] = np.ascontiguousarray(r.pop(n).T)
    for n in ("L0_attn_Wq", "L0_attn_Wk", "L0_attn_Wv", "L0_attn_Wo", "L1_attn_wq", "L1_attn_wk", "L1_attn_wv",
              "L1_attn_wo", "L2_attn_qkv_w", "L2_attn_out_w", "L2_ffn_W", "L2_ffn_Wp", "L3_attn_input_weights",
              "L3_attn_output_weight", "L3_ffn_W_in", "L3_ffn_W_out"):
        turn(n)
    r["L2_ffn_WdT"] = np.ascontiguousarray(np.concatenate([r.pop(f"L2_ffn_Wd{i}") for i in range(len(RANKS))], axis=0).T)
    r["L2_ffn_WuT"] = np.ascontiguousarray(np.concatenate([r.pop(f"L2_ffn_Wu{i}") for i in range(len(RANKS))], axis=1).T)
    for n in ("L3_ffn_keys_a", "L3_ffn_keys_b"):
        r[n + "T"] = np.ascontiguousarray(r.pop(n).transpose(0, 2, 1).reshape(D, NS))
    return r


EARLY = (("coupling", coupling_ffn, 80.0), ("attention", lambda k: attention(k, 0), 55.0),
         ("coupling", coupling_ffn, 80.0), ("experts", expert_ffn, 88.0),
         ("attention", lambda k: attention(k, 1), 75.0))
LATE = (("experts", expert_ffn, 88.0), ("low rank", lora_ffn, 47.0),
        ("attention", lambda k: attention(k, 2), 50.0), ("low rank", lora_ffn, 47.0))


def layers(k, stages):
    for _, stage, us in stages:
        stage(k)

        @k.block.vector
        def _(dve):
            k.pass_time(dve, us)


def program(nc, x, out, a):
    with ExitStack() as ctx:
        ctx.enter_context(nc.allow_non_contiguous_dma(reason="biases and router weights as columns"))
        k = Core(nc, ctx, a)
        constants(k)
        with nc.Block() as block:
            k.open(block)
            load_batch(k, x, 0)
            layers(k, EARLY + LATE)
            hand_over(k)
        k.end_block()
        with nc.Fori(1, B) as b:
            with nc.Block() as block:
                k.open(block)
                load_batch(k, x, b)
                choose_experts(k)
                layers(k, EARLY)
                finish_experts(k)
                gaussian_attention(k)
                choose_experts(k)
                layers(k, LATE)
                finish_experts(k)
                store_batch(k, out, b - 1)
                hand_over(k)
            k.end_block()
        with nc.Block() as block:
            k.open(block)
            choose_experts(k)
            finish_experts(k)
            gaussian_attention(k)
            choose_experts(k)
            finish_experts(k)
            store_batch(k, out, B - 1)
        k.end_block()


def kernel(**inputs):
    import concourse.bacc as _bacc
    from concourse import mybir as _mybir
    from concourse.bass_utils import run_bass_kernel_spmd as _run

    nc = _bacc.Bacc("TRN2", target_bir_lowering=False, num_devices=1)
    arrays = layout(inputs)
    aps = {n: nc.dram_tensor("in_" + n, v.shape, _mybir.dt.from_np(v.dtype), kind="ExternalInput").ap()
           for n, v in arrays.items()}
    out = nc.dram_tensor("out_0", (B, S, D), F32, kind="ExternalOutput").ap()
    program(nc, aps["L0_attn_x"], out, aps)
    r = _run(nc, [{"in_" + n: v for n, v in arrays.items()}], core_ids=[0])
    return r.results[0]["out_0"]
```
